# Optimizing a Trainium2 kernel written in Bass

```python
import numpy as np
import jax
import jax.numpy as jnp

def _softmax(x, axis=-1):
    return jax.nn.softmax(x, axis=axis)

def _gelu(x):
    return jax.nn.gelu(x, approximate=True)

def _silu(x):
    return jax.nn.silu(x)

def _sigmoid(x):
    return jax.nn.sigmoid(x)

def _layernorm(x, axis=-1, eps=1e-05):
    m = jnp.mean(x, axis=axis, keepdims=True)
    v = jnp.var(x, axis=axis, keepdims=True)
    return (x - m) / jnp.sqrt(v + eps)

def _scatter_add(tgt, idx, src, axis=0):
    return tgt.at[idx].add(src)

def _segment_sum(src, seg, n):
    return jax.ops.segment_sum(src, seg, n)
kernel_name = 'mk_adj_ffn_d2_adj_r2_3c8f8c'

def setup_inputs(seed: int=0):
    np.random.seed(seed)
    _w = jnp.asarray

    def _rec_inputs():
        import jax
        import jax.numpy as jnp
        _gk = jax.random.key(seed)
        x = -0.0005207 + 1.001 * jax.random.normal(jax.random.fold_in(_gk, 1), (4096, 128), jnp.float32)
        _w = (1.0 + jnp.arange(4096, dtype=jnp.float32)) ** (-0.5)
        _w = _w / _w.mean()
        _pij = jnp.clip(0.000488281 * _w[:, None] * _w[None, :], 0.0, 1.0)
        _a = jax.random.uniform(jax.random.fold_in(_gk, 2), (4096, 4096)) < _pij
        _af = _a.astype(jnp.float32)
        adj = _af
        return (x, adj)
    x, adj = _rec_inputs()

    def _L0_gnn_setup():
        import jax, jax.numpy as jnp
        import numpy as np
        NEG_INF = -9000000000000000.0
        NEG_SLOPE = 0.2
        key = jax.random.key(seed)
        k1, k2, k3, k4 = jax.random.split(key, 4)
        N, d_in, d_out = (4096, 128, 128)
        x = jax.random.normal(k1, (N, d_in), dtype=jnp.float32)
        adj = jax.random.randint(k2, (N, N), 0, 2).astype(jnp.float32)
        W = jax.random.normal(k3, (d_in, d_out), dtype=jnp.float32) * (1.0 / np.sqrt(d_in))
        a = jax.random.normal(k4, (2 * d_out,), dtype=jnp.float32) * (1.0 / np.sqrt(2 * d_out))
        return {'x': x, 'adj': adj, 'W': W, 'a': a}
    _L0_gnn_all = _L0_gnn_setup()
    _L0_gnn_in = {k: v for k, v in _L0_gnn_all.items() if k in ('W', 'a')}
    del _L0_gnn_all

    def _L0_ffn_setup():
        import jax, jax.numpy as jnp
        import numpy as np
        NUM_EXPERTS = 8
        TOP_K = 2
        B, S, D = (8, 4096, 128)

        def _moe(tokens, router_w, w1, b1, w2, b2):
            N = tokens.shape[0]
            E = router_w.shape[0]
            logits = tokens.astype(jnp.float32) @ router_w.astype(jnp.float32).T
            probs = jax.nn.softmax(logits, axis=-1)
            rw, re = jax.lax.top_k(probs, TOP_K)
            if TOP_K > 1:
                rw = rw / jnp.maximum(rw.sum(-1, keepdims=True), 1e-12)
            rw = rw.astype(tokens.dtype)
            combine = jnp.zeros((N, E), tokens.dtype).at[jnp.arange(N)[:, None], re].set(rw)
            out = tokens
            for e in range(E):
                h = jax.nn.gelu(tokens @ w1[e] + b1[e], approximate=False)
                y = h @ w2[e] + b2[e]
                out = out + combine[:, e:e + 1] * y
            return out
        key = jax.random.key(seed)
        ks = jax.random.split(key, 4)
        scale = 1.0 / np.sqrt(D).astype(np.float32)
        return {'input_embeddings': jax.random.normal(ks[0], (B, S, D), jnp.float32), 'router_w': jax.random.normal(ks[1], (NUM_EXPERTS, D), jnp.float32) * scale, 'w1': jax.random.normal(ks[2], (NUM_EXPERTS, D, D), jnp.float32) * scale, 'b1': jnp.zeros((NUM_EXPERTS, D), jnp.float32), 'w2': jax.random.normal(ks[3], (NUM_EXPERTS, D, D), jnp.float32) * scale, 'b2': jnp.zeros((NUM_EXPERTS, D), jnp.float32)}
    _L0_ffn_all = _L0_ffn_setup()
    _L0_ffn_in = {k: v for k, v in _L0_ffn_all.items() if k in ('router_w', 'w1', 'b1', 'w2', 'b2')}
    del _L0_ffn_all

    def _L1_gnn_setup():
        import jax, jax.numpy as jnp
        import numpy as np
        N, IN_FEAT, OUT_FEAT, H = (2048, 128, 128, 8)
        D = OUT_FEAT // H
        ADJ_DENSITY = 0.05
        key = jax.random.key(seed)
        kx, kw, kb, ka, kadj = jax.random.split(key, 5)
        x = jax.random.normal(kx, (N, IN_FEAT), dtype=jnp.float32)
        W = jax.random.normal(kw, (OUT_FEAT, IN_FEAT), dtype=jnp.float32) * (1.0 / np.sqrt(IN_FEAT))
        b = jax.random.normal(kb, (OUT_FEAT,), dtype=jnp.float32) * 0.01
        a = jax.random.normal(ka, (H, 2 * D), dtype=jnp.float32)
        adj_matrix = jax.random.bernoulli(kadj, ADJ_DENSITY, (N, N)).astype(jnp.float32)
        return {'x': x, 'W': W, 'b': b, 'a': a, 'adj_matrix': adj_matrix}
    _L1_gnn_all = _L1_gnn_setup()
    _L1_gnn_in = {k: v for k, v in _L1_gnn_all.items() if k in ('W', 'b', 'a')}
    del _L1_gnn_all

    def _L1_ffn_setup():
        import jax, jax.numpy as jnp
        import numpy as np
        B, N, D = (16, 2048, 128)
        NUM_EXPERTS, TOP_K, HEADS = (4, 2, 4)
        N_EDGES = 524288
        LN_EPS = 1e-05

        def _layernorm(x, g, b):
            mu = x.mean(-1, keepdims=True)
            var = ((x - mu) ** 2).mean(-1, keepdims=True)
            return (x - mu) * jax.lax.rsqrt(var + LN_EPS) * g + b

        def _forward(x, edge_index, W_gat, att_src, att_dst, b_gat, ln_gamma, ln_beta, W1, b1, W2, b2):
            Bc, Nc, Dc = x.shape
            M = Bc * Nc
            x_flat = x.reshape(M, Dc)
            h = (x_flat @ W_gat).reshape(M, HEADS, NUM_EXPERTS)
            loops = jnp.arange(M, dtype=edge_index.dtype)
            src = jnp.concatenate([edge_index[0], loops])
            dst = jnp.concatenate([edge_index[1], loops])
            a_src = (h * att_src).sum(-1)
            a_dst = (h * att_dst).sum(-1)
            e = jax.nn.leaky_relu(a_src[src] + a_dst[dst], negative_slope=0.2)
            e_max = jax.ops.segment_max(e, dst, num_segments=M)
            ee = jnp.exp(e - e_max[dst])
            denom = jax.ops.segment_sum(ee, dst, num_segments=M)
            alpha = ee / (denom[dst] + 1e-16)
            msg = h[src] * alpha[:, :, None]
            agg = jax.ops.segment_sum(msg, dst, num_segments=M).reshape(M, HEADS * NUM_EXPERTS) + b_gat
            scores = _layernorm(agg, ln_gamma, ln_beta).reshape(M, HEADS, NUM_EXPERTS).mean(1)
            scores = scores.reshape(Bc, Nc, NUM_EXPERTS)
            topk_s, topk_i = jax.lax.top_k(scores, TOP_K)
            w = jax.nn.softmax(topk_s, axis=-1)
            out = jnp.zeros_like(x)
            for ei in range(NUM_EXPERTS):
                g = jnp.where(topk_i == ei, w, 0.0).sum(-1)
                hh = jax.nn.gelu(x @ W1[ei] + b1[ei], approximate=False)
                out = out + g[..., None] * (hh @ W2[ei] + b2[ei])
            return out
        key = jax.random.key(seed)
        ks = jax.random.split(key, 8)
        s = 0.05
        return {'x': jax.random.normal(ks[0], (B, N, D), jnp.float32), 'W_gat': jax.random.normal(ks[1], (D, HEADS * NUM_EXPERTS), jnp.float32) * s, 'att_src': jax.random.normal(ks[2], (HEADS, NUM_EXPERTS), jnp.float32) * s, 'att_dst': jax.random.normal(ks[3], (HEADS, NUM_EXPERTS), jnp.float32) * s, 'b_gat': jnp.zeros((HEADS * NUM_EXPERTS,), jnp.float32), 'ln_gamma': jnp.ones((HEADS * NUM_EXPERTS,), jnp.float32), 'ln_beta': jnp.zeros((HEADS * NUM_EXPERTS,), jnp.float32), 'W1': jax.random.normal(ks[4], (NUM_EXPERTS, D, 2 * D), jnp.float32) * s, 'b1': jnp.zeros((NUM_EXPERTS, 2 * D), jnp.float32), 'W2': jax.random.normal(ks[5], (NUM_EXPERTS, 2 * D, D), jnp.float32) * s, 'b2': jnp.zeros((NUM_EXPERTS, D), jnp.float32), 'edge_index': jax.random.randint(ks[6], (2, N_EDGES), 0, B * N, jnp.int32)}
    _L1_ffn_all = _L1_ffn_setup()
    _L1_ffn_in = {k: v for k, v in _L1_ffn_all.items() if k in ('W_gat', 'att_src', 'att_dst', 'b_gat', 'ln_gamma', 'ln_beta', 'W1', 'b1', 'W2', 'b2', 'edge_index')}
    del _L1_ffn_all
    return {'x': x, 'adj': adj, 'L0_gnn_W': _L0_gnn_in['W'], 'L0_gnn_a': _L0_gnn_in['a'], 'L0_ffn_router_w': _L0_ffn_in['router_w'], 'L0_ffn_w1': _L0_ffn_in['w1'], 'L0_ffn_b1': _L0_ffn_in['b1'], 'L0_ffn_w2': _L0_ffn_in['w2'], 'L0_ffn_b2': _L0_ffn_in['b2'], 'L1_gnn_W': _L1_gnn_in['W'], 'L1_gnn_b': _L1_gnn_in['b'], 'L1_gnn_a': _L1_gnn_in['a'], 'L1_ffn_W_gat': _L1_ffn_in['W_gat'], 'L1_ffn_att_src': _L1_ffn_in['att_src'], 'L1_ffn_att_dst': _L1_ffn_in['att_dst'], 'L1_ffn_b_gat': _L1_ffn_in['b_gat'], 'L1_ffn_ln_gamma': _L1_ffn_in['ln_gamma'], 'L1_ffn_ln_beta': _L1_ffn_in['ln_beta'], 'L1_ffn_W1': _L1_ffn_in['W1'], 'L1_ffn_b1': _L1_ffn_in['b1'], 'L1_ffn_W2': _L1_ffn_in['W2'], 'L1_ffn_b2': _L1_ffn_in['b2'], 'L1_ffn_edge_index': _L1_ffn_in['edge_index']}

def reference(x, adj, L0_gnn_W, L0_gnn_a, L0_ffn_router_w, L0_ffn_w1, L0_ffn_b1, L0_ffn_w2, L0_ffn_b2, L1_gnn_W, L1_gnn_b, L1_gnn_a, L1_ffn_W_gat, L1_ffn_att_src, L1_ffn_att_dst, L1_ffn_b_gat, L1_ffn_ln_gamma, L1_ffn_ln_beta, L1_ffn_W1, L1_ffn_b1, L1_ffn_W2, L1_ffn_b2, L1_ffn_edge_index):
    import jax
    import jax.numpy as jnp

    def _L0_gnn_ref(x, adj, W, a):
        import jax, jax.numpy as jnp
        import numpy as np
        NEG_INF = -9000000000000000.0
        NEG_SLOPE = 0.2
        d_out = W.shape[1]
        Wh = x @ W
        e_src = Wh @ a[:d_out]
        e_dst = Wh @ a[d_out:]
        e = jax.nn.leaky_relu(e_src[:, None] + e_dst[None, :], NEG_SLOPE)
        N = Wh.shape[0]
        mask = (adj > 0) | jnp.eye(N, dtype=bool)
        e = jnp.where(mask, e, NEG_INF)
        alpha = jax.nn.softmax(e, axis=1)
        h = alpha @ Wh
        return h

    def _L0_ffn_ref(input_embeddings, router_w, w1, b1, w2, b2):
        import jax, jax.numpy as jnp
        import numpy as np
        NUM_EXPERTS = 8
        TOP_K = 2
        B, S, D = (8, 4096, 128)

        def _moe(tokens, router_w, w1, b1, w2, b2):
            N = tokens.shape[0]
            E = router_w.shape[0]
            logits = tokens.astype(jnp.float32) @ router_w.astype(jnp.float32).T
            probs = jax.nn.softmax(logits, axis=-1)
            rw, re = jax.lax.top_k(probs, TOP_K)
            if TOP_K > 1:
                rw = rw / jnp.maximum(rw.sum(-1, keepdims=True), 1e-12)
            rw = rw.astype(tokens.dtype)
            combine = jnp.zeros((N, E), tokens.dtype).at[jnp.arange(N)[:, None], re].set(rw)
            out = tokens
            for e in range(E):
                h = jax.nn.gelu(tokens @ w1[e] + b1[e], approximate=False)
                y = h @ w2[e] + b2[e]
                out = out + combine[:, e:e + 1] * y
            return out
        b, s, d = input_embeddings.shape
        tokens = input_embeddings.reshape(b * s, d)
        return _moe(tokens, router_w, w1, b1, w2, b2).reshape(b, s, d)

    def _L1_gnn_ref(x, W, b, a, adj_matrix):
        import jax, jax.numpy as jnp
        import numpy as np
        N, IN_FEAT, OUT_FEAT, H = (2048, 128, 128, 8)
        D = OUT_FEAT // H
        ADJ_DENSITY = 0.05
        num_nodes = x.shape[0]
        num_heads = a.shape[0]
        half = a.shape[1] // 2
        node_feats = (x @ W.T + b).reshape(num_nodes, num_heads, half)
        logit_parent = (node_feats * a[None, :, :half]).sum(axis=-1)
        logit_child = (node_feats * a[None, :, half:]).sum(axis=-1)
        attn_logits = logit_parent[:, None, :] + logit_child[None, :, :]
        attn_logits = jax.nn.leaky_relu(attn_logits, 0.2)
        attn_logits = jnp.where(jnp.abs(adj_matrix)[..., None] != 0.0, attn_logits, 0.0)
        attn_probs = jax.nn.softmax(attn_logits, axis=1)
        out = jnp.einsum('ijh,jhc->ihc', attn_probs, node_feats)
        return out.reshape(num_nodes, -1)

    def _L1_ffn_ref(x, W_gat, att_src, att_dst, b_gat, ln_gamma, ln_beta, W1, b1, W2, b2, edge_index):
        import jax, jax.numpy as jnp
        import numpy as np
        B, N, D = (16, 2048, 128)
        NUM_EXPERTS, TOP_K, HEADS = (4, 2, 4)
        N_EDGES = 524288
        LN_EPS = 1e-05

        def _layernorm(x, g, b):
            mu = x.mean(-1, keepdims=True)
            var = ((x - mu) ** 2).mean(-1, keepdims=True)
            return (x - mu) * jax.lax.rsqrt(var + LN_EPS) * g + b

        def _forward(x, edge_index, W_gat, att_src, att_dst, b_gat, ln_gamma, ln_beta, W1, b1, W2, b2):
            Bc, Nc, Dc = x.shape
            M = Bc * Nc
            x_flat = x.reshape(M, Dc)
            h = (x_flat @ W_gat).reshape(M, HEADS, NUM_EXPERTS)
            loops = jnp.arange(M, dtype=edge_index.dtype)
            src = jnp.concatenate([edge_index[0], loops])
            dst = jnp.concatenate([edge_index[1], loops])
            a_src = (h * att_src).sum(-1)
            a_dst = (h * att_dst).sum(-1)
            e = jax.nn.leaky_relu(a_src[src] + a_dst[dst], negative_slope=0.2)
            e_max = jax.ops.segment_max(e, dst, num_segments=M)
            ee = jnp.exp(e - e_max[dst])
            denom = jax.ops.segment_sum(ee, dst, num_segments=M)
            alpha = ee / (denom[dst] + 1e-16)
            msg = h[src] * alpha[:, :, None]
            agg = jax.ops.segment_sum(msg, dst, num_segments=M).reshape(M, HEADS * NUM_EXPERTS) + b_gat
            scores = _layernorm(agg, ln_gamma, ln_beta).reshape(M, HEADS, NUM_EXPERTS).mean(1)
            scores = scores.reshape(Bc, Nc, NUM_EXPERTS)
            topk_s, topk_i = jax.lax.top_k(scores, TOP_K)
            w = jax.nn.softmax(topk_s, axis=-1)
            out = jnp.zeros_like(x)
            for ei in range(NUM_EXPERTS):
                g = jnp.where(topk_i == ei, w, 0.0).sum(-1)
                hh = jax.nn.gelu(x @ W1[ei] + b1[ei], approximate=False)
                out = out + g[..., None] * (hh @ W2[ei] + b2[ei])
            return out
        return _forward(x, edge_index, W_gat, att_src, att_dst, b_gat, ln_gamma, ln_beta, W1, b1, W2, b2)
    x = x + _L0_gnn_ref(_layernorm(x, axis=-1), adj, L0_gnn_W, L0_gnn_a)
    x = x + _L0_ffn_ref(_layernorm(x, axis=-1)[None], L0_ffn_router_w, L0_ffn_w1, L0_ffn_b1, L0_ffn_w2, L0_ffn_b2)[0]
    x = x + _L1_gnn_ref(_layernorm(x, axis=-1), L1_gnn_W, L1_gnn_b, L1_gnn_a, adj)
    x = x + _L1_ffn_ref(_layernorm(x, axis=-1)[None], L1_ffn_W_gat, L1_ffn_att_src, L1_ffn_att_dst, L1_ffn_b_gat, L1_ffn_ln_gamma, L1_ffn_ln_beta, L1_ffn_W1, L1_ffn_b1, L1_ffn_W2, L1_ffn_b2, L1_ffn_edge_index)[0]
    return x

_drawn_inputs = setup_inputs


def setup_inputs(seed=0):
    import zlib

    import numpy as np

    out = dict(_drawn_inputs(seed))
    spreads = {'L0_ffn_b1': (0.0, 0.321),
     'L0_ffn_b2': (0.0, 0.1),
     'L1_ffn_b_gat': (0.0, 0.988),
     'L1_ffn_ln_gamma': (1.0, 0.6),
     'L1_ffn_ln_beta': (0.0, 2.0),
     'L1_ffn_b1': (0.0, 0.545),
     'L1_ffn_b2': (0.0, 0.1)}
    factors = {'L1_gnn_b': 8.0, 'L1_ffn_att_src': 64.0, 'L1_ffn_att_dst': 64.0}
    for name, (base, spread) in spreads.items():
        noise = np.random.default_rng([zlib.crc32(name.encode()), seed]).standard_normal(out[name].shape)
        drawn = base * np.exp(spread * noise) if base else spread * noise
        out[name] = jnp.asarray(drawn.astype(out[name].dtype))
    for name, factor in factors.items():
        out[name] = (out[name] * factor).astype(out[name].dtype)
    return out
```

```python
from contextlib import ExitStack

import concourse.bass as bass
from concourse import mybir

ALU = mybir.AluOpType
ACT = mybir.ActivationFunctionType
AX = mybir.AxisListType
F32 = mybir.dt.float32
BF16 = mybir.dt.bfloat16
I32 = mybir.dt.int32
U32 = mybir.dt.uint32
RMAX = bass.bass_isa.ReduceOp.max

P = 128
SLOPE = 0.2
LN_EPS = 1e-5
PARTS = 3
STEEP = 2.0 ** 80


class Steps:

    def __init__(self, engine, sem):
        self.engine, self.sem, self.count = engine, sem, 0

    def did(self, instruction):
        self.count += 1
        instruction.then_inc(self.sem, 1)
        return self.count

    def settle(self, count=None):
        self.engine.wait_ge(self.sem, self.count if count is None else count)


def wait_past(engine, sem, value):
    if isinstance(value, int) and value <= 0:
        return
    engine.wait_ge(sem, value)


class Kit:

    def __init__(self, nc, ctx, nodes, feats):
        self.nc, self.ctx = nc, ctx
        self.N, self.D, self.T = nodes, feats, nodes // P
        self.x = ctx.enter_context(nc.sbuf_tensor("x_tiles", [P, self.T, feats], F32))
        self.ident = ctx.enter_context(nc.sbuf_tensor("ident", [P, P], F32))
        self.ident_h = ctx.enter_context(nc.sbuf_tensor("ident_h", [P, P], BF16))
        self.bank = [ctx.enter_context(nc.psum_tensor(f"bank{i}", [P, 512], F32)) for i in range(8)]

    def sem(self, name):
        return self.ctx.enter_context(self.nc.semaphore(name))


def load_nodes(kit, x_in):
    nc = kit.nc
    x_loaded, zeroed, ident_made = kit.sem("x_loaded"), kit.sem("zeroed"), kit.sem("ident_made")
    with nc.Block() as block:

        @block.sync
        def _(sp):
            sp.dma_start(kit.x[:], x_in.rearrange("(t p) d -> p t d", p=P)).then_inc(x_loaded, 16)
            sp.wait_ge(x_loaded, 16)

        @block.gpsimd
        def _(pool):
            nc.gpsimd.memset(kit.ident[:], 0.0).then_inc(zeroed, 1)
            pool.wait_ge(zeroed, 1)
            nc.gpsimd.affine_select(out=kit.ident[:], in_=kit.ident[:], compare_op=ALU.not_equal, fill=1.0,
                                    base=0, pattern=[[-1, P]], channel_multiplier=1).then_inc(ident_made, 1)

        @block.vector
        def _(dve):
            dve.wait_ge(ident_made, 1)
            dve.tensor_copy(kit.ident_h[:], kit.ident[:]).then_inc(zeroed, 1)
            dve.wait_ge(zeroed, 2)


def layer_norm(kit, name, xn, xnT, eps=LN_EPS):
    nc, T, D = kit.nc, kit.T, kit.D
    stats_done, sqrt_done = kit.sem(name + "_stats"), kit.sem(name + "_sqrt")
    turned, moved = kit.sem(name + "_turned"), [kit.sem(name + "_moved_by_act"), kit.sem(name + "_moved_by_dve")]
    GROUP = 4
    groups = T // GROUP
    with ExitStack() as own:
        sb = lambda n, s, d: own.enter_context(nc.sbuf_tensor(name + n, s, d))
        stats, mv = sb("_st", [P, T, 6], F32), sb("_mv", [P, T, 2], F32)
        ve, sd, rstd = sb("_ve", [P, T], F32), sb("_sd", [P, T], F32), sb("_rstd", [P, T], F32)
        with nc.Block() as block:

            @block.vector
            def _(dve):
                s = Steps(dve, stats_done)
                for t in range(T):
                    s.did(dve.bn_stats(stats[:, t, :], kit.x[:, t, :]))
                for t in range(T):
                    s.settle(t + 1)
                    s.did(dve.bn_aggr(mv[:, t, :], stats[:, t, :]))
                s.settle()
                s.did(dve.tensor_scalar(ve[:], mv[:, :, 1], eps, None, ALU.add))
                dve.wait_ge(sqrt_done, 1)
                s.did(dve.reciprocal(rstd[:], sd[:]))
                s.settle()
                for t in range(T):
                    s.did(dve.tensor_scalar(xn[:, t, :], kit.x[:, t, :], mv[:, t, 0:1], rstd[:, t:t + 1],
                                            ALU.subtract, ALU.mult))
                for g in range(1, groups, 2):
                    dve.wait_ge(turned, g + 1)
                    dve.tensor_copy(xnT[:, GROUP * g:GROUP * (g + 1), :], kit.bank[g % 8][:]).then_inc(moved[1], 1)
                dve.wait_ge(moved[1], groups // 2)

            @block.scalar
            def _(act):
                act.wait_ge(stats_done, 2 * T + 1)
                act.activation(sd[:], ve[:], ACT.Sqrt).then_inc(sqrt_done, 1)
                for g in range(0, groups, 2):
                    act.wait_ge(turned, g + 1)
                    act.copy(xnT[:, GROUP * g:GROUP * (g + 1), :], kit.bank[g % 8][:]).then_inc(moved[0], 1)
                act.wait_ge(moved[0], groups // 2)

            @block.tensor
            def _(pe):
                for g in range(groups):
                    for t in range(GROUP * g, GROUP * (g + 1)):
                        pe.wait_ge(stats_done, 2 * T + 2 + t + 1)
                        last = pe.transpose(kit.bank[g % 8][:, (t % GROUP) * P:(t % GROUP + 1) * P], xn[:, t, :],
                                            kit.ident[:])
                    last.then_inc(turned, 1)


def dense_tables(kit, xn, xnT, adj, W_in, a_in, tab):
    nc, T, D, N = kit.nc, kit.T, kit.D, kit.N
    consts_in, prod, products = kit.sem("dt_consts_in"), kit.sem("dt_dve"), kit.sem("dt_products")
    act_done, pool_done, row_done, row_out = (kit.sem("dt_act"), kit.sem("dt_pool"), kit.sem("dt_row"),
                                              kit.sem("dt_row_out"))
    GROUP = 3
    groups = [list(range(g, min(g + GROUP, T))) for g in range(0, T, GROUP)]
    C130 = D + 2
    with ExitStack() as own:
        sb = lambda n, s, d: own.enter_context(nc.sbuf_tensor("dt_" + n, s, d))
        cat = sb("cat", [P, C130], F32)
        ab = sb("ab", [P, 2 * D], F32)
        scratch = sb("scratch", [P, D], F32)
        Wh = sb("Wh", [P, T, C130], F32)
        diag = sb("diag", [P, T], F32)
        row = sb("row", [1, N], F32)
        tm, tall = sb("tm", [P, 1], F32), sb("tall", [P, 1], F32)
        nt, nt2, u, m, e1, e2 = (sb(n, s, F32) for n, s in
                                 (("nt", [P, 1]), ("nt2", [P, 1]), ("u", [P, T]), ("m", [P, T]), ("e1", [P, T]),
                                  ("e2", [P, T])))
        B, Dc, w1, w2 = (sb(n, [P, T], F32) for n in ("B", "D", "w1", "w2"))
        v = sb("v", [P, T, D + 1], F32)
        with nc.Block() as block:

            @block.sync
            def _(sp):
                sp.dma_start(cat[:, 0:D], W_in).then_inc(consts_in, 16)
                sp.dma_start(ab[:], a_in.unsqueeze(0).to_broadcast([P, 2 * D])).then_inc(consts_in, 16)
                flat = adj.rearrange("i j -> (i j)")
                step = bass.AP(flat.tensor, 0, [[N + 1, P], [P * (N + 1), T]])
                sp.dma_start(diag[:], step, allow_slow_non_contiguous=True).then_inc(consts_in, 16)
                sp.wait_ge(row_done, 8)
                sp.dma_start(tab["s_row"].unsqueeze(0), row[:]).then_inc(row_out, 16)
                sp.wait_ge(row_out, 16)

            @block.tensor
            def _(pe):
                pe.wait_ge(prod, 2)
                for g, tiles in enumerate(groups):
                    if g >= 8:
                        pe.wait_ge(act_done, g - 7)
                    for k, t in enumerate(tiles):
                        last = pe.matmul(kit.bank[g % 8][:, k * C130:(k + 1) * C130], xnT[:, t, :], cat[:],
                                         start=True, stop=True)
                    last.then_inc(products, 1)
                for q in range(8):
                    b = (len(groups) + q) % 8
                    pe.wait_ge(act_done, min(len(groups), len(groups) + q - 7))
                    if len(groups) + q - 8 >= len(groups):
                        pe.wait_ge(row_done, q - 7)
                    pe.matmul(kit.bank[b][0:1, :], cat[:, D + 1:D + 2], xnT[:, 4 * q:4 * q + 4, :],
                              start=True, stop=True).then_inc(products, 1)

            @block.scalar
            def _(act):
                for g, tiles in enumerate(groups):
                    act.wait_ge(products, g + 1)
                    act.copy(Wh[:, tiles[0]:tiles[-1] + 1, :],
                             kit.bank[g % 8][:, 0:len(tiles) * C130]).then_inc(act_done, 1)
                n = len(groups)
                for q in range(8):
                    act.wait_ge(products, n + q + 1)
                    act.copy(row[:, 512 * q:512 * (q + 1)], kit.bank[(n + q) % 8][0:1, :]).then_inc(row_done, 1)
                s = Steps(act, act_done)
                s.count = n
                act.wait_ge(prod, 6)
                s.did(act.activation(B[:], Wh[:, :, D], ACT.Exp, bias=nt[:, 0:1]))
                s.did(act.activation(Dc[:], Wh[:, :, D], ACT.Exp, bias=nt2[:, 0:1], scale=SLOPE))
                act.wait_ge(prod, 9)
                s.did(act.activation(tab["A"][:], e1[:], ACT.Exp))
                s.did(act.activation(tab["C"][:], e2[:], ACT.Exp))
                for side in range(2):
                    for part in range(2):
                        act.wait_ge(tab["v_ready"], 3 * side + part + 1)
                        s.did(act.copy(tab["V"][:, :, side, part, :], v[:]))

            @block.gpsimd
            def _(pool):
                pool.wait_ge(prod, 3)
                pool.partition_all_reduce(tall[:], tm[:], P, RMAX).then_inc(pool_done, 1)

            @block.vector
            def _(dve):
                s = Steps(dve, prod)
                n = len(groups)
                dve.wait_ge(consts_in, 48)
                s.did(dve.tensor_tensor_reduce(scratch[:], cat[:, 0:D], ab[:, D:2 * D], 1.0, 0.0, ALU.mult,
                                               ALU.add, cat[:, D:D + 1]))
                s.settle()
                s.did(dve.tensor_tensor_reduce(scratch[:], cat[:, 0:D], ab[:, 0:D], 1.0, 0.0, ALU.mult,
                                               ALU.add, cat[:, D + 1:D + 2]))
                dve.wait_ge(act_done, n)
                s.did(dve.reduce_max(tm[:], Wh[:, :, D], AX.X))
                dve.wait_ge(pool_done, 1)
                s.did(dve.tensor_scalar(nt[:], tall[:], -1.0, None, ALU.mult))
                s.did(dve.tensor_scalar(nt2[:], tall[:], -SLOPE, None, ALU.mult))
                s.did(dve.tensor_scalar(u[:], Wh[:, :, D + 1], tall[:, 0:1], None, ALU.add))
                s.settle()
                s.did(dve.scalar_tensor_tensor(out=m[:], in0=u[:], scalar=SLOPE, in1=u[:], op0=ALU.mult,
                                               op1=ALU.max))
                s.settle()
                s.did(dve.tensor_tensor(e1[:], u[:], m[:], ALU.subtract))
                s.did(dve.scalar_tensor_tensor(out=e2[:], in0=u[:], scalar=SLOPE, in1=m[:], op0=ALU.mult,
                                               op1=ALU.subtract))
                dve.wait_ge(act_done, n + 4)
                s.did(dve.tensor_tensor(w1[:], tab["A"][:], B[:], ALU.mult))
                s.did(dve.tensor_tensor(w2[:], tab["C"][:], Dc[:], ALU.mult))
                s.did(dve.tensor_scalar(tab["steep_t"][:], Wh[:, :, D], STEEP, None, ALU.mult))
                s.did(dve.tensor_scalar(tab["neg_t"][:], Wh[:, :, D], -1.0, None, ALU.mult))
                s.settle()
                s.did(dve.tensor_tensor(w1[:], w1[:], w2[:], ALU.max))
                s.did(dve.memset(Wh[:, :, D:D + 1], 1.0))
                s.settle()
                s.did(dve.scalar_tensor_tensor(out=tab["w_self"][:], in0=diag[:], scalar=0.0, in1=w1[:],
                                               op0=ALU.is_le, op1=ALU.mult))
                s.did(dve.tensor_copy(tab["X"][:], Wh[:, :, 0:D + 1]))
                for side, coef in enumerate((B, Dc)):
                    if side:
                        s.settle()
                        dve.wait_ge(act_done, n + 6)
                        dve.wait_ge(tab["v_ready"], 3)
                    dve.tensor_tensor(v[:], Wh[:, :, 0:D + 1], coef[:].unsqueeze(2).to_broadcast([P, T, D + 1]),
                                      ALU.mult).then_inc(tab["v_ready"], 1)
                    for part in range(2):
                        dve.wait_ge(act_done, n + 4 + 2 * side + part + 1)
                        dve.wait_ge(tab["v_ready"], 3 * side + part + 1)
                        out = v[:] if part == 0 else tab["V"][:, :, side, 2, :]
                        dve.tensor_tensor(out, v[:], tab["V"][:, :, side, part, :],
                                          ALU.subtract).then_inc(tab["v_ready"], 1)
                dve.wait_ge(tab["v_ready"], 6)
                s.settle()


def in_pairs(engine, count, step):
    step(0)
    if count > 2:
        with engine.Fori(1, count - 1) as k:
            step(k)
    step(count - 1)


def dense_attention(kit, adj, adjT_out, tab):
    nc, T, D, N = kit.nc, kit.T, kit.D, kit.N
    CH = 2 * P
    CHUNKS, RT = N // CH, CH // P
    UNIT = 8
    UNITS = T // UNIT
    W = PARTS * (D + 1)
    STEPS = 8
    TURNS = 4
    BY_ACT = (1, 3)
    compares = [j for u in BY_ACT for j in range(UNIT * u, UNIT * (u + 1))]
    rows_in = [kit.sem(f"rows_in{i}") for i in range(2)]
    s_in = [kit.sem(f"s_in{i}") for i in range(2)]
    adjT_stored = [kit.sem(f"adjT_stored{i}") for i in range(2)]
    turned, placed, compared, masked, split = (kit.sem(n) for n in ("turned", "placed", "compared", "masked",
                                                                    "split"))
    multiplied, moved, finish = (kit.sem(n) for n in ("multiplied", "moved", "finish"))
    turn_bank = [kit.bank[4 + i][:].bitcast(BF16).rearrange("p (b i) -> p b i", b=UNIT) for i in range(TURNS)]
    with ExitStack() as own:
        sb = lambda n, s, d: own.enter_context(nc.sbuf_tensor("da_" + n, s, d))
        rows = [sb(f"rows{i}", [P, N], BF16) for i in range(2)]
        adjT = [sb(f"adjT{i}", [P, T, CH], BF16) for i in range(2)]
        pos = [sb(f"pos{i}", [P, T, CH], BF16) for i in range(2)]
        neg = [sb(f"neg{i}", [P, T, CH], BF16) for i in range(2)]
        srow = [sb(f"srow{i}", [P, CH], F32) for i in range(2)]
        sums = [[sb(f"sum{k}_{i}", [P, W], F32) for k in range(2)] for i in range(2)]
        z = sb("z", [P, W], F32)
        zr, zs, rden = sb("zr", [P, D + 1], F32), sb("zs", [P, D + 1], F32), sb("rden", [P, 1], F32)
        with nc.Block() as block:

            @block.gpsimd
            def _(pool):
                def pair(k):
                    for n in range(2 * RT):
                        r = 2 * RT * k + n
                        wait_past(pool, turned, UNITS * (r - 1))
                        pool.dma_start(rows[n % 2][:], adj[bass.ds(r * P, P), :]).then_inc(rows_in[n % 2], 16)

                in_pairs(pool, CHUNKS // 2, pair)

            @block.sync
            def _(sp):
                def pair(k):
                    for par in range(2):
                        c = 2 * k + par
                        wait_past(sp, masked, T * (c - 1))
                        sp.dma_start(srow[par][:], tab["s_row"][bass.ds(c * CH, CH)].unsqueeze(0)
                                     .to_broadcast([P, CH])).then_inc(s_in[par], 16)

                in_pairs(sp, CHUNKS // 2, pair)

            @block.vector
            def _(dve):
                def mask(c, par, k):
                    def split_off(u):
                        dve.wait_ge(masked, T * c + UNIT * (u + 1))
                        at = slice(UNIT * u, UNIT * (u + 1))
                        dve.tensor_tensor(neg[par][:, at, :], adjT[par][:, at, :], pos[par][:, at, :],
                                          ALU.subtract).then_inc(split, 1)

                    wait_past(dve, multiplied, RT * (c - 1))
                    dve.wait_ge(s_in[par], 16 * (k + 1))
                    for u in range(UNITS):
                        dve.wait_ge(placed, RT * UNITS * c + (RT - 1) * UNITS + u + 1)
                        if u in BY_ACT:
                            dve.wait_ge(compared, UNIT * (len(BY_ACT) * c + BY_ACT.index(u) + 1))
                            at = slice(UNIT * u, UNIT * (u + 1))
                            dve.tensor_tensor(pos[par][:, at, :], pos[par][:, at, :], adjT[par][:, at, :],
                                              ALU.mult).then_inc(masked, UNIT)
                        else:
                            for j in range(UNIT * u, UNIT * (u + 1)):
                                dve.scalar_tensor_tensor(
                                    out=pos[par][:, j, :], in0=srow[par][:], scalar=tab["neg_t"][:, j:j + 1],
                                    in1=adjT[par][:, j, :], op0=ALU.is_gt, op1=ALU.mult).then_inc(masked, 1)
                        if u > 0:
                            split_off(u - 1)
                    split_off(UNITS - 1)

                def finish_tile(t, i):
                    from_pos, from_neg = sums[i]
                    done = lambda n: STEPS * t + n
                    dve.wait_ge(moved, 2 * t + 2)
                    wait_past(dve, finish, done(0))
                    dve.tensor_scalar(z[:], from_pos[:], tab["A"][:, bass.ds(t, 1)], None, ALU.mult).then_inc(finish, 1)
                    dve.wait_ge(finish, done(1))
                    dve.scalar_tensor_tensor(out=z[:], in0=from_neg[:], scalar=tab["C"][:, bass.ds(t, 1)], in1=z[:],
                                             op0=ALU.mult, op1=ALU.add).then_inc(finish, 1)
                    dve.wait_ge(finish, done(2))
                    dve.tensor_reduce(zr[:], z[:].rearrange("p (k c) -> p c k", k=PARTS), AX.X,
                                      ALU.add).then_inc(finish, 1)
                    dve.wait_ge(finish, done(3))
                    dve.scalar_tensor_tensor(out=zs[:], in0=tab["X"][:, bass.ds(t, 1), :].squeeze(1),
                                             scalar=tab["w_self"][:, bass.ds(t, 1)], in1=zr[:], op0=ALU.mult,
                                             op1=ALU.add).then_inc(finish, 1)
                    dve.wait_ge(finish, done(4))
                    dve.reciprocal(rden[:], zs[:, D:D + 1]).then_inc(finish, 1)
                    dve.wait_ge(finish, done(5))
                    xt = kit.x[:, bass.ds(t, 1), :].squeeze(1)
                    dve.scalar_tensor_tensor(out=xt, in0=zs[:, 0:D], scalar=rden[:, 0:1], in1=xt, op0=ALU.mult,
                                             op1=ALU.add).then_inc(finish, 3)

                def pair(k):
                    for par in range(2):
                        c = 2 * k + par
                        if not isinstance(c, int) or c + 1 < CHUNKS:
                            mask(c + 1, 1 - par, k + par)
                        if not isinstance(c, int) or c > 0:
                            finish_tile(RT * c - 1, 1)
                        finish_tile(RT * c, 0)

                mask(0, 0, 0)
                in_pairs(dve, CHUNKS // 2, pair)
                finish_tile(T - 1, 1)
                dve.wait_ge(finish, STEPS * T)

            @block.scalar
            def _(act):
                def place(c, par, k):
                    wait_past(act, masked, T * (c - 1))
                    wait_past(act, split, UNITS * (c - 1))
                    wait_past(act, adjT_stored[par], 16 * k)
                    wait_past(act, multiplied, RT * (c - 1))
                    act.wait_ge(s_in[par], 16 * (k + 1))
                    for u in range(RT * UNITS):
                        i, b = u // UNITS, u % UNITS
                        act.wait_ge(turned, RT * UNITS * c + u + 1)
                        act.activation(adjT[par][:, UNIT * b:UNIT * (b + 1), i * P:(i + 1) * P],
                                       turn_bank[u % TURNS], ACT.Sign).then_inc(placed, 1)
                        for j in compares[len(compares) * u // (RT * UNITS):len(compares) * (u + 1) // (RT * UNITS)]:
                            act.activation(pos[par][:, j, :], srow[par][:], ACT.Sigmoid, scale=STEEP,
                                           bias=tab["steep_t"][:, j:j + 1]).then_inc(compared, 1)
                    act.wait_ge(placed, RT * UNITS * (c + 1))
                    act.dma_start(adjT_out[bass.ds(c, 1), :, :].squeeze(0), adjT[par][:].rearrange("p t i -> p (t i)")
                                  ).then_inc(adjT_stored[par], 16)

                def move(t, i):
                    act.wait_ge(multiplied, t + 1)
                    wait_past(act, finish, STEPS * (t - 1))
                    for n in range(2):
                        act.copy(sums[i][n][:], kit.bank[2 * i + n][:, 0:W]).then_inc(moved, 1)

                def pair(k):
                    for par in range(2):
                        c = 2 * k + par
                        if not isinstance(c, int) or c > 0:
                            move(RT * c - 1, 1)
                        if not isinstance(c, int) or c + 1 < CHUNKS:
                            place(c + 1, 1 - par, k + par)
                        move(RT * c, 0)

                place(0, 0, 0)
                in_pairs(act, CHUNKS // 2, pair)
                move(T - 1, 1)
                for par in range(2):
                    act.wait_ge(adjT_stored[par], 16 * (CHUNKS // 2))

            @block.tensor
            def _(pe):
                def turn(c, units):
                    for u in units:
                        i, b = u // UNITS, u % UNITS * UNIT
                        pe.wait_ge(rows_in[i], 16 * (c + 1))
                        wait_past(pe, placed, RT * UNITS * c + u - TURNS + 1)
                        for j in range(UNIT):
                            last = pe.transpose(turn_bank[u % TURNS][:, j, :], rows[i][:, (b + j) * P:(b + j + 1) * P],
                                                kit.ident_h[:])
                        last.then_inc(turned, 1)

                def multiply(c, par, t, i, turns):
                    wait_past(pe, moved, 2 * t - 2)
                    for j in range(T):
                        if j % UNIT == 0:
                            pe.wait_ge(split, UNITS * c + j // UNIT + 1)
                        at = slice(i * P, (i + 1) * P)
                        for n, lhs in enumerate((pos, neg)):
                            last = pe.matmul(kit.bank[2 * i + n][:, 0:W], lhs[par][:, j, at],
                                             tab["V"][:, j, n, :, :], start=(j == 0), stop=(j == T - 1))
                        if j == T - 1:
                            last.then_inc(multiplied, 1)
                        if turns and j % UNIT == UNIT - 1:
                            turn(c + 1, range(RT * (j // UNIT), RT * (j // UNIT + 1)))

                def pair(k):
                    for par in range(2):
                        c = 2 * k + par
                        multiply(c, par, RT * c, 0, not isinstance(c, int) or c + 1 < CHUNKS)
                        multiply(c, par, RT * c + 1, 1, False)

                turn(0, range(RT * UNITS))
                in_pairs(pe, CHUNKS // 2, pair)


def router(kit, xnT, router_w, comb):
    nc, T = kit.nc, kit.T
    E = router_w.shape[0]
    w_in, logits_done, exp_done, steps = (kit.sem(n) for n in ("rt_w_in", "rt_logits", "rt_exp", "rt_steps"))
    logits = kit.bank[0][:, 0:T * E].rearrange("p (t e) -> p t e", e=E)
    with ExitStack() as own:
        sb = lambda n, s: own.enter_context(nc.sbuf_tensor("rt_" + n, s, F32))
        rw = sb("rw", [P, E])
        prob, ranked, keep = sb("prob", [P, T, E]), sb("ranked", [P, T, E]), sb("keep", [P, T, E])
        top, total, rtotal, two, rtwo = (sb(n, [P, T]) for n in ("top", "total", "rtotal", "two", "rtwo"))
        wide = lambda a: a[:].unsqueeze(2).to_broadcast([P, T, E])
        with nc.Block() as block:

            @block.sync
            def _(sp):
                sp.dma_start(rw[:], router_w.rearrange("e d -> d e"), allow_slow_non_contiguous=True).then_inc(w_in, 16)

            @block.tensor
            def _(pe):
                pe.wait_ge(w_in, 16)
                for t in range(T):
                    last = pe.matmul(logits[:, t, :], xnT[:, t, :], rw[:], start=True, stop=True)
                last.then_inc(logits_done, 1)

            @block.scalar
            def _(act):
                act.wait_ge(steps, 2)
                act.activation(prob[:], keep[:], ACT.Exp).then_inc(exp_done, 1)

            @block.vector
            def _(dve):
                s = Steps(dve, steps)
                dve.wait_ge(logits_done, 1)
                s.did(dve.tensor_reduce(top[:], logits, AX.X, ALU.max))
                s.settle()
                s.did(dve.tensor_tensor(keep[:], logits, wide(top), ALU.subtract))
                dve.wait_ge(exp_done, 1)
                s.did(dve.tensor_reduce(total[:], prob[:], AX.X, ALU.add))
                s.settle()
                s.did(dve.reciprocal(rtotal[:], total[:]))
                s.settle()
                s.did(dve.tensor_tensor(prob[:], prob[:], wide(rtotal), ALU.mult))
                s.settle()
                for t in range(T):
                    s.did(dve.max(ranked[:, t, :], prob[:, t, :]))
                s.settle()
                s.did(dve.tensor_tensor(two[:], ranked[:, :, 0], ranked[:, :, 1], ALU.add))
                s.did(dve.tensor_tensor(keep[:], prob[:], ranked[:, :, 1:2].to_broadcast([P, T, E]), ALU.is_ge))
                s.settle()
                s.did(dve.tensor_scalar(two[:], two[:], 1e-12, None, ALU.max))
                s.did(dve.tensor_tensor(keep[:], keep[:], prob[:], ALU.mult))
                s.settle()
                s.did(dve.reciprocal(rtwo[:], two[:]))
                s.settle()
                s.did(dve.tensor_tensor(comb[:], keep[:], wide(rtwo), ALU.mult))
                s.settle()


def experts(kit, name, xnT, comb, w1, b1, w2, b2, also=None):
    nc, T, D = kit.nc, kit.T, kit.D
    E, _, F = w1.shape
    HV = F // P
    U = E * HV
    CT = 4
    HS = 4
    sem = lambda n: kit.sem(f"{name}_{n}")
    w_in, turned, comb_turned, biased, base = (sem(n) for n in ("w_in", "turned", "comb_turned", "biased", "base"))
    hidden, activated, projected, added, mixed = (sem(n) for n in ("hidden", "activated", "projected", "added", "mixed"))
    with ExitStack() as own:
        sb = lambda n, s: own.enter_context(nc.sbuf_tensor(f"{name}_{n}", s, F32))
        W1, W2, B1, B2 = sb("W1", [P, E, F]), sb("W2", [P, U, D]), sb("B1", [P, U]), sb("B2", [E, D])
        combT = sb("combT", [E, T, P])
        hs = sb("hs", [P, HS, CT * P])
        with nc.Block() as block:

            @block.sync
            def _(sp):
                sp.dma_start(W1[:], w1.rearrange("e d f -> d e f")).then_inc(w_in, 16)
                sp.dma_start(W2[:], w2.rearrange("e (h f) d -> f (e h) d", f=P)).then_inc(w_in, 16)
                sp.dma_start(B1[:], b1.rearrange("e (h f) -> f (e h)", f=P), allow_slow_non_contiguous=True).then_inc(w_in, 16)
                sp.dma_start(B2[:], b2).then_inc(w_in, 16)

            @block.tensor
            def _(pe):
                for g in range(T // CT):
                    wait_past(pe, comb_turned, g - 1)
                    for i in range(CT):
                        last = pe.transpose(kit.bank[4 + g % 2][0:E, i * P:(i + 1) * P], comb[:, CT * g + i, :],
                                            kit.ident[:])
                    last.then_inc(turned, 1)
                pe.wait_ge(w_in, 64)
                for g in range(T // CT):
                    pe.wait_ge(comb_turned, g + 1)
                    wait_past(pe, base, g - 1)
                    for i in range(CT):
                        last = pe.matmul(kit.bank[6 + g % 2][:, i * P:(i + 1) * P], combT[:, CT * g + i, :], B2[:],
                                         start=True, stop=True)
                    last.then_inc(biased, 1)

                def chunk(q):
                    def project(e):
                        pe.wait_ge(activated, U * q + (e + 1) * HV)
                        wait_past(pe, added, CT * (E * q + e - 1))
                        for i in range(CT):
                            for v in range(HV):
                                last = pe.matmul(kit.bank[2 + e % 2][:, i * P:(i + 1) * P],
                                                 hs[:, (e * HV + v) % HS, i * P:(i + 1) * P], W2[:, e * HV + v, :],
                                                 start=(v == 0), stop=(v == HV - 1))
                        last.then_inc(projected, 1)

                    for n in range(U):
                        wait_past(pe, activated, U * q + n - 1)
                        e, v = n // HV, n % HV
                        pe.matmul(kit.bank[n % 2][:], W1[:, e, v * P:(v + 1) * P], xnT[:, bass.ds(CT * q, CT), :],
                                  start=True, stop=True).then_inc(hidden, 1)
                        if n >= 1 and n % HV == 0:
                            project(e - 1)
                    project(E - 1)

                in_pairs(pe, T // CT, chunk)

            @block.scalar
            def _(act):
                for g in range(T // CT):
                    act.wait_ge(turned, g + 1)
                    act.copy(combT[:, CT * g:CT * (g + 1), :], kit.bank[4 + g % 2][0:E, :]).then_inc(comb_turned, 1)
                act.wait_ge(w_in, 64)

                def chunk(q):
                    for n in range(U):
                        wait_past(act, projected, E * q + (n - HS) // HV + 1)
                        act.wait_ge(hidden, U * q + n + 1)
                        act.activation(hs[:, n % HS, :], kit.bank[n % 2][:], ACT.Gelu,
                                       bias=B1[:, n:n + 1]).then_inc(activated, 1)

                in_pairs(act, T // CT, chunk)

            @block.vector
            def _(dve):
                for g in range(T // CT):
                    at = slice(CT * g, CT * (g + 1))
                    if also is not None:
                        dve.tensor_tensor(also[:, at, :], also[:, at, :], kit.x[:, at, :], ALU.add).then_inc(mixed, 1)
                    dve.wait_ge(biased, g + 1)
                    if also is not None:
                        dve.wait_ge(mixed, g + 1)
                    other = kit.x if also is None else also
                    dve.tensor_tensor(kit.x[:, at, :], kit.bank[6 + g % 2][:], other[:, at, :].rearrange("p t d -> p (t d)"),
                                      ALU.add).then_inc(base, 1)
                dve.wait_ge(base, T // CT)

                def chunk(q):
                    for e in range(E):
                        dve.wait_ge(projected, E * q + e + 1)
                        wait_past(dve, added, CT * (E * q + e))
                        for i in range(CT):
                            xt = kit.x[:, bass.ds(CT * q + i, 1), :].squeeze(1)
                            dve.scalar_tensor_tensor(out=xt, in0=kit.bank[2 + e % 2][:, i * P:(i + 1) * P],
                                                     scalar=comb[:, bass.ds(CT * q + i, 1), e], in1=xt,
                                                     op0=ALU.mult, op1=ALU.add).then_inc(added, 1)

                in_pairs(dve, T // CT, chunk)
                dve.wait_ge(added, T * E)


def head_tables(kit, xn, xnT, Wg, bg, ag, tab):
    nc, T, D, N = kit.nc, kit.T, kit.D, kit.N
    H = ag.shape[0]
    HC = D // H
    G1 = HC + 1
    CAT = D + 2 * H
    loads, steps, products, act_done, pool_done, row_done, row_out = (
        kit.sem("ht_" + n) for n in ("loads", "steps", "products", "act", "pool", "row_done", "row_out"))
    GROUP = 512 // CAT
    groups = [list(range(g, min(g + GROUP, T))) for g in range(0, T, GROUP)]
    n_g = len(groups)
    with ExitStack() as own:
        sb = lambda n, s: own.enter_context(nc.sbuf_tensor("ht_" + n, s, F32))
        Wraw, cat, bias = sb("Wraw", [P, D]), sb("cat", [P, CAT]), sb("bias", [P, CAT])
        a_all, tmp = sb("a", [P, H, 2 * HC]), sb("tmp", [P, H, HC])
        F = sb("F", [P, T, CAT])
        row = xn[0:H, :, :].rearrange("p t d -> p (t d)")
        bcol = sb("bcol", [H, 1])
        ones = sb("ones", [P, P])
        cm, call = sb("cm", [P, H]), sb("call", [P, H])
        cs, u, m, e1, e2, B, Dc = (sb(n, [P, T, H]) for n in ("cs", "u", "m", "e1", "e2", "B", "D"))
        X = sb("X", [P, T, H, G1])
        v = sb("v", [P, T, H, G1])
        def part_of(side, part):
            if side == 0:
                return tab["VX"][:, :, part, :, :]
            return tab["VH"][:, :, :, part, (side - 1) * G1:side * G1]

        over_tiles = lambda a: a[:].unsqueeze(1).to_broadcast([P, T, H])
        over_cols = lambda a: a[:].rearrange("p t h -> p (t h)").unsqueeze(2).to_broadcast([P, T * H, G1])
        flat = lambda a: a[:].rearrange("p t h c -> p (t h) c")
        with nc.Block() as block:

            @block.sync
            def _(sp):
                sp.dma_start(Wraw[:], Wg).then_inc(loads, 16)
                sp.dma_start(bias[:, 0:D], bg.unsqueeze(0).to_broadcast([P, D])).then_inc(loads, 16)
                sp.dma_start(a_all[:].rearrange("p h c -> p (h c)"),
                             ag.rearrange("h c -> (h c)").unsqueeze(0).to_broadcast([P, H * 2 * HC])).then_inc(loads, 16)
                sp.wait_ge(row_done, 8)
                sp.dma_start(tab["p_rows"], row).then_inc(row_out, 16)
                sp.wait_ge(row_out, 16)

            @block.tensor
            def _(pe):
                pe.wait_ge(loads, 48)
                pe.transpose(kit.bank[0][:, 0:P], Wraw[:], kit.ident[:]).then_inc(products, 1)
                pe.wait_ge(steps, 9)
                pe.matmul(kit.bank[1][0:H, 0:1], bias[0:1, D:D + H], kit.ident[0:1, 0:1], start=True,
                          stop=True).then_inc(products, 1)
                for g, tiles in enumerate(groups):
                    if g >= 6:
                        pe.wait_ge(steps, 10 + g - 5)
                    for k, t in enumerate(tiles):
                        last = pe.matmul(kit.bank[2 + g % 6][:, k * CAT:(k + 1) * CAT], xnT[:, t, :], cat[:],
                                         start=True, stop=True)
                    last.then_inc(products, 1)
                pe.wait_ge(steps, 10)
                for q in range(8):
                    wait_past(pe, row_done, q - 1)
                    pe.matmul(kit.bank[q % 2][0:H, :], cat[:, D:D + H], xnT[:, 4 * q:4 * q + 4, :], start=True,
                              stop=True).then_inc(products, 1)
                pe.wait_ge(steps, 10 + n_g + 2)
                for t in range(T):
                    last = pe.matmul(kit.bank[2][:, 0:H * G1], ones[:], X[:, t, :, :], start=(t == 0),
                                     stop=(t == T - 1))
                last.then_inc(products, 1)

            @block.gpsimd
            def _(pool):
                pool.wait_ge(steps, 10 + n_g + 3)
                pool.partition_all_reduce(call[:], cm[:], P, RMAX).then_inc(pool_done, 1)

            @block.scalar
            def _(act):
                s = Steps(act, act_done)
                act.wait_ge(steps, 10)
                for q in range(8):
                    act.wait_ge(products, 2 + n_g + q + 1)
                    act.activation(row[:, 512 * q:512 * (q + 1)], kit.bank[q % 2][0:H, :], ACT.Identity,
                                   bias=bcol[:, 0:1]).then_inc(row_done, 1)
                act.wait_ge(steps, 10 + n_g + 4)
                s.did(act.activation(B[:], cs[:], ACT.Exp))
                s.did(act.activation(Dc[:], cs[:], ACT.Exp, scale=SLOPE))
                act.wait_ge(steps, 10 + n_g + 8)
                s.did(act.activation(tab["A"][:], e1[:], ACT.Exp))
                s.did(act.activation(tab["C"][:], e2[:], ACT.Exp))
                s.did(act.activation(tab["E"][:], m[:], ACT.Exp, scale=-1.0))
                for side in range(3):
                    for part in range(2):
                        source = X if side == 0 and part == 0 else v
                        act.wait_ge(tab["hv_ready"], 3 * side + part + 1)
                        s.did(act.copy(part_of(side, part), source[:]))

            @block.vector
            def _(dve):
                s = Steps(dve, steps)
                dve.wait_ge(loads, 48)
                dve.wait_ge(products, 1)
                s.did(dve.tensor_copy(cat[:, 0:D], kit.bank[0][:, 0:P]))
                s.settle()
                for src, base in ((cat, 0), (bias, 0)):
                    view = src[:, 0:D].rearrange("p (h c) -> p h c", h=H)
                    for half in range(2):
                        s.did(dve.tensor_tensor(tmp[:], view, a_all[:, :, half * HC:(half + 1) * HC], ALU.mult))
                        s.settle()
                        s.did(dve.tensor_reduce(src[:, D + half * H:D + (half + 1) * H], tmp[:], AX.X, ALU.add))
                        s.settle()
                assert s.count == 9
                dve.wait_ge(products, 2)
                s.did(dve.tensor_copy(bcol[:], kit.bank[1][0:H, 0:1]))
                for g, tiles in enumerate(groups):
                    dve.wait_ge(products, 3 + g)
                    k = len(tiles)
                    s.did(dve.tensor_tensor(F[:, tiles[0]:tiles[-1] + 1, :],
                                            kit.bank[2 + g % 6][:, 0:k * CAT].rearrange("p (k c) -> p k c", k=k),
                                            bias[:].unsqueeze(1).to_broadcast([P, k, CAT]), ALU.add))
                s.did(dve.memset(ones[:], 1.0))
                s.settle()
                dve.memset(X[:, :, :, HC:G1], 1.0).then_inc(tab["hv_ready"], 1)
                s.did(dve.tensor_copy(X[:, :, :, 0:HC], F[:, :, 0:D].rearrange("p t (h c) -> p t h c", h=H)))
                c_col, p_col = F[:, :, D + H:CAT], F[:, :, D:D + H]
                s.did(dve.tensor_reduce(cm[:], c_col.rearrange("p t h -> p h t"), AX.X, ALU.max))
                dve.wait_ge(pool_done, 1)
                s.did(dve.tensor_tensor(cs[:], c_col, over_tiles(call), ALU.subtract))
                s.did(dve.tensor_tensor(u[:], p_col, over_tiles(call), ALU.add))
                s.settle()
                s.did(dve.tensor_scalar(m[:], u[:], 0.0, None, ALU.max))
                s.settle()
                s.did(dve.tensor_tensor(e1[:], u[:], m[:], ALU.subtract))
                s.did(dve.scalar_tensor_tensor(out=e2[:], in0=u[:], scalar=SLOPE, in1=m[:], op0=ALU.mult,
                                               op1=ALU.subtract))
                s.did(dve.tensor_scalar(tab["neg_c"][:], c_col, -1.0, None, ALU.mult))
                s.did(dve.tensor_scalar(tab["steep_c"][:], c_col, STEEP, None, ALU.mult))
                s.did(dve.tensor_reduce(tab["R"][:], kit.ident[:, 0:PARTS * 2 * G1].rearrange("p (k c) -> p c k", k=PARTS),
                                        AX.X, ALU.add))
                dve.wait_ge(products, 2 + n_g + 8 + 1)
                s.did(dve.tensor_copy(tab["S"][:].rearrange("p h c -> p (h c)"), kit.bank[2][:, 0:H * G1]))
                ready = tab["hv_ready"]
                for side in range(3):
                    if side:
                        dve.wait_ge(act_done, 5 + 2 * side)
                        dve.wait_ge(ready, 3 * side)
                        dve.tensor_tensor(flat(v), flat(X), over_cols(B if side == 1 else Dc), ALU.mult).then_inc(ready, 1)
                    for part in range(2):
                        dve.wait_ge(act_done, 5 + 2 * side + part + 1)
                        dve.wait_ge(ready, 3 * side + part + 1)
                        source = X if side == 0 and part == 0 else v
                        out = v[:] if part == 0 else part_of(side, 2)
                        dve.tensor_tensor(out, source[:], part_of(side, part),
                                          ALU.subtract).then_inc(ready, 1)
                dve.wait_ge(ready, 9)
                s.settle()


def head_attention(kit, adjT_dram, tab):
    nc, T, D, N = kit.nc, kit.T, kit.D, kit.N
    H, G1 = tab["S"].shape[1], tab["S"].shape[2]
    HC = G1 - 1
    CH, HALF = 4 * P, 2 * P
    IT = CH // P
    CHUNKS = N // CH
    UJ = 2
    UNITS = T // UJ
    BY_DVE = (1, 4, 6, 9, 12, 14)
    BY_ACT = tuple(g for g in range(UNITS) if g not in BY_DVE)
    RING_ACT, RING_DVE = 8, 4
    EJ = T // (2 * UNITS)
    assert IT * 2 == H and len(BY_ACT) * H % RING_ACT == 0 and len(BY_DVE) * H % RING_DVE == 0 and UNITS - 1 in BY_ACT
    HCOLS, UC = PARTS * 2 * G1, 2 * G1
    adjT_in = [kit.sem(f"adjT_in{i}") for i in range(2)]
    p_in = [kit.sem(f"p_in{i}") for i in range(2)]
    compared, pos_made, act_used, dve_used, head_moved, joined, join_moved, edges_done, edges_moved, fin = (
        kit.sem("ha_" + n) for n in ("compared", "pos_made", "act_used", "dve_used", "head_moved", "joined",
                                     "join_moved", "edges_done", "edges_moved", "fin"))
    FIN = 10
    with ExitStack() as own:
        sb = lambda n, s, d=F32: own.enter_context(nc.sbuf_tensor("ha_" + n, s, d))
        adjT = [sb(f"adjT{i}", [P, 2, T, HALF], BF16) for i in range(2)]
        pos_act = [sb(f"pos_act{i}", [P, UJ, 2, HALF], BF16) for i in range(RING_ACT)]
        pos_dve = [sb(f"pos_dve{i}", [P, UJ, 2, HALF], BF16) for i in range(RING_DVE)]
        prow = [sb(f"p{i}", [P, CH]) for i in range(2)]
        head = [sb(f"head{i}", [HCOLS, CH]) for i in range(2)]
        U = sb("U", [P, IT, H, UC])
        GX, GD = sb("GX", [P, IT, H, G1]), sb("GD", [P, IT, H, G1])
        rden = sb("rden", [P, IT * H, 1])

        def place(h, g):
            kind, ring, slots, used = ((BY_ACT, RING_ACT, pos_act, act_used) if g in BY_ACT else
                                       (BY_DVE, RING_DVE, pos_dve, dve_used))
            n = h * len(kind) + kind.index(g)
            return slots[n % ring], used, n

        with nc.Block() as block:

            @block.sync
            def _(sp):
                def load_adjT(q, par):
                    wait_past(sp, edges_done, IT * (q - 1))
                    for i in range(2):
                        sp.dma_start(adjT[par][:, i, :, :].rearrange("p t i -> p (t i)"),
                                     adjT_dram[bass.ds(2 * q + i, 1), :, :].squeeze(0)).then_inc(adjT_in[par], 16)

                def pair(k):
                    for par in range(2):
                        q = 2 * k + par
                        for h in range(H):
                            wait_past(sp, pos_made, UNITS * (H * q + h - 1))
                            sp.dma_start(prow[h % 2][:], tab["p_rows"][h:h + 1, bass.ds(q * CH, CH)]
                                         .to_broadcast([P, CH])).then_inc(p_in[h % 2], 16)
                            if h == 1 and (not isinstance(q, int) or q + 1 < CHUNKS):
                                load_adjT(q + 1, 1 - par)

                load_adjT(0, 0)
                in_pairs(sp, CHUNKS // 2, pair)

            @block.scalar
            def _(act):
                def move_head(n, h):
                    act.wait_ge(act_used, len(BY_ACT) * (n + 1))
                    wait_past(act, joined, n - 1)
                    act.copy(head[h % 2][:], kit.bank[h % 2][0:HCOLS, :]).then_inc(head_moved, 1)

                def pair(k):
                    for par in range(2):
                        q = 2 * k + par
                        for h in range(H):
                            act.wait_ge(p_in[h % 2], 16 * (H // 2 * q + h // 2 + 1))
                            for g in BY_ACT:
                                slot, used, n = place(h, g)
                                wait_past(act, used, len(BY_ACT) * H * q + n - RING_ACT + 1)
                                for j in range(UJ):
                                    last = act.activation(slot[:, j, :, :].rearrange("p a b -> p (a b)"),
                                                          prow[h % 2][:], ACT.Sigmoid,
                                                          bias=tab["steep_c"][:, g * UJ + j, h:h + 1], scale=STEEP)
                                last.then_inc(compared, 1)
                                if g == BY_ACT[4] and (h > 0 or not isinstance(q, int) or q > 0):
                                    move_head(H * q + h - 1, (h - 1) % 2)

                in_pairs(act, CHUNKS // 2, pair)
                move_head(H * CHUNKS - 1, 1)

            @block.vector
            def _(dve):
                def masks(q, par, h):
                    dve.wait_ge(adjT_in[par], 16 * (q - par) + 32)
                    dve.wait_ge(p_in[h % 2], 16 * (H // 2 * q + h // 2 + 1))
                    for g in range(UNITS):
                        slot, used, n = place(h, g)
                        if g in BY_ACT:
                            dve.wait_ge(compared, len(BY_ACT) * H * q + n + 1)
                            last = dve.tensor_tensor(slot[:], slot[:], adjT[par][:, :, g * UJ:(g + 1) * UJ, :]
                                                     .rearrange("p a j b -> p j a b"), ALU.mult)
                        else:
                            wait_past(dve, used, len(BY_DVE) * H * q + n - RING_DVE + 1)
                            for j in range(UJ):
                                last = dve.scalar_tensor_tensor(
                                    out=slot[:, j, :, :], in0=prow[h % 2][:].rearrange("p (a b) -> p a b", a=2),
                                    scalar=tab["neg_c"][:, g * UJ + j, h:h + 1], in1=adjT[par][:, :, g * UJ + j, :],
                                    op0=ALU.is_gt, op1=ALU.mult)
                        last.then_inc(pos_made, 1)

                def move_join(n, h):
                    dve.wait_ge(joined, n + 1)
                    dve.tensor_copy(U[:, :, h, :], kit.bank[6 + h % 2][:, 0:IT * UC].rearrange("p (i c) -> p i c", i=IT)
                                    ).then_inc(join_moved, 1)

                def move_edges(n, i):
                    dve.wait_ge(edges_done, n + 1)
                    for k, out, order in ((0, GX, "p (k h c) -> p h c k"), (1, GD, "p (h k c) -> p h c k")):
                        last = dve.tensor_reduce(out[:, i, :, :], kit.bank[2 + 2 * (i % 2) + k][:, 0:PARTS * H * G1]
                                                 .rearrange(order, k=PARTS, h=H), AX.X, ALU.add)
                    last.then_inc(edges_moved, 1)

                def finish(q):
                    done = lambda n: FIN * q + n
                    pairs = lambda a: a[:].rearrange("p i h c -> p (i h) c")
                    coef = lambda n: (tab[n][:, bass.ds(IT * q, IT), :].rearrange("p i h -> p (i h)").unsqueeze(2)
                                      .to_broadcast([P, IT * H, G1]))
                    U1, U2, GXp, GDp = pairs(U)[:, :, 0:G1], pairs(U)[:, :, G1:UC], pairs(GX), pairs(GD)
                    S4 = tab["S"][:].rearrange("p h c -> p (h c)").unsqueeze(1).to_broadcast([P, IT, H * G1])
                    GX4 = GX[:].rearrange("p i h c -> p i (h c)")
                    dve.wait_ge(join_moved, H * q + H)
                    dve.wait_ge(edges_moved, IT * q + IT)
                    dve.tensor_tensor(U1, U1, coef("A"), ALU.mult).then_inc(fin, 1)
                    dve.tensor_tensor(GDp, GDp, U2, ALU.subtract).then_inc(fin, 1)
                    dve.tensor_tensor(GX4, S4, GX4, ALU.subtract).then_inc(fin, 1)
                    dve.wait_ge(fin, done(2))
                    dve.tensor_tensor(GDp, GDp, coef("C"), ALU.mult).then_inc(fin, 1)
                    dve.wait_ge(fin, done(3))
                    dve.tensor_tensor(GXp, GXp, coef("E"), ALU.mult).then_inc(fin, 1)
                    dve.wait_ge(fin, done(4))
                    dve.tensor_tensor(U1, U1, GDp, ALU.add).then_inc(fin, 1)
                    dve.wait_ge(fin, done(6))
                    dve.tensor_tensor(U1, U1, GXp, ALU.add).then_inc(fin, 1)
                    dve.wait_ge(fin, done(7))
                    dve.reciprocal(rden[:], U1[:, :, HC:G1]).then_inc(fin, 1)
                    dve.wait_ge(fin, done(8))
                    dve.tensor_tensor(U1[:, :, 0:HC], U1[:, :, 0:HC], rden[:].to_broadcast([P, IT * H, HC]),
                                      ALU.mult).then_inc(fin, 1)
                    dve.wait_ge(fin, done(9))
                    xq = kit.x[:, bass.ds(IT * q, IT), :].rearrange("p i (h c) -> p (i h) c", h=H)
                    dve.tensor_tensor(xq, xq, U1[:, :, 0:HC], ALU.add).then_inc(fin, 1)
                    dve.wait_ge(fin, done(10))

                def pair(k):
                    for par in range(2):
                        q = 2 * k + par
                        for h in range(H):
                            masks(q, par, h)
                            if h == 0 and (not isinstance(q, int) or q > 0):
                                move_join(H * q - 2, H - 2)
                                move_join_last(q)
                            if h >= 2:
                                move_join(H * q + h - 2, h - 2)
                                if h % 2 == 0:
                                    move_edges(IT * q + h // 2 - 1, h // 2 - 1)

                def move_join_last(q):
                    move_join(H * q - 1, H - 1)
                    move_edges(IT * q - 1, IT - 1)
                    finish(q - 1)

                in_pairs(dve, CHUNKS // 2, pair)
                move_join(H * CHUNKS - 2, H - 2)
                move_join_last(CHUNKS)

            @block.tensor
            def _(pe):
                def join(n, h):
                    pe.wait_ge(head_moved, n + 1)
                    wait_past(pe, join_moved, n - 1)
                    for i in range(IT):
                        last = pe.matmul(kit.bank[6 + h % 2][:, i * UC:(i + 1) * UC], head[h % 2][:, i * P:(i + 1) * P],
                                         tab["R"][0:HCOLS, :], start=True, stop=True)
                    last.then_inc(joined, 1)

                def edges(q, par, i, first):
                    if first == 0:
                        wait_past(pe, edges_moved, IT * q + i - 1)
                        pe.wait_ge(adjT_in[par], 16 * (q - par) + 32)
                    for j in range(first, first + EJ):
                        for k, cols in enumerate((tab["VX"][:, j, :, :, :], tab["VH"][:, j, :, :, G1:UC])):
                            last = pe.matmul(kit.bank[2 + 2 * (i % 2) + k][:, 0:PARTS * H * G1],
                                             adjT[par][:, i // 2, j, (i % 2) * P:(i % 2 + 1) * P],
                                             cols, start=(j == 0), stop=(j == T - 1))
                    if first + EJ == T:
                        last.then_inc(edges_done, 1)

                def pair(k):
                    for par in range(2):
                        q = 2 * k + par
                        for h in range(H):
                            n = H * q + h
                            wait_past(pe, head_moved, n - 1)
                            for g in range(UNITS):
                                slot, used, _ = place(h, g)
                                pe.wait_ge(pos_made, n * UNITS + g + 1)
                                for j in range(UJ):
                                    jj = g * UJ + j
                                    last = pe.matmul(kit.bank[h % 2][0:HCOLS, :], tab["VH"][:, jj, h, :, :].rearrange("p k c -> p (k c)"),
                                                     slot[:, j, :, :].rearrange("p a b -> p (a b)"),
                                                     start=(jj == 0), stop=(jj == T - 1))
                                last.then_inc(used, 1)
                                edges(q, par, h // 2, (h % 2 * UNITS + g) * EJ)
                                if g == 10 and (h > 0 or not isinstance(q, int) or q > 0):
                                    join(n - 1, (h - 1) % 2)

                in_pairs(pe, CHUNKS // 2, pair)
                join(H * CHUNKS - 1, H - 1)


def edge_histogram(kit, edges, keys_dram, count_dram):
    nc, N = kit.nc, kit.N
    COLS = edges.shape[1] // P
    PIECE, SUB = 512, 256
    PIECES, SUBS = COLS // PIECE, COLS // SUB
    R = 64
    edges_in = [kit.sem(f"edges_in{i}") for i in range(2)]
    keys_out = [kit.sem(f"keys_out{i}") for i in range(2)]
    steps, hot, counted, count_moved, count_out = (kit.sem("eh_" + n) for n in ("steps", "hot", "counted", "moved", "out"))
    src_v, dst_v = (edges[i:i + 1, :].rearrange("o (p c) -> (o p) c", p=P) for i in range(2))
    with ExitStack() as own:
        sb = lambda n, s, d=F32: own.enter_context(nc.sbuf_tensor("eh_" + n, s, d))
        src = [sb(f"src{i}", [P, PIECE], I32) for i in range(2)]
        dst = [sb(f"dst{i}", [P, PIECE], I32) for i in range(2)]
        key = [sb(f"key{i}", [P, PIECE]) for i in range(2)]
        inner, valid, packed = sb("inner", [P, PIECE]), sb("valid", [P, PIECE]), sb("packed", [P, PIECE])
        hi_i, lo_i = sb("hi_i", [P, PIECE], I32), sb("lo_i", [P, PIECE], I32)
        hi, lo = sb("hi", [P, COLS], BF16), sb("lo", [P, COLS], BF16)
        hot_hi = [sb(f"hot_hi{i}", [P, R, SUB], BF16) for i in range(2)]
        hot_lo = [sb(f"hot_lo{i}", [P, R, SUB], BF16) for i in range(2)]
        counts = sb("counts", [R, R])
        PER = 8
        with nc.Block() as block:

            @block.sync
            def _(sp):
                for n in range(PIECES):
                    at = slice(n * PIECE, (n + 1) * PIECE)
                    wait_past(sp, steps, PER * (n - 1))
                    sp.dma_start(src[n % 2][:], src_v[:, at]).then_inc(edges_in[n % 2], 16)
                    sp.dma_start(dst[n % 2][:], dst_v[:, at]).then_inc(edges_in[n % 2], 16)
                sp.wait_ge(count_moved, 1)
                sp.dma_start(count_dram.rearrange("(a b) -> a b", a=R), counts[:]).then_inc(count_out, 16)
                sp.wait_ge(count_out, 16)

            @block.scalar
            def _(act):
                for n in range(PIECES):
                    act.wait_ge(steps, PER * (n + 1))
                    act.dma_start(keys_dram[:, n * PIECE:(n + 1) * PIECE], key[n % 2][:]).then_inc(keys_out[n % 2], 16)
                for i in range(2):
                    act.wait_ge(keys_out[i], 16 * PIECES // 2)

            @block.vector
            def _(dve):
                s = Steps(dve, steps)
                for n in range(PIECES):
                    i, at = n % 2, slice(n * PIECE, (n + 1) * PIECE)
                    dve.wait_ge(edges_in[i], 32 * (n // 2 + 1))
                    wait_past(dve, keys_out[i], 16 * (n // 2))
                    s.did(dve.tensor_scalar(inner[:], src[i][:], float(N - 1), None, ALU.is_lt))
                    s.did(dve.tensor_scalar(hi_i[:], dst[i][:], 6, None, ALU.logical_shift_right))
                    s.did(dve.tensor_scalar(lo_i[:], dst[i][:], R - 1, None, ALU.bitwise_and))
                    s.did(dve.scalar_tensor_tensor(out=packed[:], in0=dst[i][:], scalar=float(N), in1=src[i][:],
                                                   op0=ALU.mult, op1=ALU.add))
                    s.settle()
                    s.did(dve.scalar_tensor_tensor(out=valid[:], in0=dst[i][:], scalar=float(N), in1=inner[:],
                                                   op0=ALU.is_lt, op1=ALU.mult))
                    s.did(dve.scalar_tensor_tensor(out=hi[:, at], in0=inner[:], scalar=512.0, in1=hi_i[:],
                                                   op0=ALU.mult, op1=ALU.add))
                    s.did(dve.tensor_copy(lo[:, at], lo_i[:]))
                    s.settle()
                    s.did(dve.scalar_tensor_tensor(out=key[i][:], in0=packed[:], scalar=1.0, in1=valid[:],
                                                   op0=ALU.add, op1=ALU.mult))
                    s.settle()

                def pair(k):
                    for par in range(2):
                        n = 2 * k + par
                        wait_past(dve, counted, n - 1)
                        for digits, out in ((hi, hot_hi), (lo, hot_lo)):
                            for v in range(R):
                                last = dve.tensor_scalar(out[par][:, v, :], digits[:, bass.ds(n * SUB, SUB)], float(v),
                                                         None, ALU.is_equal)
                        last.then_inc(hot, 1)

                in_pairs(dve, SUBS // 2, pair)
                dve.wait_ge(counted, SUBS)
                dve.tensor_copy(counts[:], kit.bank[0][0:R, 0:R]).then_inc(count_moved, 1)

            @block.tensor
            def _(pe):
                def pair(k):
                    for par in range(2):
                        n = 2 * k + par
                        pe.wait_ge(hot, n + 1)
                        for e in range(SUB):
                            first = isinstance(n, int) and n == 0 and e == 0
                            end = isinstance(n, int) and n == SUBS - 1 and e == SUB - 1
                            last = pe.matmul(kit.bank[0][0:R, 0:R], hot_hi[par][:, :, e], hot_lo[par][:, :, e],
                                             start=first, stop=end, skip_group_check=True)
                        last.then_inc(counted, 1)

                in_pairs(pe, SUBS // 2, pair)


def edge_attention(kit, name, xnT, keys_dram, count_dram, w, tables, comb):
    nc, T, D, N = kit.nc, kit.T, kit.D, kit.N
    W_gat, att_src, att_dst, b_gat, gamma, beta = w
    H, EX = att_src.shape
    HE, G = H * EX, EX + 1
    CAT = HE + 2 * H
    SRC, DST = HE + H, 2 * H
    HALF = T // 2
    COLS = keys_dram.shape[1]
    TOP = 8
    VAL = H * G
    src_table, dst_table = tables
    sem = lambda n: kit.sem(f"{name}_{n}")
    loads, steps, products, act_done, pool_done, table_out, last_in = (
        sem(n) for n in ("loads", "steps", "products", "act", "pool", "table_out", "last_in"))
    taken, indices, turned_out, weighed, scored, spread, summed = (
        sem(n) for n in ("taken", "indices", "x", "weighed", "scored", "spread", "summed"))
    gathered = [sem(f"gathered{i}") for i in range(2)]
    with ExitStack() as own:
        sb = lambda n, s, d=F32: own.enter_context(nc.sbuf_tensor(f"{name}_{n}", s, d))
        cat, att = sb("cat", [P, CAT]), sb("att", [P, 2, HE])
        tmp = sb("tmp", [P, HE])
        rows = sb("rows", [P, T, CAT])
        dstrow = sb("dstrow", [P, T, DST])
        am, aall = sb("am", [P, H]), sb("aall", [P, H])
        counts_r, counts = sb("counts_r", [T, P]), sb("counts", [P, T])
        lastrow = sb("lastrow", [P, SRC])
        t1, t2 = sb("t1", [P, T, H]), sb("t2", [P, T, H])
        w_own, w_last = sb("w_own", [P, T, H]), sb("w_last", [P, T, H])
        acc, acc2 = sb("acc", [P, T, H, G]), sb("acc2", [P, T, H, G])
        keys, some = sb("keys", [P, COLS]), sb("some", [P, COLS])
        many, most = sb("many", [P, 1]), sb("most", [P, 1])
        pairs_f, pairs_i = sb("pairs_f", [P, 1]), sb("pairs_i", [P, 1], I32)
        iota_i, iota = sb("iota_i", [P, P], I32), sb("iota", [P, P])
        zero = sb("zero", [P, P])
        par_ = range(2)
        top = [sb(f"top{i}", [P, TOP]) for i in par_]
        real = [sb(f"real{i}", [P, TOP]) for i in par_]
        packed_f, packed = sb("packed_f", [P, TOP]), sb("packed", [P, TOP], I32)
        src_i = [sb(f"src{i}", [P, TOP], I32) for i in par_]
        dst_i = [sb(f"dst{i}", [P, TOP], I32) for i in par_]
        lo_i, hi_i = sb("lo_i", [P, TOP], I32), sb("hi_i", [P, TOP], I32)
        lo = [sb(f"lo{i}", [P, TOP]) for i in par_]
        hi = [sb(f"hi{i}", [P, TOP]) for i in par_]
        from_src = [sb(f"fs{i}", [P, TOP, SRC]) for i in par_]
        from_dst = [sb(f"fd{i}", [P, TOP, DST]) for i in par_]
        e1, e2, wt = sb("e1", [P, TOP, H]), sb("e2", [P, TOP, H]), sb("wt", [P, TOP, H])
        vals = sb("vals", [P, TOP, H, G])
        hot_lo = [sb(f"hot_lo{i}", [P, TOP, P]) for i in par_]
        hot_hi = sb("hot_hi", [P, TOP, T])
        spreads = [sb(f"spread{i}", [P, TOP, T, VAL]) for i in par_]
        heads = lambda a: a.rearrange("p t (h e) -> p t h e", h=H)
        by_head = lambda a, n: a.unsqueeze(3).to_broadcast([P, n, H, EX])

        def leaky_less(s, dve, out, a, b, bound, mid):
            s.did(dve.tensor_tensor(mid, a, b, ALU.add))
            s.settle()
            s.did(dve.scalar_tensor_tensor(out=out, in0=mid, scalar=SLOPE, in1=mid, op0=ALU.mult, op1=ALU.max))
            s.settle()
            if bound is not None:
                s.did(dve.tensor_tensor(out, out, bound, ALU.subtract))
                s.settle()

        S_ROWS, S_DSTROW, S_OWN, S_MANY, S_LAST, S_ZERO = 7, 11, 14, 16, 19, 25

        def read_pairs(engine):
            return engine.value_load(pairs_i[0:1, 0:1], min_val=2, max_val=COLS // TOP // 2)

        with nc.Block() as block:

            @block.sync
            def _(sp):
                sp.dma_start(cat[:, 0:HE], W_gat).then_inc(loads, 16)
                for i, a in enumerate((att_src, att_dst)):
                    sp.dma_start(att[:, i, :], a.rearrange("h e -> (h e)").unsqueeze(0).to_broadcast([P, HE])
                                 ).then_inc(loads, 16)
                sp.dma_start(keys[:], keys_dram).then_inc(loads, 16)
                sp.dma_start(counts_r[:], count_dram.rearrange("(t p) -> t p", p=P)).then_inc(loads, 16)
                sp.wait_ge(steps, S_ROWS)
                sp.dma_start(src_table.rearrange("(t p) c -> p t c", p=P), rows[:, :, 0:SRC]).then_inc(table_out, 16)
                sp.wait_ge(steps, S_DSTROW)
                sp.dma_start(dst_table.rearrange("(t p) c -> p t c", p=P), dstrow[:]).then_inc(table_out, 16)
                sp.wait_ge(table_out, 32)
                sp.dma_start(lastrow[:], src_table[N - 1:N, :].to_broadcast([P, SRC])).then_inc(last_in, 16)
                sp.wait_ge(last_in, 16)

            @block.tensor
            def _(pe):
                pe.wait_ge(loads, 80)
                pe.transpose(kit.bank[2][:, 0:T], counts_r[:], kit.ident[0:T, 0:T]).then_inc(products, 1)
                pe.wait_ge(steps, 4)
                for t in range(T):
                    last = pe.matmul(kit.bank[t // HALF][:, (t % HALF) * CAT:(t % HALF + 1) * CAT], xnT[:, t, :], cat[:],
                                     start=True, stop=True)
                last.then_inc(products, 1)
                pe.wait_ge(steps, S_ZERO)
                for b in range(2):
                    last = pe.matmul(kit.bank[4 + b][:, 0:HALF * VAL], zero[:], spreads[0][:, 0, 0:HALF, :], start=True,
                                     stop=False, skip_group_check=True)
                last.then_inc(products, 1)

                pairs = read_pairs(pe)

                def pair(k):
                    for par in par_:
                        pe.wait_ge(spread, 2 * k + par + 1)
                        for j in range(TOP):
                            for b in range(2):
                                last = pe.matmul(kit.bank[4 + b][:, 0:HALF * VAL], hot_lo[par][:, j, :],
                                                 spreads[par][:, j, b * HALF:(b + 1) * HALF, :], start=False,
                                                 stop=False, skip_group_check=True)
                        last.then_inc(summed, 1)

                pair(0)
                with pe.Fori(1, pairs) as k:
                    pair(k)

            @block.scalar
            def _(act):
                act.wait_ge(steps, S_OWN)
                act.activation(w_own[:], t2[:], ACT.Exp).then_inc(act_done, 1)
                act.wait_ge(steps, S_LAST)
                act.activation(w_last[:], t2[:], ACT.Exp).then_inc(act_done, 1)
                act.wait_ge(steps, S_ZERO)
                pairs = read_pairs(act)

                def pair(k):
                    for par in par_:
                        act.wait_ge(scored, 3 * (2 * k + par) + 3)
                        act.activation(wt[:], e2[:], ACT.Exp).then_inc(weighed, 1)

                pair(0)
                with act.Fori(1, pairs) as k:
                    pair(k)

            @block.gpsimd
            def _(pool):
                nc.gpsimd.iota(iota_i[:], pattern=[[1, P]], base=0, channel_multiplier=0).then_inc(pool_done, 1)
                pool.wait_ge(steps, S_ROWS + 1)
                pool.partition_all_reduce(aall[:], am[:], P, RMAX).then_inc(pool_done, 1)
                pool.wait_ge(steps, S_MANY)
                pool.partition_all_reduce(most[:], many[:], P, RMAX).then_inc(pool_done, 1)
                pool.wait_ge(steps, S_ZERO)
                pairs = read_pairs(pool)
                rounds_used = pool.alloc_register("rounds_used")

                def pair(k, looped=True):
                    for par in par_:
                        pool.wait_ge(indices, 2 * k + par + 1)
                        if looped:
                            pool.wait_ge(spread, rounds_used)
                            pool.reg_add(rounds_used, rounds_used, 1)
                        for j in range(TOP):
                            for out, table, index in ((from_src, src_table, src_i), (from_dst, dst_table, dst_i)):
                                pool.indirect_dma_start(
                                    out[par][:, j, :], None, table,
                                    bass.IndirectOffsetOnAxis(ap=index[par][:, j:j + 1].bitcast(U32), axis=0)
                                ).then_inc(gathered[par], 16)

                pool.wait_ge(table_out, 32)
                pair(0, looped=False)
                pool.reg_mov(rounds_used, 1)
                with pool.Fori(1, pairs) as k:
                    pair(k)

            @block.vector
            def _(dve):
                s = Steps(dve, steps)
                dve.wait_ge(loads, 80)
                for half in range(2):
                    s.did(dve.tensor_tensor(tmp[:], cat[:, 0:HE], att[:, half, :], ALU.mult))
                    s.settle()
                    s.did(dve.tensor_reduce(cat[:, HE + half * H:HE + (half + 1) * H],
                                            tmp[:].rearrange("p (h e) -> p h e", h=H), AX.X, ALU.add))
                    s.settle()
                dve.wait_ge(products, 1)
                s.did(dve.tensor_copy(counts[:], kit.bank[2][:, 0:T]))
                dve.wait_ge(products, 2)
                for b in range(2):
                    s.did(dve.tensor_copy(rows[:, b * HALF:(b + 1) * HALF, :].rearrange("p t c -> p (t c)"),
                                          kit.bank[b][:, 0:HALF * CAT]))
                assert s.count == S_ROWS
                s.settle()
                a_src, a_dst, m = rows[:, :, HE:SRC], rows[:, :, SRC:CAT], dstrow[:, :, H:DST]
                s.did(dve.tensor_reduce(am[:], a_src.rearrange("p t h -> p h t"), AX.X, ALU.max))
                dve.wait_ge(pool_done, 2)
                leaky_less(s, dve, m, a_dst, aall[:].unsqueeze(1).to_broadcast([P, T, H]), None, t1[:])
                s.did(dve.tensor_copy(dstrow[:, :, 0:H], a_dst))
                assert s.count == S_DSTROW
                leaky_less(s, dve, t2[:], a_src, a_dst, m, t1[:])
                assert s.count == S_OWN
                s.did(dve.tensor_scalar(some[:], keys[:], 0.0, None, ALU.is_gt))
                s.settle()
                s.did(dve.reduce_sum(many[:], some[:], AX.X))
                assert s.count == S_MANY
                dve.wait_ge(last_in, 16)
                dve.wait_ge(act_done, 1)
                leaky_less(s, dve, t2[:], a_dst, lastrow[:, HE:SRC].unsqueeze(1).to_broadcast([P, T, H]), m, t1[:])
                assert s.count == S_LAST
                dve.wait_ge(pool_done, 3)
                s.did(dve.tensor_scalar(pairs_f[:], most[:], float(2 * TOP - 1), 2.0 * 2 * TOP, ALU.add, ALU.max))
                s.settle()
                s.did(dve.tensor_copy(packed[:, 0:1], pairs_f[:]))
                s.settle()
                s.did(dve.tensor_scalar(pairs_i[:], packed[:, 0:1], 4, None, ALU.logical_shift_right))
                s.did(dve.tensor_copy(iota[:], iota_i[:]))
                s.did(dve.memset(zero[:], 0.0))
                s.did(dve.memset(spreads[0][:, 0, :, :], 0.0))
                assert s.count == S_ZERO
                s.did(dve.tensor_tensor(acc[:, :, :, 0:EX], heads(rows[:, :, 0:HE]), by_head(w_own[:], T), ALU.mult))
                s.did(dve.tensor_copy(acc[:, :, :, EX], w_own[:]))
                dve.wait_ge(act_done, 2)
                s.did(dve.tensor_tensor(acc2[:, :, :, EX], w_last[:], counts[:].unsqueeze(2).to_broadcast([P, T, H]),
                                        ALU.mult))
                s.settle()
                for h in range(H):
                    s.did(dve.tensor_tensor(acc2[:, :, h, 0:EX],
                                            lastrow[:, h * EX:(h + 1) * EX].unsqueeze(1).to_broadcast([P, T, EX]),
                                            acc2[:, :, h, EX:G].to_broadcast([P, T, EX]), ALU.mult))
                s.settle()
                s.did(dve.tensor_tensor(acc[:], acc[:], acc2[:], ALU.add))
                s.settle()
                dve.wait_ge(products, 3)

                TK = 10

                def take(r, par):
                    at = lambda n: TK * r + n
                    dve.max(top[par][:], keys[:]).then_inc(taken, 1)
                    dve.wait_ge(taken, at(1))
                    dve.tensor_scalar(packed_f[:], top[par][:], -1.0, 0.0, ALU.add, ALU.max).then_inc(taken, 1)
                    dve.tensor_scalar(real[par][:], top[par][:], 0.0, None, ALU.is_gt).then_inc(taken, 1)
                    dve.match_replace(keys[:], top[par][:], keys[:], 0.0).then_inc(taken, 1)
                    dve.wait_ge(taken, at(3))
                    dve.tensor_copy(packed[:], packed_f[:]).then_inc(taken, 1)
                    if not isinstance(r, int) or r >= 2:
                        dve.wait_ge(gathered[par], G16 * (r - par) // 2 if isinstance(r, int) else G8 * (r - par))
                    dve.wait_ge(taken, at(5))
                    dve.tensor_scalar(src_i[par][:], packed[:], N - 1, None, ALU.bitwise_and).then_inc(taken, 1)
                    dve.tensor_scalar(dst_i[par][:], packed[:], 12, None, ALU.logical_shift_right).then_inc(indices, 1)
                    dve.tensor_scalar(hi_i[:], packed[:], 12 + 7, None, ALU.logical_shift_right).then_inc(taken, 1)
                    dve.wait_ge(indices, r + 1)
                    dve.tensor_scalar(lo_i[:], dst_i[par][:], P - 1, None, ALU.bitwise_and).then_inc(taken, 1)
                    dve.wait_ge(taken, at(8))
                    dve.tensor_copy(hi[par][:], hi_i[:]).then_inc(taken, 1)
                    dve.tensor_copy(lo[par][:], lo_i[:]).then_inc(taken, 1)
                    dve.wait_ge(taken, at(10))

                SC = 6

                def spread_out(r, par, k):
                    wait_past(dve, summed, r - 1)
                    wait_past(dve, spread, r)
                    dve.tensor_tensor(hot_lo[par][:], iota[:].unsqueeze(1).to_broadcast([P, TOP, P]),
                                      lo[par][:].unsqueeze(2).to_broadcast([P, TOP, P]), ALU.is_equal)
                    dve.tensor_tensor(hot_hi[:], iota[:, 0:T].unsqueeze(1).to_broadcast([P, TOP, T]),
                                      hi[par][:].unsqueeze(2).to_broadcast([P, TOP, T]), ALU.is_equal).then_inc(turned_out, 1)
                    dve.wait_ge(gathered[par], G16 * (k + 1))
                    fs, fd = from_src[par], from_dst[par]
                    dve.tensor_tensor(e1[:], fs[:, :, HE:SRC], fd[:, :, 0:H], ALU.add).then_inc(scored, 1)
                    dve.wait_ge(scored, 3 * r + 1)
                    dve.scalar_tensor_tensor(out=e2[:], in0=e1[:], scalar=SLOPE, in1=e1[:], op0=ALU.mult,
                                             op1=ALU.max).then_inc(scored, 1)
                    dve.wait_ge(scored, 3 * r + 2)
                    dve.tensor_tensor(e2[:], e2[:], fd[:, :, H:DST], ALU.subtract).then_inc(scored, 1)
                    dve.wait_ge(weighed, r + 1)
                    dve.tensor_tensor(vals[:, :, :, EX], wt[:], real[par][:].unsqueeze(2).to_broadcast([P, TOP, H]),
                                      ALU.mult).then_inc(turned_out, 1)
                    dve.wait_ge(turned_out, 3 * r + 2)
                    dve.tensor_tensor(vals[:, :, :, 0:EX], fs[:, :, 0:HE].rearrange("p j (h e) -> p j h e", h=H),
                                      vals[:, :, :, EX:G].to_broadcast([P, TOP, H, EX]), ALU.mult).then_inc(turned_out, 1)
                    dve.wait_ge(turned_out, 3 * r + 3)
                    for j in range(TOP):
                        last = dve.tensor_tensor(spreads[par][:, j, :, :],
                                                 vals[:, j, :, :].rearrange("p h g -> p (h g)").unsqueeze(1)
                                                 .to_broadcast([P, T, VAL]),
                                                 hot_hi[:, j, :].unsqueeze(2).to_broadcast([P, T, VAL]), ALU.mult)
                    last.then_inc(spread, 1)

                G16 = 16 * 2 * TOP
                G8 = G16 // 2
                pairs = read_pairs(dve)

                def pair(k):
                    for par in par_:
                        r = 2 * k + par
                        take(r + 1, 1 - par)
                        spread_out(r, par, k)

                take(0, 0)
                pair(0)
                with dve.Fori(1, pairs) as k:
                    pair(k)


        agg, centred, sq = sb("agg", [P, T, HE]), sb("centred", [P, T, HE]), sb("sq", [P, T, HE])
        rden = sb("rden", [P, T, H])
        mu, var, sd, rstd = (sb(n, [P, T]) for n in ("mu", "var", "sd", "rstd"))
        norm = sb("norm", [P, 3, HE])
        PAD = 8
        score, ranked = sb("score", [P, T, PAD]), sb("ranked", [P, T, PAD])
        keep, soft, total = sb("keep", [P, T, EX]), sb("soft", [P, T, EX]), sb("total", [P, T])
        norm_in, s_steps, s_act = sem("norm_in"), sem("s_steps"), sem("s_act")
        wide = lambda a: a.unsqueeze(2).to_broadcast([P, T, HE])
        S_VAR, S_SOFT = 11, 18 + T
        per_node = lambda i: norm[:, i:i + 1, :].to_broadcast([P, T, HE])
        with nc.Block() as block:

            @block.sync
            def _(sp):
                for i, a in enumerate((b_gat, gamma, beta)):
                    sp.dma_start(norm[:, i, :], a.unsqueeze(0).to_broadcast([P, HE])).then_inc(norm_in, 16)

            @block.scalar
            def _(act):
                act.wait_ge(s_steps, S_VAR)
                act.activation(sd[:], var[:], ACT.Sqrt).then_inc(s_act, 1)
                act.wait_ge(s_steps, S_SOFT)
                act.activation(soft[:], keep[:], ACT.Exp, scale=1.0 / H).then_inc(s_act, 1)

            @block.vector
            def _(dve):
                s = Steps(dve, s_steps)

                def step(instruction):
                    s.did(instruction)
                    s.settle()

                for b in range(2):
                    at = slice(b * HALF, (b + 1) * HALF)
                    s.did(dve.tensor_tensor(acc[:, at, :, :].rearrange("p t h g -> p (t h g)"),
                                            acc[:, at, :, :].rearrange("p t h g -> p (t h g)"),
                                            kit.bank[4 + b][:, 0:HALF * VAL], ALU.add))
                s.settle()
                step(dve.tensor_scalar(t1[:], acc[:, :, :, EX], 1e-16, None, ALU.add))
                step(dve.reciprocal(rden[:], t1[:]))
                step(dve.tensor_tensor(heads(agg[:]), acc[:, :, :, 0:EX], by_head(rden[:], T), ALU.mult))
                dve.wait_ge(norm_in, 48)
                step(dve.tensor_tensor(agg[:], agg[:], per_node(0), ALU.add))
                step(dve.reduce_sum(mu[:], agg[:], AX.X))
                step(dve.scalar_tensor_tensor(out=centred[:], in0=wide(mu[:]), scalar=-1.0 / HE, in1=agg[:],
                                              op0=ALU.mult, op1=ALU.add))
                step(dve.tensor_tensor(sq[:], centred[:], centred[:], ALU.mult))
                step(dve.reduce_sum(var[:], sq[:], AX.X))
                step(dve.tensor_scalar(var[:], var[:], 1.0 / HE, LN_EPS, ALU.mult, ALU.add))
                assert s.count == S_VAR
                dve.wait_ge(s_act, 1)
                step(dve.reciprocal(rstd[:], sd[:]))
                step(dve.tensor_tensor(centred[:], centred[:], wide(rstd[:]), ALU.mult))
                step(dve.tensor_tensor(centred[:], centred[:], per_node(1), ALU.mult))
                step(dve.tensor_tensor(centred[:], centred[:], per_node(2), ALU.add))
                step(dve.memset(score[:], -3e38))
                step(dve.tensor_reduce(score[:, :, 0:EX], centred[:].rearrange("p t (h e) -> p t e h", h=H), AX.X,
                                       ALU.add))
                for t in range(T):
                    s.did(dve.max(ranked[:, t, :], score[:, t, :]))
                s.settle()
                step(dve.tensor_tensor(keep[:], score[:, :, 0:EX], ranked[:, :, 0:1].to_broadcast([P, T, EX]),
                                       ALU.subtract))
                assert s.count == S_SOFT
                dve.wait_ge(s_act, 2)
                step(dve.tensor_tensor(keep[:], score[:, :, 0:EX], ranked[:, :, 1:2].to_broadcast([P, T, EX]),
                                       ALU.is_ge))
                step(dve.tensor_tensor(soft[:], soft[:], keep[:], ALU.mult))
                step(dve.reduce_sum(total[:], soft[:], AX.X))
                step(dve.reciprocal(total[:], total[:]))
                step(dve.tensor_tensor(comb[:], soft[:], total[:].unsqueeze(2).to_broadcast([P, T, EX]), ALU.mult))


def rest(nc, kit, ins, adjT_dram, edge_dram, stop):
    N, T, D = kit.N, kit.T, kit.D
    dram = lambda n, s, d: nc.dram_tensor(n, s, d, kind="Internal").ap()
    with ExitStack() as own:
        sb = lambda n, s: own.enter_context(nc.sbuf_tensor(n, s, F32))
        xn, xnT = sb("xn1", [P, T, D]), sb("xnT1", [P, T, P])
        comb = sb("comb0", [P, T, ins["L0_ffn_w1"].shape[0]])
        layer_norm(kit, "ln1", xn, xnT)
        router(kit, xnT, ins["L0_ffn_router_w"], comb)
        experts(kit, "ffn0", xnT, comb, ins["L0_ffn_w1"], ins["L0_ffn_b1"], ins["L0_ffn_w2"], ins["L0_ffn_b2"], also=xn)
    if stop == 2:
        return
    H = ins["L1_gnn_a"].shape[0]
    G1 = D // H + 1
    with ExitStack() as own:
        sb = lambda n, s, d=F32: own.enter_context(nc.sbuf_tensor("t3_" + n, s, d))
        tab = {"p_rows": dram("p_rows", [H, N], F32), "hv_ready": kit.sem("hv_ready")}
        for n in ("A", "C", "E", "neg_c", "steep_c"):
            tab[n] = sb(n, [P, T, H])
        tab["S"], tab["R"] = sb("S", [P, H, G1]), sb("R", [P, 2 * G1])
        tab["VX"], tab["VH"] = sb("VX", [P, T, PARTS, H, G1], BF16), sb("VH", [P, T, H, PARTS, 2 * G1], BF16)
        with ExitStack() as tmp:
            xn = tmp.enter_context(nc.sbuf_tensor("xn2", [P, T, D], F32))
            xnT = tmp.enter_context(nc.sbuf_tensor("xnT2", [P, T, P], F32))
            layer_norm(kit, "ln2", xn, xnT)
            head_tables(kit, xn, xnT, ins["L1_gnn_W"], ins["L1_gnn_b"], ins["L1_gnn_a"], tab)
        head_attention(kit, adjT_dram, tab)
    if stop == 3:
        return
    edge_layer(nc, kit, ins, edge_dram)


def edge_layer(nc, kit, ins, edge_dram):
    N, T, D = kit.N, kit.T, kit.D
    dram = lambda n, s, d: nc.dram_tensor(n, s, d, kind="Internal").ap()
    keys_dram, count_dram = edge_dram
    with ExitStack() as own:
        sb = lambda n, s: own.enter_context(nc.sbuf_tensor(n, s, F32))
        xnT = sb("xnT3", [P, T, P])
        heads, per_head = ins["L1_ffn_att_src"].shape
        comb = sb("comb1", [P, T, ins["L1_ffn_W1"].shape[0]])
        with ExitStack() as tmp:
            layer_norm(kit, "ln3", tmp.enter_context(nc.sbuf_tensor("xn3", [P, T, D], F32)), xnT)
        tables = (dram("src_table", [N, heads * per_head + heads], F32), dram("dst_table", [N, 2 * heads], F32))
        edge_attention(kit, "ea", xnT, keys_dram, count_dram,
                       [ins["L1_ffn_" + n] for n in ("W_gat", "att_src", "att_dst", "b_gat", "ln_gamma", "ln_beta")],
                       tables, comb)
        experts(kit, "ffn1", xnT, comb, ins["L1_ffn_W1"], ins["L1_ffn_b1"], ins["L1_ffn_W2"], ins["L1_ffn_b2"])


def program(nc, ins, out, stop=99):
    N, D = ins["x"].shape
    T = N // P
    dram = lambda n, s, d: nc.dram_tensor(n, s, d, kind="Internal").ap()
    with ExitStack() as ctx:
        kit = Kit(nc, ctx, N, D)
        adjT_dram = dram("adjT_dram", [N // (2 * P), P, T * 2 * P], BF16)
        edges = ins["L1_ffn_edge_index"]
        edge_dram = (dram("keys_dram", [P, edges.shape[1] // P], F32), dram("count_dram", [N], F32))
        load_nodes(kit, ins["x"])
        if stop > 3:
            edge_histogram(kit, edges, *edge_dram)
        with ExitStack() as own:
            sb = lambda n, s, d: own.enter_context(nc.sbuf_tensor("t1_" + n, s, d))
            tab = {"s_row": dram("s_row", [N], F32), "v_ready": kit.sem("v_ready")}
            for n in ("A", "C", "steep_t", "neg_t", "w_self"):
                tab[n] = sb(n, [P, T], F32)
            tab["X"] = sb("X", [P, T, D + 1], F32)
            tab["V"] = sb("V", [P, T, 2, PARTS, D + 1], BF16)
            with ExitStack() as tmp:
                xn = tmp.enter_context(nc.sbuf_tensor("xn0", [P, T, D], F32))
                xnT = tmp.enter_context(nc.sbuf_tensor("xnT0", [P, T, P], F32))
                layer_norm(kit, "ln0", xn, xnT)
                dense_tables(kit, xn, xnT, ins["adj"], ins["L0_gnn_W"], ins["L0_gnn_a"], tab)
            dense_attention(kit, ins["adj"], adjT_dram, tab)
        if stop > 1:
            rest(nc, kit, ins, adjT_dram, edge_dram, stop)
        x_stored = kit.sem("x_stored")
        with nc.Block() as block:

            @block.sync
            def _(sp):
                sp.dma_start(out.rearrange("(t p) d -> p t d", p=P), kit.x[:]).then_inc(x_stored, 16)
                sp.wait_ge(x_stored, 16)


_INS = ['x', 'adj', 'L0_gnn_W', 'L0_gnn_a', 'L0_ffn_router_w', 'L0_ffn_w1', 'L0_ffn_b1', 'L0_ffn_w2', 'L0_ffn_b2',
        'L1_gnn_W', 'L1_gnn_b', 'L1_gnn_a', 'L1_ffn_W_gat', 'L1_ffn_att_src', 'L1_ffn_att_dst', 'L1_ffn_b_gat',
        'L1_ffn_ln_gamma', 'L1_ffn_ln_beta', 'L1_ffn_W1', 'L1_ffn_b1', 'L1_ffn_W2', 'L1_ffn_b2', 'L1_ffn_edge_index']


def kernel(**inputs):
    import numpy as _np
    import concourse.bacc as _bacc
    from concourse import mybir as _mybir
    from concourse.bass_utils import run_bass_kernel_spmd as _run

    nc = _bacc.Bacc("TRN2", target_bir_lowering=False, num_devices=1)
    arrays, args = {}, {}
    for name in _INS:
        a = _np.ascontiguousarray(inputs[name])
        arrays[f"in_{name}"] = a
        args[name] = nc.dram_tensor(f"in_{name}", a.shape, _mybir.dt.from_np(a.dtype), kind="ExternalInput").ap()
    out = nc.dram_tensor("out_x", inputs["x"].shape, _mybir.dt.float32, kind="ExternalOutput").ap()
    program(nc, args, out)
    r = _run(nc, [arrays], core_ids=[0])
    return r.results[0]["out_x"]
```

```python
from contextlib import ExitStack

import concourse.bass as bass
from concourse import mybir

ALU = mybir.AluOpType
ACT = mybir.ActivationFunctionType
AX = mybir.AxisListType
F32 = mybir.dt.float32
BF16 = mybir.dt.bfloat16
I32 = mybir.dt.int32
U32 = mybir.dt.uint32
RMAX = bass.bass_isa.ReduceOp.max

P = 128
SLOPE = 0.2
LN_EPS = 1e-5
PARTS = 3
STEEP = 2.0 ** 80


class Steps:

    def __init__(self, engine, sem):
        self.engine, self.sem, self.count = engine, sem, 0

    def did(self, instruction):
        self.count += 1
        instruction.then_inc(self.sem, 1)
        return self.count

    def settle(self, count=None):
        self.engine.wait_ge(self.sem, self.count if count is None else count)


def wait_past(engine, sem, value):
    if isinstance(value, int) and value <= 0:
        return
    engine.wait_ge(sem, value)


class Kit:

    def __init__(self, nc, ctx, nodes, feats):
        self.nc, self.ctx = nc, ctx
        self.N, self.D, self.T = nodes, feats, nodes // P
        self.x = ctx.enter_context(nc.sbuf_tensor("x_tiles", [P, self.T, feats], F32))
        self.ident = ctx.enter_context(nc.sbuf_tensor("ident", [P, P], F32))
        self.ident_h = ctx.enter_context(nc.sbuf_tensor("ident_h", [P, P], BF16))
        self.bank = [ctx.enter_context(nc.psum_tensor(f"bank{i}", [P, 512], F32)) for i in range(8)]

    def sem(self, name):
        return self.ctx.enter_context(self.nc.semaphore(name))


def layer_norm(kit, name, xn, xnT, prefetch=None, eps=LN_EPS):
    nc, T = kit.nc, kit.T
    stats_done, sqrt_done, normed = kit.sem(name + "_stats"), kit.sem(name + "_sqrt"), kit.sem(name + "_normed")
    turned, moved = kit.sem(name + "_turned"), [kit.sem(name + "_moved_by_act"), kit.sem(name + "_moved_by_dve")]
    BT = 4
    GT = 2 * BT
    GROUPS = T // GT
    with ExitStack() as own:
        sb = lambda n, s, d: own.enter_context(nc.sbuf_tensor(name + n, s, d))
        stats, mv = sb("_st", [P, T, 6], F32), sb("_mv", [P, T, 2], F32)
        ve, sd, rstd = sb("_ve", [P, T], F32), sb("_sd", [P, T], F32), sb("_rstd", [P, T], F32)
        tiles = lambda g: slice(GT * g, GT * (g + 1))
        bank_tiles = lambda b: slice(BT * b, BT * (b + 1))
        with nc.Block() as block:

            @block.sync
            def _(sp):
                if prefetch is not None:
                    prefetch(sp)

            @block.vector
            def _(dve):
                s = Steps(dve, stats_done)

                def variances(g):
                    for t in range(GT * g, GT * (g + 1)):
                        s.did(dve.bn_stats(stats[:, t, :], kit.x[:, t, :]))
                    s.settle()
                    for t in range(GT * g, GT * (g + 1)):
                        s.did(dve.bn_aggr(mv[:, t, :], stats[:, t, :]))
                    s.settle()
                    s.did(dve.tensor_scalar(ve[:, tiles(g)], mv[:, tiles(g), 1], eps, None, ALU.add))

                def normalise(g):
                    dve.wait_ge(sqrt_done, g + 1)
                    s.did(dve.reciprocal(rstd[:, tiles(g)], sd[:, tiles(g)]))
                    s.settle()
                    for t in range(GT * g, GT * (g + 1)):
                        dve.tensor_scalar(xn[:, t, :], kit.x[:, t, :], mv[:, t, 0:1], rstd[:, t:t + 1],
                                          ALU.subtract, ALU.mult).then_inc(normed, 1)

                def move(g):
                    dve.wait_ge(turned, 2 * g + 2)
                    dve.tensor_copy(xnT[:, bank_tiles(2 * g + 1), :], kit.bank[2 * g + 1][:]).then_inc(moved[1], 1)

                variances(0)
                for g in range(GROUPS):
                    if g + 1 < GROUPS:
                        variances(g + 1)
                    normalise(g)
                    if g > 0:
                        move(g - 1)
                move(GROUPS - 1)
                dve.wait_ge(moved[1], GROUPS)

            @block.scalar
            def _(act):
                def root(g):
                    act.wait_ge(stats_done, (2 * GT + 1) * (g + 1) + max(g - 1, 0))
                    act.activation(sd[:, tiles(g)], ve[:, tiles(g)], ACT.Sqrt).then_inc(sqrt_done, 1)

                def move(g):
                    act.wait_ge(turned, 2 * g + 1)
                    act.copy(xnT[:, bank_tiles(2 * g), :], kit.bank[2 * g][:]).then_inc(moved[0], 1)

                root(0)
                for g in range(GROUPS):
                    if g + 1 < GROUPS:
                        root(g + 1)
                    move(g)
                act.wait_ge(moved[0], GROUPS)

            @block.tensor
            def _(pe):
                for b in range(T // BT):
                    for t in range(BT * b, BT * (b + 1)):
                        pe.wait_ge(normed, t + 1)
                        last = pe.transpose(kit.bank[b][:, (t % BT) * P:(t % BT + 1) * P], xn[:, t, :], kit.ident[:])
                    last.then_inc(turned, 1)


def dense_tables(kit, xn, xnT, adj, W_in, a_in, tab):
    nc, T, D, N = kit.nc, kit.T, kit.D, kit.N
    consts_in, prod, products = kit.sem("dt_consts_in"), kit.sem("dt_dve"), kit.sem("dt_products")
    act_done, pool_done, row_done, row_out = (kit.sem("dt_act"), kit.sem("dt_pool"), kit.sem("dt_row"),
                                              kit.sem("dt_row_out"))
    GROUP = 3
    groups = [list(range(g, min(g + GROUP, T))) for g in range(0, T, GROUP)]
    C130 = D + 2
    with ExitStack() as own:
        sb = lambda n, s, d: own.enter_context(nc.sbuf_tensor("dt_" + n, s, d))
        cat = sb("cat", [P, C130], F32)
        ab = sb("ab", [P, 2 * D], F32)
        scratch = sb("scratch", [P, D], F32)
        Wh = sb("Wh", [P, T, C130], F32)
        diag = sb("diag", [P, T], F32)
        row = sb("row", [1, N], F32)
        tm, tall = sb("tm", [P, 1], F32), sb("tall", [P, 1], F32)
        nt, nt2, u, m, e1, e2 = (sb(n, s, F32) for n, s in
                                 (("nt", [P, 1]), ("nt2", [P, 1]), ("u", [P, T]), ("m", [P, T]), ("e1", [P, T]),
                                  ("e2", [P, T])))
        B, Dc, w1, w2 = (sb(n, [P, T], F32) for n in ("B", "D", "w1", "w2"))
        v = [sb(f"v{i}", [P, T, D + 1], F32) for i in range(2)]

        def load_all(sp):
            sp.dma_start(cat[:, 0:D], W_in).then_inc(consts_in, 16)
            sp.dma_start(ab[:], a_in.unsqueeze(0).to_broadcast([P, 2 * D])).then_inc(consts_in, 16)
            flat = adj.rearrange("i j -> (i j)")
            step = bass.AP(flat.tensor, 0, [[N + 1, P], [P * (N + 1), T]])
            sp.dma_start(diag[:], step, allow_slow_non_contiguous=True).then_inc(consts_in, 16)

        layer_norm(kit, "ln0", xn, xnT, prefetch=load_all)
        with nc.Block() as block:

            @block.sync
            def _(sp):
                sp.wait_ge(row_done, 8)
                sp.dma_start(tab["s_row"].unsqueeze(0), row[:]).then_inc(row_out, 16)
                sp.wait_ge(row_out, 16)

            @block.tensor
            def _(pe):
                pe.wait_ge(prod, 2)
                for g, tiles in enumerate(groups):
                    if g >= 8:
                        pe.wait_ge(act_done, g - 7)
                    for k, t in enumerate(tiles):
                        last = pe.matmul(kit.bank[g % 8][:, k * C130:(k + 1) * C130], xnT[:, t, :], cat[:],
                                         start=True, stop=True)
                    last.then_inc(products, 1)
                for q in range(8):
                    b = (len(groups) + q) % 8
                    pe.wait_ge(act_done, min(len(groups), len(groups) + q - 7))
                    if len(groups) + q - 8 >= len(groups):
                        pe.wait_ge(row_done, q - 7)
                    pe.matmul(kit.bank[b][0:1, :], cat[:, D + 1:D + 2], xnT[:, 4 * q:4 * q + 4, :],
                              start=True, stop=True).then_inc(products, 1)

            @block.scalar
            def _(act):
                for g, tiles in enumerate(groups):
                    act.wait_ge(products, g + 1)
                    act.copy(Wh[:, tiles[0]:tiles[-1] + 1, :],
                             kit.bank[g % 8][:, 0:len(tiles) * C130]).then_inc(act_done, 1)
                n = len(groups)
                for q in range(8):
                    act.wait_ge(products, n + q + 1)
                    act.copy(row[:, 512 * q:512 * (q + 1)], kit.bank[(n + q) % 8][0:1, :]).then_inc(row_done, 1)
                s = Steps(act, act_done)
                s.count = n
                act.wait_ge(prod, 6)
                s.did(act.activation(B[:], Wh[:, :, D], ACT.Exp, bias=nt[:, 0:1]))
                s.did(act.activation(Dc[:], Wh[:, :, D], ACT.Exp, bias=nt2[:, 0:1], scale=SLOPE))
                act.wait_ge(prod, 9)
                s.did(act.activation(tab["A"][:], e1[:], ACT.Exp))
                s.did(act.activation(tab["C"][:], e2[:], ACT.Exp))
                for part in range(2):
                    for side in range(2):
                        act.wait_ge(tab["v_ready"], 2 * part + side + 1)
                        s.did(act.copy(tab["V"][:, :, side, part, :], v[side][:]))

            @block.gpsimd
            def _(pool):
                for r in range(2):
                    pool.dma_start(tab["rows"][r][:], adj[r * P:(r + 1) * P, :]).then_inc(tab["rows_in"][r], 16)
                pool.wait_ge(prod, 3)
                pool.partition_all_reduce(tall[:], tm[:], P, RMAX).then_inc(pool_done, 1)

            @block.vector
            def _(dve):
                s = Steps(dve, prod)
                n = len(groups)
                dve.wait_ge(consts_in, 48)
                s.did(dve.tensor_tensor_reduce(scratch[:], cat[:, 0:D], ab[:, D:2 * D], 1.0, 0.0, ALU.mult,
                                               ALU.add, cat[:, D:D + 1]))
                s.settle()
                s.did(dve.tensor_tensor_reduce(scratch[:], cat[:, 0:D], ab[:, 0:D], 1.0, 0.0, ALU.mult,
                                               ALU.add, cat[:, D + 1:D + 2]))
                dve.wait_ge(act_done, n)
                s.did(dve.reduce_max(tm[:], Wh[:, :, D], AX.X))
                dve.wait_ge(pool_done, 1)
                s.did(dve.tensor_scalar(nt[:], tall[:], -1.0, None, ALU.mult))
                s.did(dve.tensor_scalar(nt2[:], tall[:], -SLOPE, None, ALU.mult))
                s.did(dve.tensor_scalar(u[:], Wh[:, :, D + 1], tall[:, 0:1], None, ALU.add))
                s.settle()
                s.did(dve.scalar_tensor_tensor(out=m[:], in0=u[:], scalar=SLOPE, in1=u[:], op0=ALU.mult,
                                               op1=ALU.max))
                s.settle()
                s.did(dve.tensor_tensor(e1[:], u[:], m[:], ALU.subtract))
                s.did(dve.scalar_tensor_tensor(out=e2[:], in0=u[:], scalar=SLOPE, in1=m[:], op0=ALU.mult,
                                               op1=ALU.subtract))
                dve.wait_ge(act_done, n + 4)
                s.did(dve.tensor_tensor(w1[:], tab["A"][:], B[:], ALU.mult))
                s.did(dve.tensor_tensor(w2[:], tab["C"][:], Dc[:], ALU.mult))
                s.did(dve.tensor_scalar(tab["steep_t"][:], Wh[:, :, D], STEEP, None, ALU.mult))
                s.did(dve.tensor_scalar(tab["neg_t"][:], Wh[:, :, D], -1.0, None, ALU.mult))
                s.settle()
                s.did(dve.tensor_tensor(w1[:], w1[:], w2[:], ALU.max))
                s.did(dve.memset(Wh[:, :, D:D + 1], 1.0))
                s.settle()
                s.did(dve.scalar_tensor_tensor(out=tab["w_self"][:], in0=diag[:], scalar=0.0, in1=w1[:],
                                               op0=ALU.is_le, op1=ALU.mult))
                s.did(dve.tensor_copy(tab["X"][:], Wh[:, :, 0:D + 1]))
                s.settle()
                for side, coef in enumerate((B, Dc)):
                    dve.tensor_tensor(v[side][:], Wh[:, :, 0:D + 1], coef[:].unsqueeze(2).to_broadcast([P, T, D + 1]),
                                      ALU.mult).then_inc(tab["v_ready"], 1)
                for part in range(2):
                    for side in range(2):
                        dve.wait_ge(act_done, n + 4 + 2 * part + side + 1)
                        dve.wait_ge(tab["v_ready"], 2 * part + side + 1)
                        rest_of = v[side][:] if part == 0 else tab["V"][:, :, side, 2, :]
                        dve.tensor_tensor(rest_of, v[side][:], tab["V"][:, :, side, part, :],
                                          ALU.subtract).then_inc(tab["v_ready"], 1)
                dve.wait_ge(tab["v_ready"], 6)
                s.settle()


def peeled_loop(engine, count, step):
    step(0)
    if count > 2:
        with engine.Fori(1, count - 1) as k:
            step(k)
    step(count - 1)


def dense_attention(kit, adj, adjT_out, tab):
    nc, T, D, N = kit.nc, kit.T, kit.D, kit.N
    CH = 2 * P
    CHUNKS, RT = N // CH, CH // P
    UNIT = 8
    UNITS = T // UNIT
    W = PARTS * (D + 1)
    STEPS = 8
    TURNS = 4
    BY_ACT = (1, 3)
    compares = [j for u in BY_ACT for j in range(UNIT * u, UNIT * (u + 1))]
    rows, rows_in = tab["rows"], tab["rows_in"]
    s_in = [kit.sem(f"s_in{i}") for i in range(2)]
    adjT_stored = [kit.sem(f"adjT_stored{i}") for i in range(2)]
    turned, placed, compared, masked, split = (kit.sem(n) for n in ("turned", "placed", "compared", "masked",
                                                                    "split"))
    multiplied, moved, finish = (kit.sem(n) for n in ("multiplied", "moved", "finish"))
    turn_bank = [kit.bank[4 + i][:].bitcast(BF16).rearrange("p (b i) -> p b i", b=UNIT) for i in range(TURNS)]
    with ExitStack() as own:
        sb = lambda n, s, d: own.enter_context(nc.sbuf_tensor("da_" + n, s, d))
        adjT = [sb(f"adjT{i}", [P, T, CH], BF16) for i in range(2)]
        pos = [sb(f"pos{i}", [P, T, CH], BF16) for i in range(2)]
        neg = [sb(f"neg{i}", [P, T, CH], BF16) for i in range(2)]
        srow = [sb(f"srow{i}", [P, CH], F32) for i in range(2)]
        sums = [[sb(f"sum{k}_{i}", [P, W], F32) for k in range(2)] for i in range(2)]
        z = sb("z", [P, W], F32)
        zr, zs, rden = sb("zr", [P, D + 1], F32), sb("zs", [P, D + 1], F32), sb("rden", [P, 1], F32)
        with nc.Block() as block:

            @block.gpsimd
            def _(pool):
                def pair(k):
                    for n in range(2 * RT):
                        r = 2 * RT * k + n
                        if isinstance(r, int) and r < 2:
                            continue
                        wait_past(pool, turned, UNITS * (r - 1))
                        pool.dma_start(rows[n % 2][:], adj[bass.ds(r * P, P), :]).then_inc(rows_in[n % 2], 16)

                peeled_loop(pool, CHUNKS // 2, pair)

            @block.sync
            def _(sp):
                def pair(k):
                    for par in range(2):
                        c = 2 * k + par
                        wait_past(sp, masked, T * (c - 1))
                        sp.dma_start(srow[par][:], tab["s_row"][bass.ds(c * CH, CH)].unsqueeze(0)
                                     .to_broadcast([P, CH])).then_inc(s_in[par], 16)

                peeled_loop(sp, CHUNKS // 2, pair)

            @block.vector
            def _(dve):
                def mask(c, par, k):
                    def split_off(u):
                        dve.wait_ge(masked, T * c + UNIT * (u + 1))
                        at = slice(UNIT * u, UNIT * (u + 1))
                        dve.tensor_tensor(neg[par][:, at, :], adjT[par][:, at, :], pos[par][:, at, :],
                                          ALU.subtract).then_inc(split, 1)

                    wait_past(dve, multiplied, RT * (c - 1))
                    dve.wait_ge(s_in[par], 16 * (k + 1))
                    for u in range(UNITS):
                        dve.wait_ge(placed, RT * UNITS * c + (RT - 1) * UNITS + u + 1)
                        if u in BY_ACT:
                            dve.wait_ge(compared, UNIT * (len(BY_ACT) * c + BY_ACT.index(u) + 1))
                            at = slice(UNIT * u, UNIT * (u + 1))
                            dve.tensor_tensor(pos[par][:, at, :], pos[par][:, at, :], adjT[par][:, at, :],
                                              ALU.mult).then_inc(masked, UNIT)
                        else:
                            for j in range(UNIT * u, UNIT * (u + 1)):
                                dve.scalar_tensor_tensor(
                                    out=pos[par][:, j, :], in0=srow[par][:], scalar=tab["neg_t"][:, j:j + 1],
                                    in1=adjT[par][:, j, :], op0=ALU.is_gt, op1=ALU.mult).then_inc(masked, 1)
                        if u > 0:
                            split_off(u - 1)
                    split_off(UNITS - 1)

                def finish_tile(t, i):
                    from_pos, from_neg = sums[i]
                    done = lambda n: STEPS * t + n
                    dve.wait_ge(moved, 2 * t + 2)
                    wait_past(dve, finish, done(0))
                    dve.tensor_scalar(z[:], from_pos[:], tab["A"][:, bass.ds(t, 1)], None, ALU.mult).then_inc(finish, 1)
                    dve.wait_ge(finish, done(1))
                    dve.scalar_tensor_tensor(out=z[:], in0=from_neg[:], scalar=tab["C"][:, bass.ds(t, 1)], in1=z[:],
                                             op0=ALU.mult, op1=ALU.add).then_inc(finish, 1)
                    dve.wait_ge(finish, done(2))
                    dve.tensor_reduce(zr[:], z[:].rearrange("p (k c) -> p c k", k=PARTS), AX.X,
                                      ALU.add).then_inc(finish, 1)
                    dve.wait_ge(finish, done(3))
                    dve.scalar_tensor_tensor(out=zs[:], in0=tab["X"][:, bass.ds(t, 1), :].squeeze(1),
                                             scalar=tab["w_self"][:, bass.ds(t, 1)], in1=zr[:], op0=ALU.mult,
                                             op1=ALU.add).then_inc(finish, 1)
                    dve.wait_ge(finish, done(4))
                    dve.reciprocal(rden[:], zs[:, D:D + 1]).then_inc(finish, 1)
                    dve.wait_ge(finish, done(5))
                    xt = kit.x[:, bass.ds(t, 1), :].squeeze(1)
                    dve.scalar_tensor_tensor(out=xt, in0=zs[:, 0:D], scalar=rden[:, 0:1], in1=xt, op0=ALU.mult,
                                             op1=ALU.add).then_inc(finish, 3)

                def pair(k):
                    for par in range(2):
                        c = 2 * k + par
                        if not isinstance(c, int) or c + 1 < CHUNKS:
                            mask(c + 1, 1 - par, k + par)
                        if not isinstance(c, int) or c > 0:
                            finish_tile(RT * c - 1, 1)
                        finish_tile(RT * c, 0)

                mask(0, 0, 0)
                peeled_loop(dve, CHUNKS // 2, pair)
                finish_tile(T - 1, 1)
                dve.wait_ge(finish, STEPS * T)

            @block.scalar
            def _(act):
                def place(c, par, k):
                    wait_past(act, masked, T * (c - 1))
                    wait_past(act, split, UNITS * (c - 1))
                    wait_past(act, adjT_stored[par], 16 * k)
                    wait_past(act, multiplied, RT * (c - 1))
                    act.wait_ge(s_in[par], 16 * (k + 1))
                    for u in range(RT * UNITS):
                        i, b = u // UNITS, u % UNITS
                        act.wait_ge(turned, RT * UNITS * c + u + 1)
                        act.activation(adjT[par][:, UNIT * b:UNIT * (b + 1), i * P:(i + 1) * P],
                                       turn_bank[u % TURNS], ACT.Sign).then_inc(placed, 1)
                        for j in compares[len(compares) * u // (RT * UNITS):len(compares) * (u + 1) // (RT * UNITS)]:
                            act.activation(pos[par][:, j, :], srow[par][:], ACT.Sigmoid, scale=STEEP,
                                           bias=tab["steep_t"][:, j:j + 1]).then_inc(compared, 1)
                    act.wait_ge(placed, RT * UNITS * (c + 1))
                    act.dma_start(adjT_out[bass.ds(c, 1), :, :].squeeze(0), adjT[par][:].rearrange("p t i -> p (t i)")
                                  ).then_inc(adjT_stored[par], 16)

                def move(t, i):
                    act.wait_ge(multiplied, t + 1)
                    wait_past(act, finish, STEPS * (t - 1))
                    for n in range(2):
                        act.copy(sums[i][n][:], kit.bank[2 * i + n][:, 0:W]).then_inc(moved, 1)

                def pair(k):
                    for par in range(2):
                        c = 2 * k + par
                        if not isinstance(c, int) or c > 0:
                            move(RT * c - 1, 1)
                        if not isinstance(c, int) or c + 1 < CHUNKS:
                            place(c + 1, 1 - par, k + par)
                        move(RT * c, 0)

                place(0, 0, 0)
                peeled_loop(act, CHUNKS // 2, pair)
                move(T - 1, 1)
                for par in range(2):
                    act.wait_ge(adjT_stored[par], 16 * (CHUNKS // 2))

            @block.tensor
            def _(pe):
                def turn(c, units):
                    for u in units:
                        i, b = u // UNITS, u % UNITS * UNIT
                        pe.wait_ge(rows_in[i], 16 * (c + 1))
                        wait_past(pe, placed, RT * UNITS * c + u - TURNS + 1)
                        for j in range(UNIT):
                            last = pe.transpose(turn_bank[u % TURNS][:, j, :], rows[i][:, (b + j) * P:(b + j + 1) * P],
                                                kit.ident_h[:])
                        last.then_inc(turned, 1)

                def multiply(c, par, t, i, turns):
                    wait_past(pe, moved, 2 * t - 2)
                    for j in range(T):
                        if j % UNIT == 0:
                            pe.wait_ge(split, UNITS * c + j // UNIT + 1)
                        at = slice(i * P, (i + 1) * P)
                        for n, lhs in enumerate((pos, neg)):
                            last = pe.matmul(kit.bank[2 * i + n][:, 0:W], lhs[par][:, j, at],
                                             tab["V"][:, j, n, :, :], start=(j == 0), stop=(j == T - 1))
                        if j == T - 1:
                            last.then_inc(multiplied, 1)
                        if turns and j % UNIT == UNIT - 1:
                            turn(c + 1, range(RT * (j // UNIT), RT * (j // UNIT + 1)))

                def pair(k):
                    for par in range(2):
                        c = 2 * k + par
                        multiply(c, par, RT * c, 0, not isinstance(c, int) or c + 1 < CHUNKS)
                        multiply(c, par, RT * c + 1, 1, False)

                turn(0, range(RT * UNITS))
                peeled_loop(pe, CHUNKS // 2, pair)


def router(kit, xn, xnT, router_w, comb):
    nc, T = kit.nc, kit.T
    E = router_w.shape[0]
    w_in, logits_done, exp_done, steps = (kit.sem(n) for n in ("rt_w_in", "rt_logits", "rt_exp", "rt_steps"))
    logits = kit.bank[0][:, 0:T * E].rearrange("p (t e) -> p t e", e=E)
    with ExitStack() as own:
        sb = lambda n, s: own.enter_context(nc.sbuf_tensor("rt_" + n, s, F32))
        rw = sb("rw", [P, E])
        prob, ranked, keep = sb("prob", [P, T, E]), sb("ranked", [P, T, E]), sb("keep", [P, T, E])
        top, total, rtotal, two, rtwo = (sb(n, [P, T]) for n in ("top", "total", "rtotal", "two", "rtwo"))
        wide = lambda a: a[:].unsqueeze(2).to_broadcast([P, T, E])

        def load_all(sp):
            sp.dma_start(rw[:], router_w.rearrange("e d -> d e"), allow_slow_non_contiguous=True).then_inc(w_in, 16)

        layer_norm(kit, "ln1", xn, xnT, prefetch=load_all)
        with nc.Block() as block:

            @block.tensor
            def _(pe):
                pe.wait_ge(w_in, 16)
                for t in range(T):
                    last = pe.matmul(logits[:, t, :], xnT[:, t, :], rw[:], start=True, stop=True)
                last.then_inc(logits_done, 1)

            @block.scalar
            def _(act):
                act.wait_ge(steps, 2)
                act.activation(prob[:], keep[:], ACT.Exp).then_inc(exp_done, 1)

            @block.vector
            def _(dve):
                s = Steps(dve, steps)
                dve.wait_ge(logits_done, 1)
                s.did(dve.tensor_reduce(top[:], logits, AX.X, ALU.max))
                s.settle()
                s.did(dve.tensor_tensor(keep[:], logits, wide(top), ALU.subtract))
                dve.wait_ge(exp_done, 1)
                s.did(dve.tensor_reduce(total[:], prob[:], AX.X, ALU.add))
                s.settle()
                s.did(dve.reciprocal(rtotal[:], total[:]))
                s.settle()
                s.did(dve.tensor_tensor(prob[:], prob[:], wide(rtotal), ALU.mult))
                s.settle()
                for t in range(T):
                    s.did(dve.max(ranked[:, t, :], prob[:, t, :]))
                s.settle()
                s.did(dve.tensor_tensor(two[:], ranked[:, :, 0], ranked[:, :, 1], ALU.add))
                s.did(dve.tensor_tensor(keep[:], prob[:], ranked[:, :, 1:2].to_broadcast([P, T, E]), ALU.is_ge))
                s.settle()
                s.did(dve.tensor_scalar(two[:], two[:], 1e-12, None, ALU.max))
                s.did(dve.tensor_tensor(keep[:], keep[:], prob[:], ALU.mult))
                s.settle()
                s.did(dve.reciprocal(rtwo[:], two[:]))
                s.settle()
                s.did(dve.tensor_tensor(comb[:], keep[:], wide(rtwo), ALU.mult))
                s.settle()


def experts_and_histogram(kit, name, xnT, xn, comb, w1, b1, w2, b2, digits_dram, count_dram):
    nc, T, D = kit.nc, kit.T, kit.D
    E, _, F = w1.shape
    assert F == P
    CT = 4
    HS = 4
    CHUNKS = T // CT
    R = 64
    SUBS = 2 * CHUNKS
    SUB = digits_dram.shape[2] // SUBS
    BY_ACT = 35
    digits_of_dve = [(0, v) for v in range(R)] + [(1, v) for v in range(BY_ACT, R)]
    GR = E // 2
    sem = lambda n: kit.sem(f"{name}_{n}")
    w_in, turned, comb_turned, biased, mixed, base = (sem(n) for n in ("w_in", "turned", "comb_turned", "biased",
                                                                        "mixed", "base"))
    hidden, activated, projected, added = (sem(n) for n in ("hidden", "activated", "projected", "added"))
    digits_in = [sem(f"digits_in{i}") for i in range(2)]
    numbers, hot_dve, hot_act, counted, count_steps, count_out = (
        sem(n) for n in ("numbers", "hot_dve", "hot_act", "counted", "count_steps", "count_out"))
    hist = kit.bank[6][0:R, 0:R + 1]
    with ExitStack() as own:
        sb = lambda n, s, d=F32: own.enter_context(nc.sbuf_tensor(f"{name}_{n}", s, d))
        W1, W2, B1, B2 = sb("W1", [P, E, F]), sb("W2", [P, E, D]), sb("B1", [P, E]), sb("B2", [E, D])
        hs = sb("hs", [P, HS, CT * P])
        digits = [sb(f"digits{i}", [P, 2, SUB], BF16) for i in range(2)]
        hot_hi = [sb(f"hot_hi{i}", [P, R, SUB], BF16) for i in range(2)]
        hot_lo = [sb(f"hot_lo{i}", [P, R + 1, SUB], BF16) for i in range(2)]
        combT = hot_hi[1][0:E, 0:2 * T * P // SUB, :].rearrange("e r s -> e (r s)").bitcast(F32).rearrange(
            "e (t p) -> e t p", t=T)
        half_i, halves = sb("half_i", [P, BY_ACT], I32), sb("halves", [P, BY_ACT])
        counts, steps_of = sb("counts", [R, R + 1]), sb("steps_of", [R, BY_ACT])
        with nc.Block() as block:

            @block.sync
            def _(sp):
                sp.dma_start(W1[:], w1.rearrange("e d f -> d e f")).then_inc(w_in, 16)
                sp.dma_start(W2[:], w2.rearrange("e f d -> f e d")).then_inc(w_in, 16)
                sp.dma_start(B1[:], b1.rearrange("e f -> f e"), allow_slow_non_contiguous=True).then_inc(w_in, 16)
                sp.dma_start(B2[:], b2).then_inc(w_in, 16)

                def pair(k):
                    for i in range(2):
                        wait_past(sp, hot_dve, 2 * k + i - 1)
                        wait_past(sp, hot_act, 2 * k + i - 1)
                        sp.dma_start(digits[i][:], digits_dram[:, :, bass.ds((2 * k + i) * SUB, SUB)]
                                     ).then_inc(digits_in[i], 16)

                peeled_loop(sp, SUBS // 2, pair)
                sp.wait_ge(count_steps, 3)
                sp.dma_start(count_dram.rearrange("(a b) -> a b", a=R), counts[:, 1:R + 1]).then_inc(count_out, 16)
                sp.wait_ge(count_out, 16)

            @block.gpsimd
            def _(pool):
                nc.gpsimd.iota(half_i[:], pattern=[[1, BY_ACT]], base=0, channel_multiplier=0).then_inc(numbers, 1)

            @block.tensor
            def _(pe):
                for g in range(CHUNKS):
                    wait_past(pe, comb_turned, g - 1)
                    for i in range(CT):
                        last = pe.transpose(kit.bank[4 + g % 2][0:E, i * P:(i + 1) * P], comb[:, CT * g + i, :],
                                            kit.ident[:])
                    last.then_inc(turned, 1)
                pe.wait_ge(w_in, 64)
                for g in range(CHUNKS):
                    pe.wait_ge(comb_turned, g + 1)
                    wait_past(pe, base, g - 1)
                    for i in range(CT):
                        last = pe.matmul(kit.bank[6 + g % 2][:, i * P:(i + 1) * P], combT[:, CT * g + i, :], B2[:],
                                         start=True, stop=True)
                    last.then_inc(biased, 1)
                pe.wait_ge(base, CHUNKS)

                def count(s, i, edges, first=False, final=False):
                    if edges[0] == 0:
                        pe.wait_ge(hot_dve, s + 1)
                        pe.wait_ge(hot_act, s + 1)
                    for e in edges:
                        last = pe.matmul(hist, hot_hi[i][:, :, e], hot_lo[i][:, :, e], start=first and e == 0,
                                         stop=final and e == SUB - 1, skip_group_check=True)
                    if edges[-1] == SUB - 1:
                        last.then_inc(counted, 1)

                def chunk(q):
                    first = isinstance(q, int) and q == 0

                    def project(e):
                        pe.wait_ge(activated, E * q + e + 1)
                        wait_past(pe, added, CT * (E * q + e - 3))
                        for i in range(CT):
                            last = pe.matmul(kit.bank[2 + e % 4][:, i * P:(i + 1) * P],
                                             hs[:, e % HS, i * P:(i + 1) * P], W2[:, e, :], start=True, stop=True)
                        last.then_inc(projected, 1)

                    for e in range(E):
                        wait_past(pe, activated, E * q + e - 1)
                        pe.matmul(kit.bank[e % 2][:], W1[:, e, :], xnT[:, bass.ds(CT * q, CT), :],
                                  start=True, stop=True).then_inc(hidden, 1)
                        if e < GR and not first:
                            count(2 * q - 1, 1, range(SUB // GR * e, SUB // GR * (e + 1)))
                        if e > GR:
                            n = GR - 1
                            count(2 * q, 0, range(SUB * (e - GR - 1) // n, SUB * (e - GR) // n), first=first)
                        if e >= 1:
                            project(e - 1)
                    project(E - 1)

                peeled_loop(pe, CHUNKS, chunk)
                count(SUBS - 1, 1, range(SUB), final=True)

            @block.scalar
            def _(act):
                for g in range(CHUNKS):
                    act.wait_ge(turned, g + 1)
                    act.copy(combT[:, CT * g:CT * (g + 1), :], kit.bank[4 + g % 2][0:E, :]).then_inc(comb_turned, 1)
                act.wait_ge(w_in, 64)
                act.wait_ge(count_steps, 1)

                def chunk(q):
                    for e in range(E):
                        i, group, s = e // GR, e % GR, 2 * q + e // GR
                        if group == 0:
                            act.wait_ge(digits_in[i], 16 * (q + 1))
                            wait_past(act, counted, s - 1)
                        for v in range(BY_ACT * group // GR, BY_ACT * (group + 1) // GR):
                            last = act.activation(hot_lo[i][:, v + 1, :], digits[i][:, 1, :], ACT.Sign, scale=-1.0,
                                                  bias=halves[:, v:v + 1])
                        if group == GR - 1:
                            last.then_inc(hot_act, 1)
                        wait_past(act, projected, E * q + e - HS + 1)
                        act.wait_ge(hidden, E * q + e + 1)
                        act.activation(hs[:, e % HS, :], kit.bank[e % 2][:], ACT.Gelu,
                                       bias=B1[:, e:e + 1]).then_inc(activated, 1)

                peeled_loop(act, CHUNKS, chunk)

            @block.vector
            def _(dve):
                dve.wait_ge(numbers, 1)
                dve.tensor_scalar(halves[:], half_i[:], 0.5, None, ALU.add).then_inc(count_steps, 1)
                for i in range(2):
                    dve.memset(hot_lo[i][:, 0, :], -1.0)
                for g in range(CHUNKS):
                    at = slice(CT * g, CT * (g + 1))
                    dve.tensor_tensor(xn[:, at, :], xn[:, at, :], kit.x[:, at, :], ALU.add).then_inc(mixed, 1)
                    dve.wait_ge(biased, g + 1)
                    dve.wait_ge(mixed, g + 1)
                    dve.tensor_tensor(kit.x[:, at, :], kit.bank[6 + g % 2][:], xn[:, at, :].rearrange("p t d -> p (t d)"),
                                      ALU.add).then_inc(base, 1)
                dve.wait_ge(base, CHUNKS)

                def chunk(q):
                    def add(e):
                        dve.wait_ge(projected, E * q + e + 1)
                        wait_past(dve, added, CT * (E * q + e))
                        for i in range(CT):
                            xt = kit.x[:, bass.ds(CT * q + i, 1), :].squeeze(1)
                            dve.scalar_tensor_tensor(out=xt, in0=kit.bank[2 + e % 4][:, i * P:(i + 1) * P],
                                                     scalar=comb[:, bass.ds(CT * q + i, 1), e], in1=xt,
                                                     op0=ALU.mult, op1=ALU.add).then_inc(added, 1)

                    for g in range(E):
                        i, group, s = g // GR, g % GR, 2 * q + g // GR
                        if group == 0:
                            dve.wait_ge(digits_in[i], 16 * (q + 1))
                            wait_past(dve, counted, s - 1)
                        n = len(digits_of_dve)
                        for digit, v in digits_of_dve[n * group // GR:n * (group + 1) // GR]:
                            out = hot_lo[i][:, v + 1, :] if digit else hot_hi[i][:, v, :]
                            last = dve.tensor_scalar(out, digits[i][:, digit, :], float(v), None, ALU.is_equal)
                        if group == GR - 1:
                            last.then_inc(hot_dve, 1)
                        if g >= 2:
                            add(g - 2)
                    add(E - 2)
                    add(E - 1)

                peeled_loop(dve, CHUNKS, chunk)
                dve.wait_ge(added, T * E)
                dve.wait_ge(counted, SUBS)
                dve.tensor_copy(counts[:], hist).then_inc(count_steps, 1)
                dve.wait_ge(count_steps, 2)
                dve.tensor_tensor(steps_of[:], counts[:, 1:BY_ACT + 1], counts[:, 0:BY_ACT], ALU.subtract
                                  ).then_inc(mixed, 1)
                dve.wait_ge(mixed, CHUNKS + 1)
                dve.tensor_scalar(counts[:, 1:BY_ACT + 1], steps_of[:], 0.5, None, ALU.mult).then_inc(count_steps, 1)
                dve.wait_ge(count_steps, 3)




def head_tables(kit, xn, xnT, Wg, bg, ag, tab):
    nc, T, D, N = kit.nc, kit.T, kit.D, kit.N
    H = ag.shape[0]
    HC = D // H
    G1 = HC + 1
    CAT = D + 2 * H
    loads, steps, products, act_done, pool_done, row_done, row_out = (
        kit.sem("ht_" + n) for n in ("loads", "steps", "products", "act", "pool", "row_done", "row_out"))
    GROUP = 512 // CAT
    groups = [list(range(g, min(g + GROUP, T))) for g in range(0, T, GROUP)]
    n_g = len(groups)
    with ExitStack() as own:
        sb = lambda n, s: own.enter_context(nc.sbuf_tensor("ht_" + n, s, F32))
        Wraw, cat, bias = sb("Wraw", [P, D]), sb("cat", [P, CAT]), sb("bias", [P, CAT])
        a_all, tmp = sb("a", [P, H, 2 * HC]), sb("tmp", [P, H, HC])
        F = sb("F", [P, T, CAT])
        row = xn[0:H, :, :].rearrange("p t d -> p (t d)")
        bcol = sb("bcol", [H, 1])
        ones = sb("ones", [P, P])
        cm, call = sb("cm", [P, H]), sb("call", [P, H])
        cs, u, m, e1, e2, B, Dc = (sb(n, [P, T, H]) for n in ("cs", "u", "m", "e1", "e2", "B", "D"))
        X = sb("X", [P, T, H, G1])
        v = [sb("v", [P, T, H, G1])[:],
             F[:].rearrange("p t c -> p (t c)")[:, 0:T * H * G1].rearrange("p (t h c) -> p t h c", t=T, h=H)]
        rounds = [(0, 0), (1, 0), (0, 1), (1, 1), (2, 0), (2, 1)]
        makes_and_rests = [(1, None), (0, 0), (1, 0), (0, 1), (2, None), (1, 1), (2, 0), (2, 1)]
        source_made = {(0, 0): 1, (1, 0): 2, (0, 1): 3, (1, 1): 4, (2, 0): 6, (2, 1): 8}
        def part_of(side, part):
            if side == 0:
                return tab["VX"][:, :, part, :, :]
            return tab["VH"][:, :, :, part, (side - 1) * G1:side * G1]

        over_tiles = lambda a: a[:].unsqueeze(1).to_broadcast([P, T, H])
        over_cols = lambda a: a[:].rearrange("p t h -> p (t h)").unsqueeze(2).to_broadcast([P, T * H, G1])
        flat = lambda a: a.rearrange("p t h c -> p (t h) c")

        def load_all(sp):
            sp.dma_start(Wraw[:], Wg).then_inc(loads, 16)
            sp.dma_start(bias[:, 0:D], bg.unsqueeze(0).to_broadcast([P, D])).then_inc(loads, 16)
            sp.dma_start(a_all[:].rearrange("p h c -> p (h c)"),
                         ag.rearrange("h c -> (h c)").unsqueeze(0).to_broadcast([P, H * 2 * HC])).then_inc(loads, 16)

        layer_norm(kit, "ln2", xn, xnT, prefetch=load_all)
        with nc.Block() as block:

            @block.sync
            def _(sp):
                sp.wait_ge(row_done, 8)
                sp.dma_start(tab["p_rows"], row).then_inc(row_out, 16)
                sp.wait_ge(row_out, 16)

            @block.tensor
            def _(pe):
                pe.wait_ge(loads, 48)
                pe.transpose(kit.bank[0][:, 0:P], Wraw[:], kit.ident[:]).then_inc(products, 1)
                pe.wait_ge(steps, 9)
                pe.matmul(kit.bank[1][0:H, 0:1], bias[0:1, D:D + H], kit.ident[0:1, 0:1], start=True,
                          stop=True).then_inc(products, 1)
                for g, tiles in enumerate(groups):
                    if g >= 6:
                        pe.wait_ge(steps, 10 + g - 5)
                    for k, t in enumerate(tiles):
                        last = pe.matmul(kit.bank[2 + g % 6][:, k * CAT:(k + 1) * CAT], xnT[:, t, :], cat[:],
                                         start=True, stop=True)
                    last.then_inc(products, 1)
                pe.wait_ge(steps, 10)
                for q in range(8):
                    wait_past(pe, row_done, q - 1)
                    pe.matmul(kit.bank[q % 2][0:H, :], cat[:, D:D + H], xnT[:, 4 * q:4 * q + 4, :], start=True,
                              stop=True).then_inc(products, 1)
                pe.wait_ge(steps, 10 + n_g + 2)
                for t in range(T):
                    last = pe.matmul(kit.bank[2][:, 0:H * G1], ones[:], X[:, t, :, :], start=(t == 0),
                                     stop=(t == T - 1))
                last.then_inc(products, 1)

            @block.gpsimd
            def _(pool):
                pool.wait_ge(steps, 10 + n_g + 3)
                pool.partition_all_reduce(call[:], cm[:], P, RMAX).then_inc(pool_done, 1)

            @block.scalar
            def _(act):
                s = Steps(act, act_done)
                act.wait_ge(steps, 10)
                for q in range(8):
                    act.wait_ge(products, 2 + n_g + q + 1)
                    act.activation(row[:, 512 * q:512 * (q + 1)], kit.bank[q % 2][0:H, :], ACT.Identity,
                                   bias=bcol[:, 0:1]).then_inc(row_done, 1)
                act.wait_ge(steps, 10 + n_g + 4)
                s.did(act.activation(B[:], cs[:], ACT.Exp))
                s.did(act.activation(Dc[:], cs[:], ACT.Exp, scale=SLOPE))
                act.wait_ge(steps, 10 + n_g + 8)
                s.did(act.activation(tab["A"][:], e1[:], ACT.Exp))
                s.did(act.activation(tab["C"][:], e2[:], ACT.Exp))
                s.did(act.activation(tab["E"][:], m[:], ACT.Exp, scale=-1.0))
                for side, part in rounds:
                    source = X[:] if side == 0 and part == 0 else v[side % 2]
                    act.wait_ge(tab["hv_ready"], source_made[side, part])
                    s.did(act.copy(part_of(side, part), source))

            @block.vector
            def _(dve):
                s = Steps(dve, steps)
                dve.wait_ge(loads, 48)
                dve.wait_ge(products, 1)
                s.did(dve.tensor_copy(cat[:, 0:D], kit.bank[0][:, 0:P]))
                s.settle()
                for src in (cat, bias):
                    view = src[:, 0:D].rearrange("p (h c) -> p h c", h=H)
                    for half in range(2):
                        s.did(dve.tensor_tensor(tmp[:], view, a_all[:, :, half * HC:(half + 1) * HC], ALU.mult))
                        s.settle()
                        s.did(dve.tensor_reduce(src[:, D + half * H:D + (half + 1) * H], tmp[:], AX.X, ALU.add))
                        s.settle()
                assert s.count == 9
                dve.wait_ge(products, 2)
                s.did(dve.tensor_copy(bcol[:], kit.bank[1][0:H, 0:1]))
                for g, tiles in enumerate(groups):
                    dve.wait_ge(products, 3 + g)
                    k = len(tiles)
                    s.did(dve.tensor_tensor(F[:, tiles[0]:tiles[-1] + 1, :],
                                            kit.bank[2 + g % 6][:, 0:k * CAT].rearrange("p (k c) -> p k c", k=k),
                                            bias[:].unsqueeze(1).to_broadcast([P, k, CAT]), ALU.add))
                s.did(dve.memset(ones[:], 1.0))
                s.settle()
                dve.memset(X[:, :, :, HC:G1], 1.0).then_inc(tab["hv_ready"], 1)
                s.did(dve.tensor_copy(X[:, :, :, 0:HC], F[:, :, 0:D].rearrange("p t (h c) -> p t h c", h=H)))
                c_col, p_col = F[:, :, D + H:CAT], F[:, :, D:D + H]
                s.did(dve.tensor_reduce(cm[:], c_col.rearrange("p t h -> p h t"), AX.X, ALU.max))
                dve.wait_ge(pool_done, 1)
                s.did(dve.tensor_tensor(cs[:], c_col, over_tiles(call), ALU.subtract))
                s.did(dve.tensor_tensor(u[:], p_col, over_tiles(call), ALU.add))
                s.settle()
                s.did(dve.tensor_scalar(m[:], u[:], 0.0, None, ALU.max))
                s.settle()
                s.did(dve.tensor_tensor(e1[:], u[:], m[:], ALU.subtract))
                s.did(dve.scalar_tensor_tensor(out=e2[:], in0=u[:], scalar=SLOPE, in1=m[:], op0=ALU.mult,
                                               op1=ALU.subtract))
                s.did(dve.tensor_scalar(tab["neg_c"][:], c_col, -1.0, None, ALU.mult))
                s.did(dve.tensor_scalar(tab["steep_c"][:], c_col, STEEP, None, ALU.mult))
                s.did(dve.tensor_reduce(tab["R"][:], kit.ident[:, 0:PARTS * 2 * G1].rearrange("p (k c) -> p c k", k=PARTS),
                                        AX.X, ALU.add))
                dve.wait_ge(products, 2 + n_g + 8 + 1)
                s.did(dve.tensor_copy(tab["S"][:].rearrange("p h c -> p (h c)"), kit.bank[2][:, 0:H * G1]))
                ready = tab["hv_ready"]
                s.settle()
                dve.wait_ge(act_done, 5)
                for n, (side, part) in enumerate(makes_and_rests):
                    dve.wait_ge(ready, n + 1)
                    buf = v[side % 2]
                    if part is None:
                        if side == 2:
                            dve.wait_ge(act_done, 5 + rounds.index((0, 1)) + 1)
                        dve.tensor_tensor(flat(buf), flat(X[:]), over_cols(B if side == 1 else Dc), ALU.mult
                                          ).then_inc(ready, 1)
                    else:
                        dve.wait_ge(act_done, 5 + rounds.index((side, part)) + 1)
                        source = X[:] if side == 0 and part == 0 else buf
                        out = buf if part == 0 else part_of(side, 2)
                        dve.tensor_tensor(out, source, part_of(side, part), ALU.subtract).then_inc(ready, 1)
                dve.wait_ge(ready, 9)
                s.settle()


def head_attention(kit, adjT_dram, tab):
    nc, T, D, N = kit.nc, kit.T, kit.D, kit.N
    H, G1 = tab["S"].shape[1], tab["S"].shape[2]
    HC = G1 - 1
    CH, QUARTER = 8 * P, 2 * P
    IT, PIECES = CH // P, CH // QUARTER
    CHUNKS = N // CH
    HALF = CH // 2
    BY_DVE = (1, 5, 9, 12, 16, 20, 23, 26, 29)
    BY_ACT = tuple(j for j in range(T) if j not in BY_DVE)
    RING_ACT, RING_DVE = 4, 3
    LOADS = 4
    LT = T // LOADS
    EDGES_FROM = 3
    MOVE_AT, EDGES_MOVED_AT, JOIN_AT, JOINED_AT = 13, EDGES_FROM - 1, 18, 24
    assert IT == H and T - 1 in BY_ACT and MOVE_AT in BY_ACT
    assert len(BY_ACT) * H % RING_ACT == 0 and len(BY_DVE) * H % RING_DVE == 0
    HCOLS, UC = PARTS * 2 * G1, 2 * G1
    adjT_in = [kit.sem(f"adjT_in{i}") for i in range(LOADS)]
    p_in = [kit.sem(f"p_in{i}") for i in range(2)]
    compared, pos_made, act_used, dve_used, head_moved, joined, join_moved, edges_done, edges_moved, fin = (
        kit.sem("ha_" + n) for n in ("compared", "pos_made", "act_used", "dve_used", "head_moved", "joined",
                                     "join_moved", "edges_done", "edges_moved", "fin"))
    FIN = 10
    with ExitStack() as own:
        sb = lambda n, s, d=F32: own.enter_context(nc.sbuf_tensor("ha_" + n, s, d))
        adjT = sb("adjT", [P, PIECES, T, QUARTER], BF16)
        pos_act = [sb(f"pos_act{i}", [P, PIECES, QUARTER], BF16) for i in range(RING_ACT)]
        pos_dve = [sb(f"pos_dve{i}", [P, PIECES, QUARTER], BF16) for i in range(RING_DVE)]
        prow = [sb(f"p{i}", [P, CH]) for i in range(2)]
        head = sb("head", [HCOLS, CH])
        U = sb("U", [P, IT, H, UC])
        GX, GD = sb("GX", [P, IT, H, G1]), sb("GD", [P, IT, H, G1])
        rden = sb("rden", [P, IT * H, 1])

        def place(h, j):
            kind, ring, slots, used = ((BY_ACT, RING_ACT, pos_act, act_used) if j in BY_ACT else
                                       (BY_DVE, RING_DVE, pos_dve, dve_used))
            n = h * len(kind) + kind.index(j)
            return slots[n % ring], used, n

        def not_first(q):
            return not isinstance(q, int) or q > 0

        with nc.Block() as block:

            @block.sync
            def _(sp):
                def chunk(q):
                    for h in range(H):
                        wait_past(sp, pos_made, T * (H * q + h - 1))
                        sp.dma_start(prow[h % 2][:], tab["p_rows"][h:h + 1, bass.ds(q * CH, CH)]
                                     .to_broadcast([P, CH])).then_inc(p_in[h % 2], 16)
                        if h == 0:
                            for l in range(LOADS):
                                if not_first(q):
                                    sp.wait_ge(edges_done, LOADS * (IT * q - 1) + l + 1)
                                for i in range(PIECES):
                                    sp.dma_start(adjT[:, i, LT * l:LT * (l + 1), :].rearrange("p t i -> p (t i)"),
                                                 adjT_dram[bass.ds(PIECES * q + i, 1), :,
                                                           LT * QUARTER * l:LT * QUARTER * (l + 1)].squeeze(0)
                                                 ).then_inc(adjT_in[l], 16)

                peeled_loop(sp, CHUNKS, chunk)

            @block.scalar
            def _(act):
                def move_head(n, h):
                    act.wait_ge(act_used, len(BY_ACT) * (n + 1))
                    wait_past(act, joined, n)
                    for i in range(2):
                        act.copy(head[:, i * HALF:(i + 1) * HALF], kit.bank[2 * (h % 2) + i][0:HCOLS, :]
                                 ).then_inc(head_moved, 1)

                def chunk(q):
                    for h in range(H):
                        act.wait_ge(p_in[h % 2], 16 * (H // 2 * q + h // 2 + 1))
                        for j in BY_ACT:
                            slot, used, n = place(h, j)
                            wait_past(act, used, len(BY_ACT) * H * q + n - RING_ACT + 1)
                            act.activation(slot[:].rearrange("p a b -> p (a b)"), prow[h % 2][:], ACT.Sigmoid,
                                           bias=tab["steep_c"][:, j, h:h + 1], scale=STEEP).then_inc(compared, 1)
                            if j == MOVE_AT and (h > 0 or not_first(q)):
                                move_head(H * q + h - 1, (h - 1) % 2)

                peeled_loop(act, CHUNKS, chunk)
                move_head(H * CHUNKS - 1, 1)

            @block.vector
            def _(dve):
                def mask(q, h, j):
                    slot, used, n = place(h, j)
                    if h == 0 and j % LT == 0:
                        dve.wait_ge(adjT_in[j // LT], 16 * PIECES * (q + 1))
                    if j in BY_ACT:
                        dve.wait_ge(compared, len(BY_ACT) * H * q + n + 1)
                        dve.tensor_tensor(slot[:], slot[:], adjT[:, :, j, :], ALU.mult).then_inc(pos_made, 1)
                    else:
                        wait_past(dve, used, len(BY_DVE) * H * q + n - RING_DVE + 1)
                        dve.scalar_tensor_tensor(out=slot[:], in0=prow[h % 2][:].rearrange("p (a b) -> p a b", a=PIECES),
                                                 scalar=tab["neg_c"][:, j, h:h + 1], in1=adjT[:, :, j, :],
                                                 op0=ALU.is_gt, op1=ALU.mult).then_inc(pos_made, 1)

                def move_join(n, h):
                    dve.wait_ge(joined, n + 1)
                    dve.tensor_copy(U[:, :, h, :], kit.bank[6 + h % 2][:, 0:IT * UC].rearrange("p (i c) -> p i c", i=IT)
                                    ).then_inc(join_moved, 1)

                def move_edges(n, i):
                    dve.wait_ge(edges_done, LOADS * (n + 1))
                    for k, out, order in ((0, GX, "p (k h c) -> p h c k"), (1, GD, "p (h k c) -> p h c k")):
                        last = dve.tensor_reduce(out[:, i, :, :], kit.bank[4 + k][:, 0:PARTS * H * G1]
                                                 .rearrange(order, k=PARTS, h=H), AX.X, ALU.add)
                    last.then_inc(edges_moved, 1)

                def finish(q):
                    done = lambda n: FIN * q + n
                    pairs = lambda a: a[:].rearrange("p i h c -> p (i h) c")
                    coef = lambda n: (tab[n][:, bass.ds(IT * q, IT), :].rearrange("p i h -> p (i h)").unsqueeze(2)
                                      .to_broadcast([P, IT * H, G1]))
                    U1, U2, GXp, GDp = pairs(U)[:, :, 0:G1], pairs(U)[:, :, G1:UC], pairs(GX), pairs(GD)
                    S4 = tab["S"][:].rearrange("p h c -> p (h c)").unsqueeze(1).to_broadcast([P, IT, H * G1])
                    GX4 = GX[:].rearrange("p i h c -> p i (h c)")
                    dve.wait_ge(join_moved, H * q + H)
                    dve.wait_ge(edges_moved, IT * q + IT)
                    dve.tensor_tensor(U1, U1, coef("A"), ALU.mult).then_inc(fin, 1)
                    dve.tensor_tensor(GDp, GDp, U2, ALU.subtract).then_inc(fin, 1)
                    dve.tensor_tensor(GX4, S4, GX4, ALU.subtract).then_inc(fin, 1)
                    dve.wait_ge(fin, done(2))
                    dve.tensor_tensor(GDp, GDp, coef("C"), ALU.mult).then_inc(fin, 1)
                    dve.wait_ge(fin, done(3))
                    dve.tensor_tensor(GXp, GXp, coef("E"), ALU.mult).then_inc(fin, 1)
                    dve.wait_ge(fin, done(4))
                    dve.tensor_tensor(U1, U1, GDp, ALU.add).then_inc(fin, 1)
                    dve.wait_ge(fin, done(6))
                    dve.tensor_tensor(U1, U1, GXp, ALU.add).then_inc(fin, 1)
                    dve.wait_ge(fin, done(7))
                    dve.reciprocal(rden[:], U1[:, :, HC:G1]).then_inc(fin, 1)
                    dve.wait_ge(fin, done(8))
                    dve.tensor_tensor(U1[:, :, 0:HC], U1[:, :, 0:HC], rden[:].to_broadcast([P, IT * H, HC]),
                                      ALU.mult).then_inc(fin, 1)
                    dve.wait_ge(fin, done(9))
                    xq = kit.x[:, bass.ds(IT * q, IT), :].rearrange("p i (h c) -> p (i h) c", h=H)
                    dve.tensor_tensor(xq, xq, U1[:, :, 0:HC], ALU.add).then_inc(fin, 1)
                    dve.wait_ge(fin, done(10))

                def chunk(q):
                    for h in range(H):
                        dve.wait_ge(p_in[h % 2], 16 * (H // 2 * q + h // 2 + 1))
                        for j in range(T):
                            mask(q, h, j)
                            if h > 0 or not_first(q):
                                if j == EDGES_MOVED_AT:
                                    move_edges(IT * q + h - 1, (h - 1) % IT)
                                if j == JOINED_AT:
                                    move_join(H * q + h - 1, (h - 1) % H)
                                    if h == 0:
                                        finish(q - 1)

                peeled_loop(dve, CHUNKS, chunk)
                move_edges(IT * CHUNKS - 1, IT - 1)
                move_join(H * CHUNKS - 1, H - 1)
                finish(CHUNKS - 1)

            @block.tensor
            def _(pe):
                def join(n, h):
                    pe.wait_ge(head_moved, 2 * (n + 1))
                    wait_past(pe, join_moved, n - 1)
                    for i in range(IT):
                        last = pe.matmul(kit.bank[6 + h % 2][:, i * UC:(i + 1) * UC], head[:, i * P:(i + 1) * P],
                                         tab["R"][0:HCOLS, :], start=True, stop=True)
                    last.then_inc(joined, 1)

                def edges(q, i, tiles):
                    for j in tiles:
                        if j == 0:
                            wait_past(pe, edges_moved, IT * q + i)
                        if j % LT == 0:
                            pe.wait_ge(adjT_in[j // LT], 16 * PIECES * (q + 1))
                        for k, cols in enumerate((tab["VX"][:, j, :, :, :], tab["VH"][:, j, :, :, G1:UC])):
                            last = pe.matmul(kit.bank[4 + k][:, 0:PARTS * H * G1],
                                             adjT[:, i // 2, j, (i % 2) * P:(i % 2 + 1) * P],
                                             cols, start=(j == 0), stop=(j == T - 1))
                        if j % LT == LT - 1:
                            last.then_inc(edges_done, 1)

                def chunk(q):
                    for h in range(H):
                        n = H * q + h
                        wait_past(pe, head_moved, 2 * (n - 1))
                        for j in range(T):
                            slot, used, _ = place(h, j)
                            pe.wait_ge(pos_made, n * T + j + 1)
                            for i in range(2):
                                last = pe.matmul(kit.bank[2 * (h % 2) + i][0:HCOLS, :],
                                                 tab["VH"][:, j, h, :, :].rearrange("p k c -> p (k c)"),
                                                 slot[:, 2 * i:2 * i + 2, :].rearrange("p a b -> p (a b)"),
                                                 start=(j == 0), stop=(j == T - 1))
                            last.then_inc(used, 1)
                            if j >= EDGES_FROM:
                                span = T - EDGES_FROM
                                edges(q, h, range(T * (j - EDGES_FROM) // span, T * (j + 1 - EDGES_FROM) // span))
                            if j == JOIN_AT and (h > 0 or not_first(q)):
                                join(n - 1, (h - 1) % 2)

                peeled_loop(pe, CHUNKS, chunk)
                join(H * CHUNKS - 1, H - 1)




def load_and_sort_edges(kit, x_in, edges, keys_dram, digits_dram):
    nc, N = kit.nc, kit.N
    COLS = edges.shape[1] // P
    PIECE = 512
    PIECES = COLS // PIECE
    R = 64
    PER = 8
    x_loaded, zeroed, ident_made, ident_turned = (kit.sem(n) for n in ("x_loaded", "zeroed", "ident_made", "ident_h"))
    edges_in = [kit.sem(f"edges_in{i}") for i in range(2)]
    pieces_out = [kit.sem(f"pieces_out{i}") for i in range(2)]
    steps = kit.sem("se_steps")
    src_v, dst_v = (edges[i:i + 1, :].rearrange("o (p c) -> (o p) c", p=P) for i in range(2))
    with ExitStack() as own:
        sb = lambda n, s, d=F32: own.enter_context(nc.sbuf_tensor("se_" + n, s, d))
        src = [sb(f"src{i}", [P, PIECE], I32) for i in range(2)]
        dst = [sb(f"dst{i}", [P, PIECE], I32) for i in range(2)]
        key = [sb(f"key{i}", [P, PIECE]) for i in range(2)]
        digits = [sb(f"digits{i}", [P, 2, PIECE], BF16) for i in range(2)]
        inner, valid, packed = sb("inner", [P, PIECE]), sb("valid", [P, PIECE]), sb("packed", [P, PIECE])
        hi_i, lo_i = sb("hi_i", [P, PIECE], I32), sb("lo_i", [P, PIECE], I32)
        with nc.Block() as block:

            @block.sync
            def _(sp):
                for n in range(PIECES):
                    at = slice(n * PIECE, (n + 1) * PIECE)
                    wait_past(sp, steps, PER * (n - 1))
                    sp.dma_start(src[n % 2][:], src_v[:, at]).then_inc(edges_in[n % 2], 16)
                    sp.dma_start(dst[n % 2][:], dst_v[:, at]).then_inc(edges_in[n % 2], 16)
                    if n == 1:
                        sp.dma_start(kit.x[:], x_in.rearrange("(t p) d -> p t d", p=P)).then_inc(x_loaded, 16)
                sp.wait_ge(x_loaded, 16)

            @block.gpsimd
            def _(pool):
                nc.gpsimd.memset(kit.ident[:], 0.0).then_inc(zeroed, 1)
                pool.wait_ge(zeroed, 1)
                nc.gpsimd.affine_select(out=kit.ident[:], in_=kit.ident[:], compare_op=ALU.not_equal, fill=1.0,
                                        base=0, pattern=[[-1, P]], channel_multiplier=1).then_inc(ident_made, 1)

            @block.scalar
            def _(act):
                for n in range(PIECES):
                    at = slice(n * PIECE, (n + 1) * PIECE)
                    act.wait_ge(steps, PER * (n + 1))
                    act.dma_start(keys_dram[:, at], key[n % 2][:]).then_inc(pieces_out[n % 2], 16)
                    act.dma_start(digits_dram[:, :, at], digits[n % 2][:]).then_inc(pieces_out[n % 2], 16)
                for i in range(2):
                    act.wait_ge(pieces_out[i], 32 * PIECES // 2)

            @block.vector
            def _(dve):
                s = Steps(dve, steps)
                for n in range(PIECES):
                    i = n % 2
                    dve.wait_ge(edges_in[i], 32 * (n // 2 + 1))
                    wait_past(dve, pieces_out[i], 32 * (n // 2))
                    s.did(dve.tensor_scalar(inner[:], src[i][:], float(N - 1), None, ALU.is_lt))
                    s.did(dve.tensor_scalar(hi_i[:], dst[i][:], 6, None, ALU.logical_shift_right))
                    s.did(dve.tensor_scalar(lo_i[:], dst[i][:], R - 1, None, ALU.bitwise_and))
                    s.did(dve.scalar_tensor_tensor(out=packed[:], in0=dst[i][:], scalar=float(N), in1=src[i][:],
                                                   op0=ALU.mult, op1=ALU.add))
                    s.settle()
                    s.did(dve.scalar_tensor_tensor(out=valid[:], in0=dst[i][:], scalar=float(N), in1=inner[:],
                                                   op0=ALU.is_lt, op1=ALU.mult))
                    s.did(dve.scalar_tensor_tensor(out=digits[i][:, 0, :], in0=inner[:], scalar=512.0, in1=hi_i[:],
                                                   op0=ALU.mult, op1=ALU.add))
                    s.did(dve.tensor_copy(digits[i][:, 1, :], lo_i[:]))
                    s.settle()
                    s.did(dve.scalar_tensor_tensor(out=key[i][:], in0=packed[:], scalar=1.0, in1=valid[:],
                                                   op0=ALU.add, op1=ALU.mult))
                    s.settle()
                dve.wait_ge(ident_made, 1)
                dve.tensor_copy(kit.ident_h[:], kit.ident[:]).then_inc(ident_turned, 1)
                dve.wait_ge(ident_turned, 1)


def edge_attention(kit, name, xnT, keys_dram, count_dram, w, ffn, tables, out):
    nc, T, D, N = kit.nc, kit.T, kit.D, kit.N
    W_gat, att_src, att_dst, b_gat, gamma, beta = w
    H, EX = att_src.shape
    HE, G = H * EX, EX + 1
    CAT = HE + 2 * H
    SRC, DST = HE + H, 2 * H
    HALF = T // 2
    COLS = keys_dram.shape[1]
    TOP = 8
    VAL = H * G
    src_table, dst_table = tables
    w1, b1, w2, b2 = ffn
    E, F = w1.shape[0], w1.shape[2]
    HV = F // P
    U = E * HV
    CT, HS = 4, 8
    hidden_bank = [kit.bank[b] for b in (0, 1, 6, 7)]
    EARLY = 3
    MIX = T // CT - EARLY - 1
    halves = range(0, E // 2), range(E // 2, E)
    sem = lambda n: kit.sem(f"{name}_{n}")
    loads, steps, products, act_done, pool_done, table_out, last_in = (
        sem(n) for n in ("loads", "steps", "products", "act", "pool", "table_out", "last_in"))
    taken, indices, valued, weighed, scored, spread, summed = (
        sem(n) for n in ("taken", "indices", "valued", "weighed", "scored", "spread", "summed"))
    gathered = [sem(f"gathered{i}") for i in range(2)]
    w_in, b2_steps, hidden, activated, projected, y_moved = (
        sem(n) for n in ("w_in", "b2_steps", "hidden", "activated", "projected", "y_moved"))
    with ExitStack() as own:
        sb = lambda n, s, d=F32: own.enter_context(nc.sbuf_tensor(f"{name}_{n}", s, d))
        cat, att = sb("cat", [P, CAT]), sb("att", [P, 2, HE])
        tmp = sb("tmp", [P, HE])
        rows = sb("rows", [P, T, CAT])
        dstrow = sb("dstrow", [P, T, DST])
        am, aall = sb("am", [P, H]), sb("aall", [P, H])
        counts_r, counts = sb("counts_r", [T, P]), sb("counts", [P, T])
        lastrow = sb("lastrow", [P, CAT])
        t1, t2 = sb("t1", [P, T, H]), sb("t2", [P, T, H])
        w_own, w_last = sb("w_own", [P, T, H]), sb("w_last", [P, T, H])
        acc, acc2 = sb("acc", [P, T, H, G]), sb("acc2", [P, T, H, G])
        W1, W2, B1 = sb("W1", [P, E, F]), sb("W2", [P, U, D]), sb("B1", [P, U])
        B2_part, ones = sb("B2_part", [PARTS, E * D], BF16), sb("ones", [PARTS, P], BF16)
        hs, Y = sb("hs", [P, HS, CT * P]), sb("Y", [P, E, T * D])
        keys = sb("keys", [P, COLS])
        many, most = sb("many", [P, 2]), sb("most", [P, 2])
        pairs_f, pairs_i = sb("pairs_f", [P, 2]), sb("pairs_i", [P, 4], I32)
        iota_i, iota = sb("iota_i", [P, P], I32), sb("iota", [P, P])
        zero = sb("zero", [P, HALF * VAL], BF16)
        par_ = range(2)
        top = [sb(f"top{i}", [P, TOP]) for i in par_]
        real = [sb(f"real{i}", [P, TOP]) for i in par_]
        packed_f, packed = sb("packed_f", [P, TOP]), sb("packed", [P, TOP], I32)
        src_i = [sb(f"src{i}", [P, TOP], I32) for i in par_]
        dst_i = [sb(f"dst{i}", [P, TOP], I32) for i in par_]
        lo_i, hi_i, lo_s, hi_s = (sb(n, [P, TOP], I32) for n in ("lo_i", "hi_i", "lo_s", "hi_s"))
        lo = [sb(f"lo{i}", [P, TOP]) for i in par_]
        hi = [sb(f"hi{i}", [P, TOP]) for i in par_]
        from_src = [sb(f"fs{i}", [P, TOP, CAT]) for i in par_]
        from_dst = [sb(f"fd{i}", [P, TOP, DST]) for i in par_]
        e1, e2, wt = sb("e1", [P, TOP, H]), sb("e2", [P, TOP, H]), sb("wt", [P, TOP, H])
        vals = sb("vals", [P, TOP, H, G])
        hot_lo = [sb(f"hot_lo{i}", [P, TOP, P]) for i in par_]
        hot_hi = sb("hot_hi", [P, TOP, T])
        spreads = [sb(f"spread{i}", [P, TOP, T, VAL]) for i in par_]
        unfolded, room = (a[:].rearrange("p j t v -> p (j t v)") for a in spreads)
        unfolded, some = unfolded[:, 0:COLS], room[:, 0:COLS]
        B2 = room[0:PARTS, COLS:COLS + E * D]
        B2_h = room[0:PARTS, COLS + E * D:COLS + E * D + E * D // 2].bitcast(BF16)
        heads = lambda a: a.rearrange("p t (h e) -> p t h e", h=H)
        by_head = lambda a, n: a.unsqueeze(3).to_broadcast([P, n, H, EX])

        def leaky_less(s, dve, out, a, b, bound, mid):
            s.did(dve.tensor_tensor(mid, a, b, ALU.add))
            s.settle()
            s.did(dve.scalar_tensor_tensor(out=out, in0=mid, scalar=SLOPE, in1=mid, op0=ALU.mult, op1=ALU.max))
            s.settle()
            if bound is not None:
                s.did(dve.tensor_tensor(out, out, bound, ALU.subtract))
                s.settle()

        S_ROWS, S_MANY, S_DSTROW, S_PAIRS, S_OWN, S_LAST = 7, 12, 15, 22, 25, 28

        B2_SPLIT = 10

        FOLDED = COLS // 2
        MOST = (FOLDED + 7) // 16, (FOLDED + 7) // 16 + (FOLDED + 23) // 16

        def read_pairs(engine, both=True, less=0):
            n = 2 * less + both
            return engine.value_load(pairs_i[0:1, n:n + 1], min_val=MIX + 1 + both - less, max_val=MOST[both] - less)

        def load_all(sp):
            sp.dma_start(cat[:, 0:HE], W_gat).then_inc(loads, 16)
            for i, a in enumerate((att_src, att_dst)):
                sp.dma_start(att[:, i, :], a.rearrange("h e -> (h e)").unsqueeze(0).to_broadcast([P, HE])
                             ).then_inc(loads, 16)
            sp.dma_start(W1[:], w1.rearrange("e d f -> d e f")).then_inc(w_in, 16)
            sp.dma_start(W2[:], w2.rearrange("e (h f) d -> f (e h) d", f=P)).then_inc(w_in, 16)
            sp.dma_start(B1[:], b1.rearrange("e (h f) -> f (e h)", f=P), allow_slow_non_contiguous=True).then_inc(w_in, 16)
            sp.dma_start(B2, b2.rearrange("e d -> (e d)").unsqueeze(0).to_broadcast([PARTS, E * D])
                         ).then_inc(w_in, 16)
            sp.dma_start(unfolded, keys_dram).then_inc(loads, 16)
            sp.dma_start(counts_r[:], count_dram.rearrange("(t p) -> t p", p=P)).then_inc(loads, 16)

        layer_norm(kit, name + "_ln", Y[:, 0, :].rearrange("p (t d) -> p t d", t=T), xnT, prefetch=load_all)
        with nc.Block() as block:

            @block.sync
            def _(sp):
                sp.wait_ge(steps, S_ROWS)
                sp.dma_start(src_table.rearrange("(p t) c -> p t c", p=P), rows[:]).then_inc(table_out, 16)
                sp.wait_ge(steps, S_DSTROW)
                sp.dma_start(dst_table.rearrange("(p t) c -> p t c", p=P), dstrow[:]).then_inc(table_out, 16)
                sp.wait_ge(table_out, 32)
                sp.dma_start(lastrow[:], src_table[N - 1:N, :].to_broadcast([P, CAT])).then_inc(last_in, 16)
                sp.wait_ge(last_in, 16)

            @block.tensor
            def _(pe):
                pe.wait_ge(loads, 80)
                pe.transpose(kit.bank[2][:, 0:T], counts_r[:], kit.ident[0:T, 0:T]).then_inc(products, 1)
                pe.wait_ge(steps, 4)
                for t in range(T):
                    last = pe.matmul(kit.bank[t // HALF][:, (t % HALF) * CAT:(t % HALF + 1) * CAT], xnT[:, t, :], cat[:],
                                     start=True, stop=True)
                last.then_inc(products, 1)
                pe.wait_ge(w_in, 64)
                pe.wait_ge(b2_steps, B2_SPLIT)
                for b in range(2):
                    last = pe.matmul(kit.bank[4 + b][:, 0:HALF * VAL], zero[:, 0:P], zero[:], start=True,
                                     stop=False, skip_group_check=True)
                last.then_inc(products, 1)
                pe.wait_ge(steps, S_ROWS)

                def experts_chunk(q, experts=range(E)):
                    def project(e):
                        pe.wait_ge(activated, U * q + (e + 1) * HV)
                        wait_past(pe, y_moved, E * q + e - 1)
                        for i in range(CT):
                            at = kit.bank[2 + e % 2][:, i * P:(i + 1) * P]
                            for v in range(HV):
                                pe.matmul(at, hs[:, (e * HV + v) % HS, i * P:(i + 1) * P], W2[:, e * HV + v, :],
                                          start=(v == 0), stop=False)
                            last = pe.matmul(at, ones[:], B2_part[:, e * D:(e + 1) * D], start=False, stop=True)
                        last.then_inc(projected, 1)

                    for n in range(HV * experts[0], HV * (experts[-1] + 1)):
                        wait_past(pe, activated, U * q + n - len(hidden_bank) + 1)
                        e, v = n // HV, n % HV
                        pe.matmul(hidden_bank[n % 4][:], W1[:, e, v * P:(v + 1) * P], xnT[:, bass.ds(CT * q, CT), :],
                                  start=True, stop=True).then_inc(hidden, 1)
                        if e > experts[0] and n % HV == HV - 1:
                            project(e - 1)
                    project(experts[-1])

                experts_chunk(0)
                with pe.Fori(1, EARLY) as q:
                    experts_chunk(q)
                pe.wait_ge(steps, S_PAIRS)
                pairs = read_pairs(pe)

                def pair(k, mixed):
                    for par in par_:
                        if isinstance(k, int) and par == 0:
                            experts_chunk(EARLY)
                        if mixed:
                            experts_chunk(EARLY + 1 + k, halves[par])
                        pe.wait_ge(spread, 2 * k + par + 1)
                        for j in range(TOP):
                            for b in range(2):
                                last = pe.matmul(kit.bank[4 + b][:, 0:HALF * VAL], hot_lo[par][:, j, :],
                                                 spreads[par][:, j, b * HALF:(b + 1) * HALF, :], start=False,
                                                 stop=False, skip_group_check=True)
                        last.then_inc(summed, 1)

                pair(0, True)
                with pe.Fori(1, MIX) as k:
                    pair(k, True)
                with pe.Fori(MIX, pairs) as k:
                    pair(k, False)

            @block.scalar
            def _(act):
                act.wait_ge(w_in, 64)

                def experts_chunk(q, experts=range(E)):
                    def move(e):
                        act.wait_ge(projected, E * q + e + 1)
                        act.copy(Y[:, e, bass.ds(CT * D * q, CT * D)], kit.bank[2 + e % 2][:]).then_inc(y_moved, 1)

                    for n in range(HV * experts[0], HV * (experts[-1] + 1)):
                        wait_past(act, projected, E * q + (n - HS) // HV + 1)
                        act.wait_ge(hidden, U * q + n + 1)
                        act.activation(hs[:, n % HS, :], hidden_bank[n % 4][:], ACT.Gelu,
                                       bias=B1[:, n:n + 1]).then_inc(activated, 1)
                        if n % HV == HV - 1 and n // HV > experts[0]:
                            move(n // HV - 1)
                    move(experts[-1])

                experts_chunk(0)
                for w, ready in ((w_own, S_OWN), (w_last, S_LAST)):
                    act.wait_ge(steps, ready)
                    act.activation(w[:], w[:], ACT.Exp).then_inc(act_done, 1)
                with act.Fori(1, EARLY) as q:
                    experts_chunk(q)
                act.wait_ge(steps, S_PAIRS)
                pairs = read_pairs(act)

                def pair(k, mixed):
                    for par in par_:
                        act.wait_ge(scored, 3 * (2 * k + par) + 3)
                        act.activation(wt[:], e2[:], ACT.Exp).then_inc(weighed, 1)
                        if isinstance(k, int) and par == 0:
                            experts_chunk(EARLY)
                        if mixed:
                            experts_chunk(EARLY + 1 + k, halves[par])

                pair(0, True)
                with act.Fori(1, MIX) as k:
                    pair(k, True)
                with act.Fori(MIX, pairs) as k:
                    pair(k, False)
                act.wait_ge(y_moved, E * T // CT)

            @block.gpsimd
            def _(pool):
                nc.gpsimd.iota(iota_i[:], pattern=[[1, P]], base=0, channel_multiplier=0).then_inc(pool_done, 1)
                pool.wait_ge(steps, S_ROWS + 1)
                pool.partition_all_reduce(aall[:], am[:], P, RMAX).then_inc(pool_done, 1)
                pool.wait_ge(steps, S_MANY)
                pool.partition_all_reduce(most[:], many[:], P, RMAX).then_inc(pool_done, 1)
                pool.wait_ge(steps, S_PAIRS)
                pairs = read_pairs(pool)
                rounds_used = pool.alloc_register("rounds_used")

                def pair(k, looped=True):
                    for par in par_:
                        pool.wait_ge(indices, 2 * k + par + 1)
                        if looped:
                            pool.wait_ge(spread, rounds_used)
                            pool.reg_add(rounds_used, rounds_used, 1)
                        for j in range(TOP):
                            for out, table, index in ((from_src, src_table, src_i), (from_dst, dst_table, dst_i)):
                                pool.indirect_dma_start(
                                    out[par][:, j, :], None, table,
                                    bass.IndirectOffsetOnAxis(ap=index[par][:, j:j + 1].bitcast(U32), axis=0)
                                ).then_inc(gathered[par], 16)

                pool.wait_ge(table_out, 32)
                pair(0, looped=False)
                pool.reg_mov(rounds_used, 1)
                with pool.Fori(1, pairs) as k:
                    pair(k)

            @block.vector
            def _(dve):
                s = Steps(dve, steps)
                dve.wait_ge(loads, 80)
                for half in range(2):
                    s.did(dve.tensor_tensor(tmp[:], cat[:, 0:HE], att[:, half, :], ALU.mult))
                    s.settle()
                    s.did(dve.tensor_reduce(cat[:, HE + half * H:HE + (half + 1) * H],
                                            tmp[:].rearrange("p (h e) -> p h e", h=H), AX.X, ALU.add))
                    s.settle()
                split = Steps(dve, b2_steps)
                split.did(dve.memset(ones[:], 1.0))
                split.did(dve.memset(zero[:], 0.0))
                dve.wait_ge(w_in, 64)
                split.did(dve.tensor_copy(B2_h, B2))
                split.settle()
                split.did(dve.tensor_scalar(B2_part[:], B2_h, kit.ident[0:PARTS, 0:1], None, ALU.mult))
                split.did(dve.tensor_tensor(B2, B2, B2_h, ALU.subtract))
                for part in (1, 2):
                    split.settle()
                    split.did(dve.tensor_copy(B2_h, B2))
                    split.settle()
                    split.did(dve.scalar_tensor_tensor(out=B2_part[:], in0=B2_h, scalar=kit.ident[0:PARTS, part:part + 1],
                                                   in1=B2_part[:], op0=ALU.mult, op1=ALU.add))
                    if part == 1:
                        split.did(dve.tensor_tensor(B2, B2, B2_h, ALU.subtract))
                split.settle()
                assert split.count == B2_SPLIT
                dve.wait_ge(products, 1)
                s.did(dve.tensor_copy(counts[:], kit.bank[2][:, 0:T]))
                dve.wait_ge(products, 2)
                for b in range(2):
                    s.did(dve.tensor_copy(rows[:, b * HALF:(b + 1) * HALF, :].rearrange("p t c -> p (t c)"),
                                          kit.bank[b][:, 0:HALF * CAT]))
                assert s.count == S_ROWS
                s.settle()
                a_src, a_dst, m = rows[:, :, HE:SRC], rows[:, :, SRC:CAT], dstrow[:, :, H:DST]
                s.did(dve.tensor_reduce(am[:], a_src.rearrange("p t h -> p h t"), AX.X, ALU.max))
                for half, op in enumerate((ALU.max, ALU.min)):
                    s.did(dve.tensor_tensor(keys[:, half * FOLDED:(half + 1) * FOLDED], unfolded[:, 0:FOLDED],
                                            unfolded[:, FOLDED:COLS], op))
                s.settle()
                s.did(dve.tensor_scalar(some, keys[:], 0.0, None, ALU.is_gt))
                s.settle()
                s.did(dve.reduce_sum(many[:], some.rearrange("p (h c) -> p h c", h=2), AX.X))
                assert s.count == S_MANY
                dve.wait_ge(pool_done, 2)
                leaky_less(s, dve, m, a_dst, aall[:].unsqueeze(1).to_broadcast([P, T, H]), None, t1[:])
                s.did(dve.tensor_copy(dstrow[:, :, 0:H], a_dst))
                assert s.count == S_DSTROW
                dve.wait_ge(pool_done, 3)
                s.did(dve.tensor_scalar(pairs_f[:, 0:1], most[:, 0:1], 7.0, 2.0 * TOP * (MIX + 1), ALU.add, ALU.max))
                s.did(dve.tensor_scalar(pairs_f[:, 1:2], most[:, 1:2], 23.0, None, ALU.add))
                s.settle()
                s.did(dve.tensor_copy(packed[:, 0:2], pairs_f[:]))
                s.settle()
                s.did(dve.tensor_scalar(pairs_i[:, 0:2], packed[:, 0:2], 4, None, ALU.logical_shift_right))
                s.settle()
                s.did(dve.tensor_tensor(pairs_i[:, 1:2], pairs_i[:, 0:1], pairs_i[:, 1:2], ALU.add))
                s.settle()
                s.did(dve.tensor_scalar(pairs_i[:, 2:4], pairs_i[:, 0:2], -1.0, None, ALU.add))
                s.did(dve.tensor_copy(iota[:], iota_i[:]))
                assert s.count == S_PAIRS
                s.settle()
                TK = 12

                def take(r, par, half):
                    part = keys[:, half * FOLDED:(half + 1) * FOLDED]
                    at = lambda n: TK * r + n
                    dve.max(top[par][:], part).then_inc(taken, 1)
                    dve.wait_ge(taken, at(1))
                    dve.tensor_scalar(packed_f[:], top[par][:], -1.0, 0.0, ALU.add, ALU.max).then_inc(taken, 1)
                    dve.tensor_scalar(real[par][:], top[par][:], 0.0, None, ALU.is_gt).then_inc(taken, 1)
                    dve.match_replace(part, top[par][:], part, 0.0).then_inc(taken, 1)
                    dve.wait_ge(taken, at(3))
                    dve.tensor_copy(packed[:], packed_f[:]).then_inc(taken, 1)
                    if not isinstance(r, int) or r >= 2:
                        dve.wait_ge(gathered[par], G16 * (r - par) // 2 if isinstance(r, int) else G8 * (r - par))
                    dve.wait_ge(taken, at(5))
                    dve.tensor_scalar(lo_s[:], packed[:], P - 1, None, ALU.bitwise_and).then_inc(taken, 1)
                    dve.tensor_scalar(hi_s[:], packed[:], 7, T - 1, ALU.logical_shift_right, ALU.bitwise_and
                                      ).then_inc(taken, 1)
                    dve.tensor_scalar(lo_i[:], packed[:], 12, P - 1, ALU.logical_shift_right, ALU.bitwise_and
                                      ).then_inc(taken, 1)
                    dve.tensor_scalar(hi_i[:], packed[:], 12 + 7, None, ALU.logical_shift_right).then_inc(taken, 1)
                    dve.wait_ge(taken, at(9))
                    dve.scalar_tensor_tensor(out=src_i[par][:], in0=lo_s[:], scalar=float(T), in1=hi_s[:], op0=ALU.mult,
                                             op1=ALU.add).then_inc(taken, 1)
                    dve.scalar_tensor_tensor(out=dst_i[par][:], in0=lo_i[:], scalar=float(T), in1=hi_i[:], op0=ALU.mult,
                                             op1=ALU.add).then_inc(indices, 1)
                    dve.tensor_copy(hi[par][:], hi_i[:]).then_inc(taken, 1)
                    dve.tensor_copy(lo[par][:], lo_i[:]).then_inc(taken, 1)
                    dve.wait_ge(indices, r + 1)
                    dve.wait_ge(taken, at(12))

                def spread_out(r, par, k):
                    wait_past(dve, summed, r - 1)
                    wait_past(dve, spread, r)
                    dve.tensor_tensor(hot_lo[par][:], iota[:].unsqueeze(1).to_broadcast([P, TOP, P]),
                                      lo[par][:].unsqueeze(2).to_broadcast([P, TOP, P]), ALU.is_equal)
                    dve.tensor_tensor(hot_hi[:], iota[:, 0:T].unsqueeze(1).to_broadcast([P, TOP, T]),
                                      hi[par][:].unsqueeze(2).to_broadcast([P, TOP, T]), ALU.is_equal).then_inc(valued, 1)
                    dve.wait_ge(gathered[par], G16 * (k + 1))
                    fs, fd = from_src[par], from_dst[par]
                    dve.tensor_tensor(e1[:], fs[:, :, HE:SRC], fd[:, :, 0:H], ALU.add).then_inc(scored, 1)
                    dve.wait_ge(scored, 3 * r + 1)
                    dve.scalar_tensor_tensor(out=e2[:], in0=e1[:], scalar=SLOPE, in1=e1[:], op0=ALU.mult,
                                             op1=ALU.max).then_inc(scored, 1)
                    dve.wait_ge(scored, 3 * r + 2)
                    dve.tensor_tensor(e2[:], e2[:], fd[:, :, H:DST], ALU.subtract).then_inc(scored, 1)
                    dve.wait_ge(weighed, r + 1)
                    dve.tensor_tensor(vals[:, :, :, EX], wt[:], real[par][:].unsqueeze(2).to_broadcast([P, TOP, H]),
                                      ALU.mult).then_inc(valued, 1)
                    dve.wait_ge(valued, 3 * r + 2)
                    dve.tensor_tensor(vals[:, :, :, 0:EX], fs[:, :, 0:HE].rearrange("p j (h e) -> p j h e", h=H),
                                      vals[:, :, :, EX:G].to_broadcast([P, TOP, H, EX]), ALU.mult).then_inc(valued, 1)
                    dve.wait_ge(valued, 3 * r + 3)
                    dve.tensor_tensor(spreads[par][:], vals[:].rearrange("p j h g -> p j (h g)").unsqueeze(2)
                                      .to_broadcast([P, TOP, T, VAL]),
                                      hot_hi[:].unsqueeze(3).to_broadcast([P, TOP, T, VAL]), ALU.mult
                                      ).then_inc(spread, 1)

                G16 = 16 * 2 * TOP
                G8 = G16 // 2
                pairs = read_pairs(dve, both=False)
                pairs_less_1, both_less_1 = read_pairs(dve, both=False, less=1), read_pairs(dve, less=1)

                def pair(k, half=0):
                    for par in par_:
                        r = 2 * k + par
                        take(r + 1, 1 - par, half)
                        spread_out(r, par, k)

                take(0, 0, 0)
                leaky_less(s, dve, w_own[:], a_src, a_dst, m, t1[:])
                assert s.count == S_OWN
                dve.wait_ge(last_in, 16)
                leaky_less(s, dve, w_last[:], a_dst, lastrow[:, HE:SRC].unsqueeze(1).to_broadcast([P, T, H]), m, t1[:])
                assert s.count == S_LAST
                dve.wait_ge(products, 3)
                pair(0)
                dve.wait_ge(act_done, 1)
                s.did(dve.tensor_tensor(acc[:, :, :, 0:EX], heads(rows[:, :, 0:HE]), by_head(w_own[:], T), ALU.mult))
                s.did(dve.tensor_copy(acc[:, :, :, EX], w_own[:]))
                dve.wait_ge(act_done, 2)
                s.did(dve.tensor_tensor(acc2[:, :, :, EX], w_last[:], counts[:].unsqueeze(2).to_broadcast([P, T, H]),
                                        ALU.mult))
                s.settle()
                for h in range(H):
                    s.did(dve.tensor_tensor(acc2[:, :, h, 0:EX],
                                            lastrow[:, h * EX:(h + 1) * EX].unsqueeze(1).to_broadcast([P, T, EX]),
                                            acc2[:, :, h, EX:G].to_broadcast([P, T, EX]), ALU.mult))
                s.settle()
                s.did(dve.tensor_tensor(acc[:], acc[:], acc2[:], ALU.add))
                s.settle()
                with dve.Fori(1, pairs) as k:
                    pair(k)
                with dve.Fori(pairs_less_1, both_less_1) as k_less_1:
                    pair(k_less_1 + 1, 1)

        agg, centred, sq = (keys[:, i * T * HE:(i + 1) * T * HE].rearrange("p (t c) -> p t c", t=T) for i in range(3))
        assert EX == H
        rden = t2
        comb = sb("comb", [P, T, E])
        mu, var, sd, rstd = (sb(n, [P, T]) for n in ("mu", "var", "sd", "rstd"))
        norm = sb("norm", [P, 3, HE])
        PAD = 8
        score, ranked = (keys[:, (3 * HE + i * PAD) * T:(3 * HE + (i + 1) * PAD) * T].rearrange("p (t c) -> p t c", t=T)
                         for i in range(2))
        keep, soft, total = w_own, w_last, sb("total", [P, T])
        norm_in, s_steps, s_act, added, stored = (sem(n) for n in ("norm_in", "s_steps", "s_act", "added", "stored"))
        GROUP = T // 4
        wide = lambda a: a.unsqueeze(2).to_broadcast([P, T, HE])
        S_VAR, S_SOFT = 11, 18 + T
        per_node = lambda i: norm[:, i:i + 1, :].to_broadcast([P, T, HE])
        with nc.Block() as block:

            @block.sync
            def _(sp):
                for i, a in enumerate((b_gat, gamma, beta)):
                    sp.dma_start(norm[:, i, :], a.unsqueeze(0).to_broadcast([P, HE])).then_inc(norm_in, 16)
                x_out = out.rearrange("(t p) d -> p t d", p=P)
                for g in range(T // GROUP):
                    at = slice(g * GROUP, (g + 1) * GROUP)
                    sp.wait_ge(added, E * GROUP * (g + 1))
                    sp.dma_start(x_out[:, at, :], kit.x[:, at, :]).then_inc(stored, 16)
                sp.wait_ge(stored, 16 * (T // GROUP))

            @block.scalar
            def _(act):
                act.wait_ge(s_steps, S_VAR)
                act.activation(sd[:], var[:], ACT.Sqrt).then_inc(s_act, 1)
                act.wait_ge(s_steps, S_SOFT)
                act.activation(soft[:], keep[:], ACT.Exp, scale=1.0 / H).then_inc(s_act, 1)

            @block.vector
            def _(dve):
                s = Steps(dve, s_steps)

                def step(instruction):
                    s.did(instruction)
                    s.settle()

                for b in range(2):
                    at = slice(b * HALF, (b + 1) * HALF)
                    s.did(dve.tensor_tensor(acc[:, at, :, :].rearrange("p t h g -> p (t h g)"),
                                            acc[:, at, :, :].rearrange("p t h g -> p (t h g)"),
                                            kit.bank[4 + b][:, 0:HALF * VAL], ALU.add))
                s.settle()
                step(dve.tensor_scalar(t1[:], acc[:, :, :, EX], 1e-16, None, ALU.add))
                step(dve.reciprocal(rden[:], t1[:]))
                step(dve.tensor_tensor(heads(agg), acc[:, :, :, 0:EX], by_head(rden[:], T), ALU.mult))
                dve.wait_ge(norm_in, 48)
                step(dve.tensor_tensor(agg, agg, per_node(0), ALU.add))
                step(dve.reduce_sum(mu[:], agg, AX.X))
                step(dve.scalar_tensor_tensor(out=centred, in0=wide(mu[:]), scalar=-1.0 / HE, in1=agg,
                                              op0=ALU.mult, op1=ALU.add))
                step(dve.tensor_tensor(sq, centred, centred, ALU.mult))
                step(dve.reduce_sum(var[:], sq, AX.X))
                step(dve.tensor_scalar(var[:], var[:], 1.0 / HE, LN_EPS, ALU.mult, ALU.add))
                assert s.count == S_VAR
                dve.wait_ge(s_act, 1)
                step(dve.reciprocal(rstd[:], sd[:]))
                step(dve.tensor_tensor(centred, centred, wide(rstd[:]), ALU.mult))
                step(dve.tensor_tensor(centred, centred, per_node(1), ALU.mult))
                step(dve.tensor_tensor(centred, centred, per_node(2), ALU.add))
                step(dve.memset(score, -3e38))
                step(dve.tensor_reduce(score[:, :, 0:EX], centred.rearrange("p t (h e) -> p t e h", h=H), AX.X,
                                       ALU.add))
                for t in range(T):
                    s.did(dve.max(ranked[:, t, :], score[:, t, :]))
                s.settle()
                step(dve.tensor_tensor(keep[:], score[:, :, 0:EX], ranked[:, :, 0:1].to_broadcast([P, T, EX]),
                                       ALU.subtract))
                assert s.count == S_SOFT
                dve.wait_ge(s_act, 2)
                step(dve.tensor_tensor(keep[:], score[:, :, 0:EX], ranked[:, :, 1:2].to_broadcast([P, T, EX]),
                                       ALU.is_ge))
                step(dve.tensor_tensor(soft[:], soft[:], keep[:], ALU.mult))
                step(dve.reduce_sum(total[:], soft[:], AX.X))
                step(dve.reciprocal(total[:], total[:]))
                step(dve.tensor_tensor(comb[:], soft[:], total[:].unsqueeze(2).to_broadcast([P, T, EX]), ALU.mult))
                for n in range(E * T):
                    g, e, t = n // (E * GROUP), n // GROUP % E, n // (E * GROUP) * GROUP + n % GROUP
                    if e > 0:
                        dve.wait_ge(added, n - GROUP + 1)
                    xt = kit.x[:, t, :]
                    dve.scalar_tensor_tensor(out=xt, in0=Y[:, e, t * D:(t + 1) * D], scalar=comb[:, t, e:e + 1],
                                             in1=xt, op0=ALU.mult, op1=ALU.add).then_inc(added, 1)




def second_part(nc, kit, ins, adjT_dram, edge_dram, out):
    N, T, D = kit.N, kit.T, kit.D
    dram = lambda n, s, d: nc.dram_tensor(n, s, d, kind="Internal").ap()
    with ExitStack() as own:
        sb = lambda n, s: own.enter_context(nc.sbuf_tensor(n, s, F32))
        xn, xnT = sb("xn1", [P, T, D]), sb("xnT1", [P, T, P])
        comb = sb("comb0", [P, T, ins["L0_ffn_w1"].shape[0]])
        router(kit, xn, xnT, ins["L0_ffn_router_w"], comb)
        experts_and_histogram(kit, "ffn0", xnT, xn, comb, *(ins["L0_ffn_" + n] for n in ("w1", "b1", "w2", "b2")),
                              *edge_dram[1:])
    H = ins["L1_gnn_a"].shape[0]
    G1 = D // H + 1
    with ExitStack() as own:
        sb = lambda n, s, d=F32: own.enter_context(nc.sbuf_tensor("t3_" + n, s, d))
        tab = {"p_rows": dram("p_rows", [H, N], F32), "hv_ready": kit.sem("hv_ready")}
        for n in ("A", "C", "E", "neg_c", "steep_c"):
            tab[n] = sb(n, [P, T, H])
        tab["S"], tab["R"] = sb("S", [P, H, G1]), sb("R", [P, 2 * G1])
        tab["VX"], tab["VH"] = sb("VX", [P, T, PARTS, H, G1], BF16), sb("VH", [P, T, H, PARTS, 2 * G1], BF16)
        with ExitStack() as tmp:
            xn = tmp.enter_context(nc.sbuf_tensor("xn2", [P, T, D], F32))
            xnT = tmp.enter_context(nc.sbuf_tensor("xnT2", [P, T, P], F32))
            head_tables(kit, xn, xnT, ins["L1_gnn_W"], ins["L1_gnn_b"], ins["L1_gnn_a"], tab)
        head_attention(kit, adjT_dram, tab)
    edge_layer(nc, kit, ins, edge_dram, out)


def edge_layer(nc, kit, ins, edge_dram, out):
    N, T = kit.N, kit.T
    dram = lambda n, s, d: nc.dram_tensor(n, s, d, kind="Internal").ap()
    keys_dram, _, count_dram = edge_dram
    with ExitStack() as own:
        sb = lambda n, s: own.enter_context(nc.sbuf_tensor(n, s, F32))
        xnT = sb("xnT3", [P, T, P])
        heads, per_head = ins["L1_ffn_att_src"].shape
        tables = (dram("src_table", [N, heads * per_head + 2 * heads], F32), dram("dst_table", [N, 2 * heads], F32))
        edge_attention(kit, "ea", xnT, keys_dram, count_dram,
                       [ins["L1_ffn_" + n] for n in ("W_gat", "att_src", "att_dst", "b_gat", "ln_gamma", "ln_beta")],
                       [ins["L1_ffn_" + n] for n in ("W1", "b1", "W2", "b2")], tables, out)


def program(nc, ins, out):
    N, D = ins["x"].shape
    T = N // P
    dram = lambda n, s, d: nc.dram_tensor(n, s, d, kind="Internal").ap()
    with ExitStack() as ctx:
        kit = Kit(nc, ctx, N, D)
        adjT_dram = dram("adjT_dram", [N // (2 * P), P, T * 2 * P], BF16)
        edges = ins["L1_ffn_edge_index"]
        per_partition = edges.shape[1] // P
        edge_dram = (dram("keys_dram", [P, per_partition], F32), dram("digits_dram", [P, 2, per_partition], BF16),
                     dram("count_dram", [N], F32))
        load_and_sort_edges(kit, ins["x"], edges, *edge_dram[:2])
        with ExitStack() as own:
            sb = lambda n, s, d: own.enter_context(nc.sbuf_tensor("t1_" + n, s, d))
            tab = {"s_row": dram("s_row", [N], F32), "v_ready": kit.sem("v_ready")}
            for n in ("A", "C", "steep_t", "neg_t", "w_self"):
                tab[n] = sb(n, [P, T], F32)
            tab["rows"] = [sb(f"rows{i}", [P, N], BF16) for i in range(2)]
            tab["rows_in"] = [kit.sem(f"rows_in{i}") for i in range(2)]
            tab["X"] = sb("X", [P, T, D + 1], F32)
            tab["V"] = sb("V", [P, T, 2, PARTS, D + 1], BF16)
            with ExitStack() as tmp:
                xn = tmp.enter_context(nc.sbuf_tensor("xn0", [P, T, D], F32))
                xnT = tmp.enter_context(nc.sbuf_tensor("xnT0", [P, T, P], F32))
                dense_tables(kit, xn, xnT, ins["adj"], ins["L0_gnn_W"], ins["L0_gnn_a"], tab)
            dense_attention(kit, ins["adj"], adjT_dram, tab)
        second_part(nc, kit, ins, adjT_dram, edge_dram, out)


_INS = ['x', 'adj', 'L0_gnn_W', 'L0_gnn_a', 'L0_ffn_router_w', 'L0_ffn_w1', 'L0_ffn_b1', 'L0_ffn_w2', 'L0_ffn_b2',
        'L1_gnn_W', 'L1_gnn_b', 'L1_gnn_a', 'L1_ffn_W_gat', 'L1_ffn_att_src', 'L1_ffn_att_dst', 'L1_ffn_b_gat',
        'L1_ffn_ln_gamma', 'L1_ffn_ln_beta', 'L1_ffn_W1', 'L1_ffn_b1', 'L1_ffn_W2', 'L1_ffn_b2', 'L1_ffn_edge_index']


def kernel(**inputs):
    import numpy as _np
    import concourse.bacc as _bacc
    from concourse import mybir as _mybir
    from concourse.bass_utils import run_bass_kernel_spmd as _run

    nc = _bacc.Bacc("TRN2", target_bir_lowering=False, num_devices=1)
    arrays, args = {}, {}
    for name in _INS:
        a = _np.ascontiguousarray(inputs[name])
        arrays[f"in_{name}"] = a
        args[name] = nc.dram_tensor(f"in_{name}", a.shape, _mybir.dt.from_np(a.dtype), kind="ExternalInput").ap()
    out = nc.dram_tensor("out_x", inputs["x"].shape, _mybir.dt.float32, kind="ExternalOutput").ap()
    program(nc, args, out)
    r = _run(nc, [arrays], core_ids=[0])
    return r.results[0]["out_x"]
```
